# Optimizing a Trainium2 kernel written in Bass

```python
import numpy as np
import jax
import jax.numpy as jnp

def _softmax(x, axis=-1):
    return jax.nn.softmax(x, axis=axis)

def _gelu(x):
    return jax.nn.gelu(x, approximate=True)

def _silu(x):
    return jax.nn.silu(x)

def _sigmoid(x):
    return jax.nn.sigmoid(x)

def _layernorm(x, axis=-1, eps=1e-05):
    m = jnp.mean(x, axis=axis, keepdims=True)
    v = jnp.var(x, axis=axis, keepdims=True)
    return (x - m) / jnp.sqrt(v + eps)

def _scatter_add(tgt, idx, src, axis=0):
    return tgt.at[idx].add(src)

def _segment_sum(src, seg, n):
    return jax.ops.segment_sum(src, seg, n)
kernel_name = 'mk_xattn_ffn_d1_seqx_r2_a7a5c8'

def setup_inputs(seed: int=0):
    np.random.seed(seed)
    _w = jnp.asarray

    def _rec_inputs():
        import jax
        import jax.numpy as jnp
        _rk = jax.random.key(seed)
        x = 7.22e-05 + 1 * jax.random.normal(jax.random.fold_in(_rk, 1), (2, 2048, 512), jnp.float32)
        _lenS = 2048 - jax.random.randint(jax.random.fold_in(_rk, 7), (2,), 0, max(1, 2048 // 4) + 1, jnp.int32)
        _lenS2 = 154 - jax.random.randint(jax.random.fold_in(_rk, 8), (2,), 0, max(1, 154 // 4) + 1, jnp.int32)
        _ctx_1024P = jax.random.normal(jax.random.fold_in(_rk, 11), (2, 16, 512), jnp.float32)
        _ctx_1024c = jax.random.dirichlet(jax.random.fold_in(_rk, 511), 0.3 * jnp.ones((16,), jnp.float32), (2, 154))
        _ctx_1024t = jnp.einsum('bsk,bkd->bsd', _ctx_1024c, _ctx_1024P)
        _ctx_1024t = _ctx_1024t * jax.lax.rsqrt(jnp.mean(jnp.square(_ctx_1024t)) + 1e-12) * 0.953939
        ctx_1024 = 4.13588e-05 + 0.999923 * (_ctx_1024t + 0.3 * jax.random.normal(jax.random.fold_in(_rk, 611), (2, 154, 512), jnp.float32))
        return (x, ctx_1024)
    x, ctx_1024 = _rec_inputs()

    def _L0_xattn_setup():
        import jax, jax.numpy as jnp
        import numpy as np
        B, S, D, H = (4, 1024, 512, 16)
        HD = D // H
        key = jax.random.key(seed)
        ks = jax.random.split(key, 11)
        s = 1.0 / np.sqrt(D)
        return {'query': jax.random.normal(ks[0], (B, S, D), jnp.float32), 'key': jax.random.normal(ks[1], (B, S, D), jnp.float32), 'value': jax.random.normal(ks[2], (B, S, D), jnp.float32), 'Wq': jax.random.normal(ks[3], (D, D), jnp.float32) * s, 'bq': jax.random.normal(ks[4], (D,), jnp.float32) * s, 'Wk': jax.random.normal(ks[5], (D, D), jnp.float32) * s, 'bk': jax.random.normal(ks[6], (D,), jnp.float32) * s, 'Wv': jax.random.normal(ks[7], (D, D), jnp.float32) * s, 'bv': jax.random.normal(ks[8], (D,), jnp.float32) * s, 'Wo': jax.random.normal(ks[9], (D, D), jnp.float32) * s, 'bo': jax.random.normal(ks[10], (D,), jnp.float32) * s}
    _L0_xattn_all = _L0_xattn_setup()
    _L0_xattn_in = {k: v for k, v in _L0_xattn_all.items() if k in ('Wq', 'bq', 'Wk', 'bk', 'Wv', 'bv', 'Wo', 'bo')}
    del _L0_xattn_all

    def _L0_ffn_setup():
        import jax, jax.numpy as jnp
        import numpy as np
        DIM = 512
        DEPTH = 2
        HEADS = 8
        DIM_HEAD = 64
        WINDOW = 256
        INNER = HEADS * DIM_HEAD
        HID = int(DIM * 4 * 2 / 3)
        B, N = (2, 4096)
        QK_SCALE = 8.0

        def shift_token(t):
            t1, t2 = jnp.split(t, 2, axis=-1)
            t2 = jnp.pad(t2, ((0, 0), (1, 0), (0, 0)))[:, :-1]
            return jnp.concatenate([t1, t2], axis=-1)

        def l2norm(t):
            return t / jnp.clip(jnp.linalg.norm(t, axis=-1, keepdims=True), 1e-12)

        def rotate_half(x):
            x1, x2 = jnp.split(x, 2, axis=-1)
            return jnp.concatenate([-x2, x1], axis=-1)

        def rotary_xpos(q, k):
            n = q.shape[-2]
            half_idx = jnp.arange(0, DIM_HEAD, 2, dtype=jnp.float32)
            inv_freq = 1.0 / 10000.0 ** (half_idx / DIM_HEAD)
            t = jnp.arange(n, dtype=jnp.float32)
            freqs = t[:, None] * inv_freq[None, :]
            freqs = jnp.concatenate([freqs, freqs], axis=-1)
            base = (half_idx + 0.4 * DIM_HEAD) / (1.4 * DIM_HEAD)
            power = (t - n // 2) / float(WINDOW // 2)
            scale = base[None, :] ** power[:, None]
            scale = jnp.concatenate([scale, scale], axis=-1)
            cos, sin = (jnp.cos(freqs), jnp.sin(freqs))
            q = q * cos * scale + rotate_half(q) * sin * scale
            k = k * cos / scale + rotate_half(k) * sin / scale
            return (q, k)

        def local_attention(q, k, v):
            b, h, n, d = q.shape
            w = n // WINDOW
            bq = q.reshape(b, h, w, WINDOW, d) * QK_SCALE
            bk = k.reshape(b, h, w, WINDOW, d)
            bv = v.reshape(b, h, w, WINDOW, d)

            def look_around(t):
                p = jnp.pad(t, ((0, 0), (0, 0), (1, 0), (0, 0), (0, 0)))
                return jnp.concatenate([p[:, :, :w], p[:, :, 1:]], axis=3)
            bk, bv = (look_around(bk), look_around(bv))
            bt = jnp.arange(n).reshape(w, WINDOW)
            btp = jnp.pad(bt, ((1, 0), (0, 0)), constant_values=-1)
            btk = jnp.concatenate([btp[:w], btp[1:]], axis=1)
            sim = jnp.einsum('bhwid,bhwjd->bhwij', bq, bk)
            i = bt[:, :, None]
            j = btk[:, None, :]
            mask = (i < j) | (i > j + WINDOW) | (j == -1)
            sim = jnp.where(mask, -jnp.finfo(sim.dtype).max, sim)
            attn = jax.nn.softmax(sim, axis=-1)
            out = jnp.einsum('bhwij,bhwjd->bhwid', attn, bv)
            return out.reshape(b, h, n, d)

        def _layer(x, wqkv, qs, ksc, wo, lg, lb, w1, b1, w2, b2):
            b, n, _ = x.shape
            h = shift_token(x)
            qkv = h @ wqkv
            q, k, v = jnp.split(qkv, 3, axis=-1)
            to_heads = lambda t: t.reshape(b, n, HEADS, DIM_HEAD).transpose(0, 2, 1, 3)
            q, k, v = (to_heads(q), to_heads(k), to_heads(v))
            q = l2norm(q) * qs
            k = l2norm(k) * ksc
            q, k = rotary_xpos(q, k)
            o = local_attention(q, k, v)
            o = o.transpose(0, 2, 1, 3).reshape(b, n, INNER)
            x = x + o @ wo
            h = shift_token(x)
            mu = h.mean(-1, keepdims=True)
            var = h.var(-1, keepdims=True)
            h = (h - mu) / jnp.sqrt(var + 1e-05) * lg + lb
            h = h @ w1 + b1
            a, g = jnp.split(h, 2, axis=-1)
            h = a * jax.nn.gelu(g, approximate=False)
            x = x + h @ w2 + b2
            return x
        key = jax.random.key(seed)
        ks = jax.random.split(key, 6)
        return {'x': jax.random.normal(ks[0], (B, N, DIM), jnp.float32), 'wqkv': jax.random.normal(ks[1], (DEPTH, DIM, 3 * INNER), jnp.float32) * 0.02, 'q_scale': jnp.ones((DEPTH, DIM_HEAD), jnp.float32), 'k_scale': jnp.ones((DEPTH, DIM_HEAD), jnp.float32), 'wo': jax.random.normal(ks[2], (DEPTH, INNER, DIM), jnp.float32) * 0.02, 'ln_g': jnp.ones((DEPTH, DIM), jnp.float32), 'ln_b': jnp.zeros((DEPTH, DIM), jnp.float32), 'w1': jax.random.normal(ks[3], (DEPTH, DIM, 2 * HID), jnp.float32) * 0.02, 'b1': jnp.zeros((DEPTH, 2 * HID), jnp.float32), 'w2': jax.random.normal(ks[4], (DEPTH, HID, DIM), jnp.float32) * 0.02, 'b2': jnp.zeros((DEPTH, DIM), jnp.float32)}
    _L0_ffn_all = _L0_ffn_setup()
    _L0_ffn_in = {k: v for k, v in _L0_ffn_all.items() if k in ('wqkv', 'q_scale', 'k_scale', 'wo', 'ln_g', 'ln_b', 'w1', 'b1', 'w2', 'b2')}
    del _L0_ffn_all
    return {'x': x, 'ctx_1024': ctx_1024, 'L0_xattn_Wq': _L0_xattn_in['Wq'], 'L0_xattn_bq': _L0_xattn_in['bq'], 'L0_xattn_Wk': _L0_xattn_in['Wk'], 'L0_xattn_bk': _L0_xattn_in['bk'], 'L0_xattn_Wv': _L0_xattn_in['Wv'], 'L0_xattn_bv': _L0_xattn_in['bv'], 'L0_xattn_Wo': _L0_xattn_in['Wo'], 'L0_xattn_bo': _L0_xattn_in['bo'], 'L0_ffn_wqkv': _L0_ffn_in['wqkv'], 'L0_ffn_q_scale': _L0_ffn_in['q_scale'], 'L0_ffn_k_scale': _L0_ffn_in['k_scale'], 'L0_ffn_wo': _L0_ffn_in['wo'], 'L0_ffn_ln_g': _L0_ffn_in['ln_g'], 'L0_ffn_ln_b': _L0_ffn_in['ln_b'], 'L0_ffn_w1': _L0_ffn_in['w1'], 'L0_ffn_b1': _L0_ffn_in['b1'], 'L0_ffn_w2': _L0_ffn_in['w2'], 'L0_ffn_b2': _L0_ffn_in['b2']}

def reference(x, ctx_1024, L0_xattn_Wq, L0_xattn_bq, L0_xattn_Wk, L0_xattn_bk, L0_xattn_Wv, L0_xattn_bv, L0_xattn_Wo, L0_xattn_bo, L0_ffn_wqkv, L0_ffn_q_scale, L0_ffn_k_scale, L0_ffn_wo, L0_ffn_ln_g, L0_ffn_ln_b, L0_ffn_w1, L0_ffn_b1, L0_ffn_w2, L0_ffn_b2):
    import jax
    import jax.numpy as jnp

    def _L0_xattn_ref(query, key, value, Wq, bq, Wk, bk, Wv, bv, Wo, bo):
        import jax, jax.numpy as jnp
        import numpy as np
        B, S, D, H = (4, 1024, 512, 16)
        HD = D // H
        b = query.shape[0]
        q = (query @ Wq.T + bq).reshape(b, -1, H, HD).transpose(0, 2, 1, 3)
        k = (key @ Wk.T + bk).reshape(b, -1, H, HD).transpose(0, 2, 1, 3)
        v = (value @ Wv.T + bv).reshape(b, -1, H, HD).transpose(0, 2, 1, 3)
        scores = jnp.einsum('bhqd,bhkd->bhqk', q, k) / jnp.sqrt(jnp.float32(HD))
        attn = jax.nn.softmax(scores, axis=-1)
        out = jnp.einsum('bhqk,bhkd->bhqd', attn, v)
        out = out.transpose(0, 2, 1, 3).reshape(b, -1, D)
        return out @ Wo.T + bo

    def _L0_ffn_ref(x, wqkv, q_scale, k_scale, wo, ln_g, ln_b, w1, b1, w2, b2):
        import jax, jax.numpy as jnp
        import numpy as np
        DIM = 512
        DEPTH = 2
        HEADS = 8
        DIM_HEAD = 64
        WINDOW = 256
        INNER = HEADS * DIM_HEAD
        HID = int(DIM * 4 * 2 / 3)
        B, N = (2, 4096)
        QK_SCALE = 8.0

        def shift_token(t):
            t1, t2 = jnp.split(t, 2, axis=-1)
            t2 = jnp.pad(t2, ((0, 0), (1, 0), (0, 0)))[:, :-1]
            return jnp.concatenate([t1, t2], axis=-1)

        def l2norm(t):
            return t / jnp.clip(jnp.linalg.norm(t, axis=-1, keepdims=True), 1e-12)

        def rotate_half(x):
            x1, x2 = jnp.split(x, 2, axis=-1)
            return jnp.concatenate([-x2, x1], axis=-1)

        def rotary_xpos(q, k):
            n = q.shape[-2]
            half_idx = jnp.arange(0, DIM_HEAD, 2, dtype=jnp.float32)
            inv_freq = 1.0 / 10000.0 ** (half_idx / DIM_HEAD)
            t = jnp.arange(n, dtype=jnp.float32)
            freqs = t[:, None] * inv_freq[None, :]
            freqs = jnp.concatenate([freqs, freqs], axis=-1)
            base = (half_idx + 0.4 * DIM_HEAD) / (1.4 * DIM_HEAD)
            power = (t - n // 2) / float(WINDOW // 2)
            scale = base[None, :] ** power[:, None]
            scale = jnp.concatenate([scale, scale], axis=-1)
            cos, sin = (jnp.cos(freqs), jnp.sin(freqs))
            q = q * cos * scale + rotate_half(q) * sin * scale
            k = k * cos / scale + rotate_half(k) * sin / scale
            return (q, k)

        def local_attention(q, k, v):
            b, h, n, d = q.shape
            w = n // WINDOW
            bq = q.reshape(b, h, w, WINDOW, d) * QK_SCALE
            bk = k.reshape(b, h, w, WINDOW, d)
            bv = v.reshape(b, h, w, WINDOW, d)

            def look_around(t):
                p = jnp.pad(t, ((0, 0), (0, 0), (1, 0), (0, 0), (0, 0)))
                return jnp.concatenate([p[:, :, :w], p[:, :, 1:]], axis=3)
            bk, bv = (look_around(bk), look_around(bv))
            bt = jnp.arange(n).reshape(w, WINDOW)
            btp = jnp.pad(bt, ((1, 0), (0, 0)), constant_values=-1)
            btk = jnp.concatenate([btp[:w], btp[1:]], axis=1)
            sim = jnp.einsum('bhwid,bhwjd->bhwij', bq, bk)
            i = bt[:, :, None]
            j = btk[:, None, :]
            mask = (i < j) | (i > j + WINDOW) | (j == -1)
            sim = jnp.where(mask, -jnp.finfo(sim.dtype).max, sim)
            attn = jax.nn.softmax(sim, axis=-1)
            out = jnp.einsum('bhwij,bhwjd->bhwid', attn, bv)
            return out.reshape(b, h, n, d)

        def _layer(x, wqkv, qs, ksc, wo, lg, lb, w1, b1, w2, b2):
            b, n, _ = x.shape
            h = shift_token(x)
            qkv = h @ wqkv
            q, k, v = jnp.split(qkv, 3, axis=-1)
            to_heads = lambda t: t.reshape(b, n, HEADS, DIM_HEAD).transpose(0, 2, 1, 3)
            q, k, v = (to_heads(q), to_heads(k), to_heads(v))
            q = l2norm(q) * qs
            k = l2norm(k) * ksc
            q, k = rotary_xpos(q, k)
            o = local_attention(q, k, v)
            o = o.transpose(0, 2, 1, 3).reshape(b, n, INNER)
            x = x + o @ wo
            h = shift_token(x)
            mu = h.mean(-1, keepdims=True)
            var = h.var(-1, keepdims=True)
            h = (h - mu) / jnp.sqrt(var + 1e-05) * lg + lb
            h = h @ w1 + b1
            a, g = jnp.split(h, 2, axis=-1)
            h = a * jax.nn.gelu(g, approximate=False)
            x = x + h @ w2 + b2
            return x
        for l in range(DEPTH):
            x = _layer(x, wqkv[l], q_scale[l], k_scale[l], wo[l], ln_g[l], ln_b[l], w1[l], b1[l], w2[l], b2[l])
        return x
    x = x + _L0_xattn_ref(_layernorm(x, axis=-1), ctx_1024, ctx_1024, L0_xattn_Wq, L0_xattn_bq, L0_xattn_Wk, L0_xattn_bk, L0_xattn_Wv, L0_xattn_bv, L0_xattn_Wo, L0_xattn_bo)
    x = x + _L0_ffn_ref(_layernorm(x, axis=-1), L0_ffn_wqkv, L0_ffn_q_scale, L0_ffn_k_scale, L0_ffn_wo, L0_ffn_ln_g, L0_ffn_ln_b, L0_ffn_w1, L0_ffn_b1, L0_ffn_w2, L0_ffn_b2)
    return x

_drawn_inputs = setup_inputs


def setup_inputs(seed=0):
    import zlib

    import numpy as np

    out = dict(_drawn_inputs(seed))
    spreads = {'L0_ffn_q_scale': (1.0, 0.6),
     'L0_ffn_k_scale': (1.0, 0.6),
     'L0_ffn_ln_g': (1.0, 0.6),
     'L0_ffn_ln_b': (0.0, 0.8),
     'L0_ffn_b1': (0.0, 0.416),
     'L0_ffn_b2': (0.0, 0.1)}
    factors = {'L0_xattn_bq': 6.04, 'L0_xattn_bk': 8.0}
    for name, (base, spread) in spreads.items():
        noise = np.random.default_rng([zlib.crc32(name.encode()), seed]).standard_normal(out[name].shape)
        drawn = base * np.exp(spread * noise) if base else spread * noise
        out[name] = jnp.asarray(drawn.astype(out[name].dtype))
    for name, factor in factors.items():
        out[name] = (out[name] * factor).astype(out[name].dtype)
    return out
```

```python
from contextlib import ExitStack

import numpy as np

import concourse.bass as bass
from concourse import mybir

F32 = mybir.dt.float32
F32R = mybir.dt.float32r
ACT = mybir.ActivationFunctionType
ALU = mybir.AluOpType
AX = mybir.AxisListType

P = 128
B, N, D = 2, 2048, 512
T = B * N
DC = D // P
HALF = D // 2
SC, XH = 154, 16
XD = D // XH
SCH = SC // 2
QUAD = P // XD
QW = QUAD * SC
QK = -(-QW // P)
DEPTH, HEADS, DH, WIN = 2, 8, 64, 256
HID = int(D * 4 * 2 / 3)
MC = -(-HID // P)
TAIL = HID - (MC - 1) * P
GT = 4
G = GT * P
NT = T // P
NG = T // G
NI = NT // 4
KEYS = 3 * P
EPS = 1e-5
MASKED = -3.0e38


FROM_ONE = ("c_ac_k", "c_dv_t", "c_dv_vf", "c_out", "c_pe_t", "x_ac_exp", "x_dv_x1", "x_pe_o", "x_st_x1",
            "x_st_y", "f_dv_u", "f_dv_ul", "f_dv_y", "f_pe_y", "f_st")


def split_matmul(pe, out, a, b, start, stop):
    (a_h, a_l), (b_h, b_l) = a, b
    pe.matmul(out, a_h, b_h, start=start, stop=False)
    pe.matmul(out, a_h, b_l, start=False, stop=False)
    return pe.matmul(out, a_l, b_h, start=False, stop=stop)


def build(nc, io):
    ctx = ExitStack()

    from_one = {name: nc.alloc_semaphore(name) for name in FROM_ONE}

    def sem(name):
        return from_one[name] if name in from_one else nc.alloc_semaphore(name)

    passed = sem("passed")

    def wait(e, s, value, alone=False):
        if isinstance(value, int) and value <= 0:
            return
        if any(s is one for one in from_one.values()):
            value = value + 1
        assert isinstance(value, int) or value.min_val > 0, s
        e.wait_ge(s, value)
        if (alone or e is nc.sync) and not isinstance(value, int):
            e.sem_inc(passed, 1)

    def scratch(name, shape, dt=F32):
        return nc.dram_tensor(name, shape, dt, kind="Internal").ap()

    x1_rows = scratch("x1_rows", (T, D))
    y_rows = scratch("y_rows", (T, D))
    y_late = scratch("y_late", (T + 1, HALF))
    z_rows = scratch("z_rows", (T, D))
    z_late = scratch("z_late", (T + 1, HALF))
    ctx_k = scratch("ctx_k", (B * 2 * P, DC * SC))
    ctx_v = scratch("ctx_v", (B * 2 * SC, D))

    ps = ctx.enter_context(nc.psum_tensor("banks", [P, 8, 512], F32))
    ident = ctx.enter_context(nc.sbuf_tensor("ident", [P, P], F32))
    neg_half = ctx.enter_context(nc.sbuf_tensor("neg_half", [P, 2 * HEADS], F32))
    zero_row = ctx.enter_context(nc.sbuf_tensor("zero_row", [1, HALF], F32))
    consts_done = sem("consts_done")

    class Split:

        def __init__(self, name, stack, width, pieces, l=0):
            self.l, self.pieces, self.width = l, pieces, width
            self.stage = stack.enter_context(nc.sbuf_tensor(f"{name}_stage", [P, 2, width], F32))
            self.loaded = split_sems[name][0:2]
            self.hi_done, self.lo_done = split_sems[name][2:4]

        def slot(self, n):
            src = self.pieces[n][0]
            return self.stage[0:src.shape[0], n % 2, 0:src.shape[1]]

        def each(self, n0, n1):
            return range(n0, len(self.pieces) if n1 is None else n1)

        def loads(self, e, n0=0, n1=None):
            for n in self.each(n0, n1):
                wait(e, self.lo_done, self.l * len(self.pieces) + n - 1 if n >= 2 else 0)
                e.dma_start(self.slot(n), self.pieces[n][0]).then_inc(self.loaded[n % 2], 16)

        def _arrived(self, e, n):
            total = (len(self.pieces) + 1 - n % 2) // 2
            wait(e, self.loaded[n % 2], 16 * (self.l * total + n // 2 + 1))

        def his(self, e, n0=0, n1=None):
            for n in self.each(n0, n1):
                self._arrived(e, n)
                e.activation(self.pieces[n][1], self.slot(n), ACT.Copy).then_inc(self.hi_done, 1)

        def los(self, e, n0=0, n1=None):
            for n in self.each(n0, n1):
                wait(e, self.hi_done, self.l * len(self.pieces) + n + 1)
                e.tensor_tensor(self.pieces[n][2], self.slot(n), self.pieces[n][1].bitcast(F32),
                                ALU.subtract).then_inc(self.lo_done, 1)

        def done(self, e, n=None):
            n = len(self.pieces) if n is None else n
            wait(e, self.lo_done, self.l * len(self.pieces) + n, alone=True)

    split_sems = {name: [sem(f"{name}_{x}") for x in ("even", "odd", "hi", "lo")]
                  for name in ("w_ctx", "w_x", "w_attn", "w_ffn")}

    with nc.Block() as block:
        @block.gpsimd
        def _(e):
            for one in from_one.values():
                e.sem_inc(one, 1)

    context_phase(nc, io, ps, ident, sem, wait, Split, dict(ctx_k=ctx_k, ctx_v=ctx_v),
                  neg_half, zero_row, consts_done, (y_late, z_late))
    cross_phase(nc, io, ps, ident, sem, wait, Split, neg_half,
                dict(ctx_k=ctx_k, ctx_v=ctx_v, x1=x1_rows, y=y_rows, late=y_late),
                zero_row, consts_done)
    attn_sems = attention_sems(sem)
    ffn_s = ffn_sems(sem)
    with nc.Fori(0, DEPTH) as l:
        attention_phase(nc, io, ps, ident, attn_sems, wait, Split, neg_half, l,
                        dict(src=y_rows, src_late=y_late, dst=z_rows, dst_late=z_late), zero_row)
        ffn_phase(nc, io, ps, ident, ffn_s, wait, Split, neg_half, l,
                  dict(src=z_rows, src_late=z_late, dst=y_rows, dst_late=y_late, x1=x1_rows),
                  zero_row)
    ctx.close()


def context_phase(nc, io, ps, ident, sem, wait, Split, dram, neg_half, zero_row, consts_done,
                  lates):
    ld_small, ld_ctx, out_done, zero_done = sem("c_small"), sem("c_ctx"), sem("c_out"), sem("c_zero")
    ident_zeroed = sem("ident_zeroed")
    pe_t, ac_t, dv_t = sem("c_pe_t"), sem("c_ac_t"), sem("c_dv_t")
    pe_k, ac_k, ac_kh, dv_k = sem("c_pe_k"), sem("c_ac_k"), sem("c_ac_kh"), sem("c_dv_k")
    pe_v, dv_vf, ac_v, dv_v = sem("c_pe_v"), sem("c_dv_vf"), sem("c_ac_v"), sem("c_dv_v")
    with ExitStack() as st:
        def sb(name, shape, dt=F32):
            return st.enter_context(nc.sbuf_tensor(name, shape, dt))

        wk = [sb(f"wk_{x}", [P, DC, D], F32R) for x in "hl"]
        wv = [sb(f"wv_{x}", [P, DC, D], F32R) for x in "hl"]
        bk = sb("bk_cols", [P, DC])
        bv = sb("bv_rows", [SCH, D])
        c_in = sb("c_in", [SCH, 2, D])
        cT = [sb(f"cT_{x}", [P, DC, SC], F32R) for x in "hl"]
        k_full = sb("k_full", [P, DC, SC])
        kT = [sb(f"ctx_kT_{x}", [P, DC, SC], F32R) for x in "hl"]
        v_full = sb("v_full", [SCH, 2, D])
        v = [sb(f"ctx_v_{x}", [SCH, 2, D], F32R) for x in "hl"]
        w = Split("w_ctx", st, D,
                  [(io["WkT"][k * P:(k + 1) * P, :], wk[0][:, k, :], wk[1][:, k, :]) for k in range(DC)]
                  + [(io["WvT"][k * P:(k + 1) * P, :], wv[0][:, k, :], wv[1][:, k, :]) for k in range(DC)])
        k_dram = dram["ctx_k"].rearrange("r (c s) -> r c s", c=DC)

        with nc.Block() as block:
            @block.sync
            def _(e):
                e.dma_start(bk[:], io["bk"]).then_inc(ld_small, 16)
                e.dma_start(bv[:], io["bv"].to_broadcast([SCH, D])).then_inc(ld_small, 16)
                w.loads(e)
                wait(e, consts_done, 3)
                for late in lates:
                    for b in range(B):
                        e.dma_start(late[b * N:b * N + 1, :], zero_row[:]).then_inc(zero_done, 16)
                with e.Fori(0, B) as b:
                    wait(e, pe_t, b * DC)
                    e.dma_start(c_in[:], io["ctx"][bass.ds(b * SC, SC), :]
                                .rearrange("(h p) d -> p h d", p=SCH)).then_inc(ld_ctx, 16)
                    wait(e, dv_k, b + 1)
                    for part in range(2):
                        e.dma_start(k_dram[bass.ds(b * 2 * P + part * P, P)], kT[part][:].bitcast(F32)).then_inc(out_done, 16)
                    wait(e, dv_v, b + 1)
                    for part in range(2):
                        e.dma_start(dram["ctx_v"][bass.ds(b * 2 * SC + part * SC, SC), :]
                                    .rearrange("(h p) d -> p h d", p=SCH), v[part][:].bitcast(F32)).then_inc(out_done, 16)
                wait(e, out_done, 16 * 4 * B)
                wait(e, zero_done, 16 * 2 * B)

            @block.gpsimd
            def _(e):
                e.memset(neg_half[:], -0.5).then_inc(consts_done, 1)
                e.memset(zero_row[:], 0.0).then_inc(consts_done, 1)
                e.memset(ident[:], 0.0).then_inc(ident_zeroed, 1)
                wait(e, ident_zeroed, 1)
                e.affine_select(out=ident[:], in_=ident[:], compare_op=ALU.not_equal, fill=1.0, base=0,
                                pattern=[[-1, P]], channel_multiplier=1).then_inc(consts_done, 1)

            @block.tensor
            def _(e):
                wait(e, consts_done, 3)
                with e.Fori(0, B) as b:
                    wait(e, ld_ctx, 16 * b + 16)
                    for c in range(DC):
                        if c == 0:
                            wait(e, dv_t, 2 * b)
                        for h in range(2):
                            last = e.transpose(ps[:, c // 2, (c % 2) * SC + h * SCH:(c % 2) * SC + (h + 1) * SCH],
                                               c_in[:, h, c * P:(c + 1) * P], ident[0:SCH, 0:SCH])
                        last.then_inc(pe_t, 1)
                    w.done(e)
                    wait(e, dv_t, 2 * b + 2)
                    wait(e, ac_k, 2 * b)
                    for c in range(DC):
                        for k in range(DC):
                            last = split_matmul(e, ps[:, 2 + c // 2, (c % 2) * SC:(c % 2 + 1) * SC],
                                                [x[:, k, c * P:(c + 1) * P] for x in wk],
                                                [x[:, k, :] for x in cT], k == 0, k == DC - 1)
                        last.then_inc(pe_k, 1)
                    wait(e, dv_vf, 2 * b)
                    for h in range(2):
                        for k in range(DC):
                            last = split_matmul(e, ps[0:SCH, 4 + h, :],
                                                [x[:, k, h * SCH:(h + 1) * SCH] for x in cT],
                                                [x[:, k, :] for x in wv], k == 0, k == DC - 1)
                        last.then_inc(pe_v, 1)

            @block.scalar
            def _(e):
                w.his(e)
                wait(e, ld_small, 32)
                with e.Fori(0, B) as b:
                    for j in range(2):
                        wait(e, pe_t, b * DC + 2 * j + 2)
                        e.activation(cT[0][:, 2 * j:2 * j + 2, :],
                                     ps[:, j, 0:2 * SC].rearrange("p (c s) -> p c s", c=2), ACT.Copy).then_inc(ac_t, 1)
                    wait(e, pe_k, DC * b + DC)
                    for c in range(DC):
                        ins = e.activation(k_full[:, c, :], ps[:, 2 + c // 2, (c % 2) * SC:(c % 2 + 1) * SC],
                                           ACT.Identity, bias=bk[:, c:c + 1])
                        if c % 2:
                            ins.then_inc(ac_k, 1)
                    wait(e, ac_k, 2 * b + 2)
                    wait(e, out_done, 64 * b, alone=True)
                    e.activation(kT[0][:], k_full[:], ACT.Copy).then_inc(ac_kh, 1)
                    wait(e, dv_vf, 2 * b + 2)
                    e.activation(v[0][:], v_full[:], ACT.Copy).then_inc(ac_v, 1)

            @block.vector
            def _(e):
                w.los(e)
                wait(e, ld_small, 32)
                with e.Fori(0, B) as b:
                    for j in range(2):
                        wait(e, ac_t, 2 * b + j + 1)
                        e.tensor_tensor(cT[1][:, 2 * j:2 * j + 2, :],
                                        ps[:, j, 0:2 * SC].rearrange("p (c s) -> p c s", c=2),
                                        cT[0][:, 2 * j:2 * j + 2, :].bitcast(F32), ALU.subtract).then_inc(dv_t, 1)
                    wait(e, ac_kh, b + 1)
                    e.tensor_tensor(kT[1][:], k_full[:], kT[0][:].bitcast(F32), ALU.subtract).then_inc(dv_k, 1)
                    for h in range(2):
                        wait(e, pe_v, 2 * b + h + 1)
                        e.tensor_tensor(v_full[:, h, :], ps[0:SCH, 4 + h, :], bv[:], ALU.add).then_inc(dv_vf, 1)
                    wait(e, ac_v, b + 1)
                    e.tensor_tensor(v[1][:], v_full[:], v[0][:].bitcast(F32), ALU.subtract).then_inc(dv_v, 1)


def cross_phase(nc, io, ps, ident, sem, wait, Split, neg_half, dram, zero_row, consts_done):
    ld_small, ld_kv = sem("x_small"), sem("x_kv")
    ld_x = [sem(f"x_ld{s}") for s in range(2)]
    st_x1, st_y = sem("x_st_x1"), sem("x_st_y")
    zeroed = sem("x_zeroed")
    dv_own, dv_ve, pl_rs, dv_xn, pl_xb = sem("x_dv_own"), sem("x_dv_ve"), sem("x_pl_rs"), sem("x_dv_xn"), sem("x_pl_xb")
    pe_x, ac_x, dv_x = sem("x_pe_x"), sem("x_ac_x"), sem("x_dv_x")
    pe_q, ac_q, dv_q = sem("x_pe_q"), sem("x_ac_q"), sem("x_dv_q")
    pe_s, dv_max, ac_exp, dv_rc, pl_p = sem("x_pe_s"), sem("x_dv_max"), sem("x_ac_exp"), sem("x_dv_rc"), sem("x_pl_p")
    pe_t, ac_t, dv_t = sem("x_pe_t"), sem("x_ac_t"), sem("x_dv_t")
    pe_o, ac_o, dv_o = sem("x_pe_o"), sem("x_ac_o"), sem("x_dv_o")
    pe_w, dv_x1, dv_y = sem("x_pe_w"), sem("x_dv_x1"), sem("x_dv_y")
    NS = DC * GT
    SCALE = float(XD) ** -0.5
    rows_of = [min(P, QW - k * P) for k in range(QK)]
    segments = [(r, k, max(SC * r, P * k), min(SC * (r + 1), P * (k + 1)))
                for r in range(QUAD) for k in range(QK) if max(SC * r, P * k) < min(SC * (r + 1), P * (k + 1))]
    KV_LOADS = 2 * (QUAD + len(segments))
    OWN = 2 * (1 + GT) + NS

    with ExitStack() as st:
        def sb(name, shape, dt=F32):
            return st.enter_context(nc.sbuf_tensor(name, shape, dt))

        wq = [sb(f"wq_{x}", [P, DC, D], F32R) for x in "hl"]
        wo = [sb(f"xwo_{x}", [P, DC, D], F32R) for x in "hl"]
        k_bd = [sb(f"k_bd_{x}", [P, DC, 2, SC], F32R) for x in "hl"]
        v_bd = [sb(f"v_bd_{x}", [P, DC, QK, P], F32R) for x in "hl"]
        bq = sb("bq_cols", [P, DC])
        bo = sb("bo_rows", [P, D])
        x_in = sb("x_in", [P, 2, GT, D])
        xn = sb("xn", [P, GT, D])
        stats = sb("x_stats", [P, GT, 6])
        mv = sb("x_mv", [P, GT, 2])
        ve = sb("x_ve", [P, GT])
        rs = sb("x_rs", [P, GT])
        xT = [sb(f"xT_{x}", [P, DC, G], F32R) for x in "hl"]
        qT = [sb(f"xqT_{x}", [P, DC, G], F32R) for x in "hl"]
        mx = sb("x_mx", [P, NS, QUAD])
        nmx = sb("x_nmx", [P, NS, QUAD])
        sm = sb("x_sm", [P, NS, QUAD])
        rc = sb("x_rc", [P, NS, QUAD])
        prob = sb("x_prob", [P, 2, GT, QW])
        pT = [sb(f"xpT_{x}", [P, QK, G], F32R) for x in "hl"]
        oT = [sb(f"xoT_{x}", [P, DC, G], F32R) for x in "hl"]
        x1 = sb("x1_t", [P, GT, D])
        y = sb("y0_t", [P, GT, D])
        w = Split("w_x", st, D,
                  [(io["WqT"][k * P:(k + 1) * P, :], wq[0][:, k, :], wq[1][:, k, :]) for k in range(DC)]
                  + [(io["WoT"][k * P:(k + 1) * P, :], wo[0][:, k, :], wo[1][:, k, :]) for k in range(DC)])
        k_dram = dram["ctx_k"].rearrange("r (c s) -> r c s", c=DC)

        def run(e, per_batch, per_group):
            with e.Fori(0, B) as b:
                per_batch(b)
                with e.Fori(0, NG // B // 2) as gg:
                    for s in range(2):
                        pair = e.snap(b * (NG // B // 2) + gg)
                        it = e.snap(b * (NG // B) + gg * 2 + s)
                        per_group(it, s, pair)

        with nc.Block() as block:
            @block.sync
            def _(e):
                e.dma_start(bq[:], io["bq"]).then_inc(ld_small, 16)
                e.dma_start(bo[:], io["bo"].to_broadcast([P, D])).then_inc(ld_small, 16)

                def rows(ap, it, late=0):
                    return ap[bass.ds(it * G + late, G), :].rearrange("(t p) d -> p t d", p=P)

                def load_x(it, s):
                    e.dma_start(x_in[:, s], rows(io["x"], it)).then_inc(ld_x[s], 16)

                load_x(0, 0)
                load_x(1, 1)
                w.loads(e)
                wait(e, zeroed, 4)

                def per_batch(b):
                    src_k = [k_dram[bass.ds(b * 2 * P + part * P, P)] for part in range(2)]
                    src_v = [dram["ctx_v"][bass.ds(b * 2 * SC + part * SC, SC), :]
                             .rearrange("s (c n) -> s c n", c=DC) for part in range(2)]
                    wait(e, pe_o, b * (NG // B) * DC)
                    for part in range(2):
                        for r in range(QUAD):
                            e.dma_start(k_bd[part][r * XD:(r + 1) * XD, :, r % 2, :].bitcast(F32),
                                        src_k[part][r * XD:(r + 1) * XD]).then_inc(ld_kv, 16)
                        for r, k, f0, f1 in segments:
                            e.dma_start(v_bd[part][f0 - k * P:f1 - k * P, :, k, r * XD:(r + 1) * XD].bitcast(F32),
                                        src_v[part][f0 - r * SC:f1 - r * SC, :, r * XD:(r + 1) * XD]).then_inc(ld_kv, 16)

                def per_group(it, s, pair):
                    dst = [rows(dram["x1"], it), rows(dram["y"], it), rows(dram["late"], it, 1)]
                    wait(e, dv_x1, GT * it + GT)
                    e.dma_start(dst[0], x1[:]).then_inc(st_x1, 16)
                    wait(e, dv_y, GT * it + GT)
                    e.dma_start(dst[1], y[:]).then_inc(st_y, 16)
                    e.dma_start(dst[2], y[:, :, HALF:D]).then_inc(st_y, 16)

                with e.Fori(0, B) as b:
                    per_batch(b)
                    with e.Fori(0, NG // B // 2) as gg:
                        for s in range(2):
                            pair = e.snap(b * (NG // B // 2) + gg)
                            it = e.snap(b * (NG // B) + gg * 2 + s)
                            per_group(it, s, pair)
                            nxt = e.snap((it + 2) % NG)
                            src = rows(io["x"], nxt)
                            wait(e, dv_x1, GT * it + GT)
                            e.dma_start(x_in[:, s], src).then_inc(ld_x[s], 16)
                wait(e, st_x1, 16 * NG)
                wait(e, st_y, 32 * NG)
                for s in range(2):
                    wait(e, ld_x[s], 16 * (NG // 2 + 1))
                e.dma_start(dram["late"][N:N + 1, :], zero_row[:]).then_inc(st_y, 16)
                wait(e, st_y, 32 * NG + 16)

            @block.gpsimd
            def _(e):
                for a in (k_bd[0], k_bd[1], v_bd[0], v_bd[1]):
                    e.memset(a[:].bitcast(F32), 0.0).then_inc(zeroed, 1)
                wait(e, ld_small, 32)

                def per_group(it, s, pair):
                    wait(e, dv_ve, 2 * it + 1)
                    e.tensor_tensor(rs[:], ve[:], neg_half[:, 0:GT], ALU.pow).then_inc(pl_rs, 1)
                    wait(e, dv_xn, GT * it + GT)
                    for tt in range(GT):
                        e.tensor_tensor(x_in[:, s, tt, :], x_in[:, s, tt, :], bo[:], ALU.add).then_inc(pl_xb, 1)
                    for n in range(NS):
                        c, tt = divmod(n, GT)
                        p4 = prob[:, c % 2, tt, :].rearrange("p (r s) -> p r s", r=QUAD)
                        wait(e, dv_rc, NS * it + n + 1)
                        e.tensor_tensor(p4, p4, rc[:, n, :].rearrange("p (r o) -> p r o", o=1)
                                        .to_broadcast([P, QUAD, SC]), ALU.mult).then_inc(pl_p, 1)
                    wait(e, dv_ve, 2 * it + 2)
                    e.tensor_tensor(rs[:], ve[:], neg_half[:, 0:GT], ALU.pow).then_inc(pl_rs, 1)

                run(e, lambda b: None, per_group)

            @block.tensor
            def _(e):
                def per_batch(b):
                    wait(e, ld_kv, 16 * KV_LOADS * b + 16 * KV_LOADS, alone=True)

                def per_group(it, s, pair):
                    for k in range(DC):
                        wait(e, dv_xn, GT * it + GT) if k == 0 else None
                        if k < 2:
                            wait(e, dv_x1, GT * it)
                        else:
                            wait(e, dv_x, DC * it + k - 1)
                        for tt in range(GT):
                            last = e.transpose(ps[:, 4 + k % 2, tt * P:(tt + 1) * P],
                                               xn[:, tt, k * P:(k + 1) * P], ident[:])
                        last.then_inc(pe_x, 1)
                    w.done(e)
                    wait(e, dv_x, DC * it + DC)
                    for c in range(DC):
                        if c >= 2:
                            wait(e, dv_q, DC * it + c - 1)
                        for k in range(DC):
                            last = split_matmul(e, ps[:, 6 + c % 2, :], [x[:, k, c * P:(c + 1) * P] for x in wq],
                                                [x[:, k, :] for x in xT], k == 0, k == DC - 1)
                        last.then_inc(pe_q, 1)

                    def scores(n):
                        c, tt = divmod(n, GT)
                        if tt == 0:
                            wait(e, dv_q, DC * it + c + 1)
                        wait(e, ac_exp, NS * it + n - 1 if n >= 2 else NS * it)
                        for pair_ in range(2):
                            r = slice(64 * pair_, 64 * pair_ + 64)
                            last = split_matmul(e, ps[:, 2 * (n % 2) + pair_, 0:2 * SC],
                                                [x[r, c, tt * P:(tt + 1) * P] for x in qT],
                                                [x[r, c, :, :].rearrange("p a s -> p (a s)") for x in k_bd], True, True)
                        last.then_inc(pe_s, 1)

                    def values(c, k):
                        wait(e, dv_t, QK * DC * it + QK * c + k + 1)
                        last = split_matmul(e, ps[:, 6 + c % 2, :], [x[0:rows_of[k], c, k, :] for x in v_bd],
                                            [x[0:rows_of[k], k, :] for x in pT], k == 0, k == QK - 1)
                        if k == QK - 1:
                            last.then_inc(pe_o, 1)

                    for tt in range(GT):
                        scores(tt)
                    for c in range(DC):
                        for k in range(QK):
                            if k == 0:
                                wait(e, pl_p, NS * it + GT * (c + 1))
                                if c >= 2:
                                    wait(e, dv_o, DC * it + c - 1)
                            m = QK * c + k
                            wait(e, dv_t, QK * DC * it + m - 1 if m >= 2 else 0)
                            for tt in range(GT):
                                last = e.transpose(ps[0:rows_of[k], 4 + m % 2, tt * P:(tt + 1) * P],
                                                   prob[:, c % 2, tt, k * P:k * P + rows_of[k]], ident[:])
                            last.then_inc(pe_t, 1)
                            if c + 1 < DC and k < GT:
                                scores(GT * (c + 1) + k)
                            if k >= 1:
                                values(c, k - 1)
                        values(c, QK - 1)
                    wait(e, dv_o, DC * it + DC)
                    for tt in range(GT):
                        if tt >= 2:
                            wait(e, dv_x1, GT * it + tt - 1)
                        for c in range(DC):
                            last = split_matmul(e, ps[:, 4 + tt % 2, :], [x[:, c, tt * P:(tt + 1) * P] for x in oT],
                                                [x[:, c, :] for x in wo], c == 0, c == DC - 1)
                        last.then_inc(pe_w, 1)

                run(e, per_batch, per_group)

            @block.scalar
            def _(e):
                w.his(e)
                wait(e, ld_small, 32)

                def per_group(it, s, pair):
                    for k in range(DC):
                        wait(e, pe_x, DC * it + k + 1)
                        e.activation(xT[0][:, k, :], ps[:, 4 + k % 2, :], ACT.Copy).then_inc(ac_x, 1)
                    for c in range(DC):
                        wait(e, pe_q, DC * it + c + 1)
                        e.activation(qT[0][:, c, :], ps[:, 6 + c % 2, :], ACT.Identity, bias=bq[:, c:c + 1]).then_inc(ac_q, 1)

                    def exps(n):
                        c, tt = divmod(n, GT)
                        wait(e, dv_max, NS * it + n + 1)
                        for r in range(QUAD):
                            ins = e.activation(prob[:, c % 2, tt, r * SC:(r + 1) * SC],
                                               ps[:, 2 * (n % 2) + r // 2, (r % 2) * SC:(r % 2 + 1) * SC], ACT.Exp,
                                               bias=nmx[:, n, r:r + 1], scale=SCALE, accum_out=sm[:, n, r:r + 1])
                        ins.then_inc(ac_exp, 1)

                    for tt in range(GT):
                        exps(tt)
                    for c in range(DC):
                        for k in range(QK):
                            m = QK * c + k
                            wait(e, pe_t, QK * DC * it + m + 1)
                            e.activation(pT[0][0:rows_of[k], k, :], ps[0:rows_of[k], 4 + m % 2, :], ACT.Copy).then_inc(ac_t, 1)
                            if c + 1 < DC and k < GT:
                                exps(GT * (c + 1) + k)
                        wait(e, pe_o, DC * it + c + 1)
                        e.activation(oT[0][:, c, :], ps[:, 6 + c % 2, :], ACT.Copy).then_inc(ac_o, 1)

                run(e, lambda b: None, per_group)

            @block.vector
            def _(e):
                w.los(e)
                wait(e, ld_small, 32)

                def per_group(it, s, pair):
                    own = [0]

                    def mark(ins):
                        ins.then_inc(dv_own, 1)
                        own[0] += 1

                    def settle():
                        wait(e, dv_own, OWN * it + own[0], alone=True)

                    def moments(src):
                        for tt in range(GT):
                            ins = e.bn_stats(stats[:, tt, :], src(tt))
                        mark(ins)
                        settle()
                        for tt in range(GT):
                            mark(e.bn_aggr(mv[:, tt, :], stats[:, tt, :]))
                        settle()
                        e.tensor_scalar(ve[:].rearrange("p (t o) -> p t o", o=1), mv[:, :, 1:2], EPS, None, ALU.add).then_inc(dv_ve, 1)

                    wait(e, ld_x[s], 16 * pair + 16, alone=True)
                    moments(lambda tt: x_in[:, s, tt, :])
                    wait(e, pl_rs, 2 * it + 1, alone=True)
                    for tt in range(GT):
                        e.tensor_scalar(xn[:, tt, :], x_in[:, s, tt, :], mv[:, tt, 0:1], rs[:, tt:tt + 1],
                                        ALU.subtract, ALU.mult).then_inc(dv_xn, 1)
                    for k in range(DC):
                        wait(e, ac_x, DC * it + k + 1)
                        e.tensor_tensor(xT[1][:, k, :], ps[:, 4 + k % 2, :], xT[0][:, k, :].bitcast(F32), ALU.subtract).then_inc(dv_x, 1)
                    for c in range(DC):
                        wait(e, ac_q, DC * it + c + 1)
                        e.scalar_tensor_tensor(out=qT[1][:, c, :], in0=ps[:, 6 + c % 2, :], scalar=bq[:, c:c + 1],
                                               in1=qT[0][:, c, :].bitcast(F32), op0=ALU.add, op1=ALU.subtract).then_inc(dv_q, 1)

                    def maxima(n):
                        wait(e, pe_s, NS * it + n + 1)
                        b0 = 2 * (n % 2)
                        mark(e.tensor_reduce(mx[:, n, :].rearrange("p (a r) -> p a r", a=2),
                                             ps[:, b0:b0 + 2, 0:2 * SC].rearrange("p a (r s) -> p a r s", r=2), AX.X, ALU.max))
                        settle()
                        e.tensor_scalar(nmx[:, n, :], mx[:, n, :], -SCALE, None, ALU.mult).then_inc(dv_max, 1)

                    def recip(n):
                        wait(e, ac_exp, NS * it + n + 1)
                        e.reciprocal(rc[:, n, :], sm[:, n, :]).then_inc(dv_rc, 1)

                    for n in range(GT):
                        maxima(n)
                        if n:
                            recip(n - 1)
                    recip(GT - 1)
                    for c in range(DC):
                        for k in range(QK):
                            m, n = QK * c + k, GT * (c + 1) + k
                            if c + 1 < DC:
                                if k < GT:
                                    maxima(n)
                                if k:
                                    recip(n - 1)
                            wait(e, ac_t, QK * DC * it + m + 1)
                            e.tensor_tensor(pT[1][0:rows_of[k], k, :], ps[0:rows_of[k], 4 + m % 2, :],
                                            pT[0][0:rows_of[k], k, :].bitcast(F32), ALU.subtract).then_inc(dv_t, 1)
                        wait(e, ac_o, DC * it + c + 1)
                        e.tensor_tensor(oT[1][:, c, :], ps[:, 6 + c % 2, :], oT[0][:, c, :].bitcast(F32), ALU.subtract).then_inc(dv_o, 1)
                    wait(e, st_x1, 16 * it, alone=True)
                    wait(e, st_y, 32 * it, alone=True)
                    wait(e, pl_xb, GT * it + GT, alone=True)
                    for tt in range(GT):
                        wait(e, pe_w, GT * it + tt + 1)
                        e.tensor_tensor(x1[:, tt, :], ps[:, 4 + tt % 2, :], x_in[:, s, tt, :], ALU.add).then_inc(dv_x1, 1)
                    wait(e, dv_x1, GT * it + GT, alone=True)
                    moments(lambda tt: x1[:, tt, :])
                    wait(e, pl_rs, 2 * it + 2, alone=True)
                    for tt in range(GT):
                        e.tensor_scalar(y[:, tt, :], x1[:, tt, :], mv[:, tt, 0:1], rs[:, tt:tt + 1],
                                        ALU.subtract, ALU.mult).then_inc(dv_y, 1)
                    assert own[0] == OWN, own[0]

                run(e, lambda b: None, per_group)


def attention_sems(sem):
    s = {n: [sem(f"a_{n}{u}") for u in range(4)] for n in ("ld_h", "ld_rot", "ld_y", "st")}
    for n in ("ld_small", "ld_mask", "k_copy", "dv_own", "pe_h", "ac_h", "dv_h", "pe_qkv", "ac_sq", "dv_ssq", "pl_rn", "dv_norm",
              "pl_tab", "pl_m1", "pl_m2", "pl_rot", "ac_v", "dv_v", "pe_r", "ac_r", "dv_r", "pe_s", "dv_s", "ac_exp", "dv_rc", "dv_p",
              "pe_t", "ac_t", "dv_t", "pe_o", "ac_o", "dv_o", "pe_w", "dv_y", "pl_init"):
        s[n] = sem(f"a_{n}")
    return s


def attention_phase(nc, io, ps, ident, s, wait, Split, neg_half, l, dram, zero_row):
    LH = NT * HEADS

    with ExitStack() as st:
        def sb(name, shape, dt=F32):
            return st.enter_context(nc.sbuf_tensor(name, shape, dt))

        wqkv = [sb(f"wqkv_{x}", [P, DC, 3 * D], F32R) for x in "hl"]
        wo = [sb(f"wo_{x}", [P, DC, D], F32R) for x in "hl"]
        hT = [sb(f"hT_{x}", [P, DC, P], F32R) for x in "hl"]
        qT = [sb(f"qT_{x}", [P, 2, DC, P], F32R) for x in "hl"]
        kT = [sb(f"kT_{x}", [P, DC, 6, P], F32R) for x in "hl"]
        v = [sb(f"v_{x}", [P, 4, D], F32R) for x in "hl"]
        pT = [sb(f"pT_{x}", [P, 4, KEYS], F32R) for x in "hl"]
        oT = [sb(f"oT_{x}", [P, DC, P], F32R) for x in "hl"]
        h_in = sb("h_in", [P, 4, D])
        y_in = sb("y_in", [P, 4, D])
        rot = sb("rot", [P, 4, 4, DH])
        qk_scale = sb("qk_scale", [P, 4, DH])
        sq = sb("sq", [P, 2, D])
        ssq = sb("ssq", [P, 2, HEADS])
        rn = sb("rn", [P, 2, HEADS])
        qk = sb("qk", [P, 2, D])
        m1 = sb("m1", [P, 2, D])
        m2 = sb("m2", [P, 2, D])
        mask = sb("mask", [P, KEYS])
        mask01 = sb("mask01", [P, 2, KEYS])
        neg_s = sb("neg_s", [P, 4, KEYS])
        neg_m = sb("neg_m", [P, 4])
        prob = sb("prob", [P, 4, KEYS])
        sm = sb("sm", [P, 4])
        rc = sb("rc", [P, 4])

        def weight(name, width):
            src = io[name].rearrange("l k n -> (l k) n")
            return [src[bass.ds(l * D + k * P, P), :] for k in range(DC)]

        w = Split("w_attn", st, D,
                  [(a[:, j * D:(j + 1) * D], wqkv[0][:, k, j * D:(j + 1) * D], wqkv[1][:, k, j * D:(j + 1) * D])
                   for k, a in enumerate(weight("wqkv", 3 * D)) for j in range(3)]
                  + [(a, wo[0][:, k, :], wo[1][:, k, :]) for k, a in enumerate(weight("wo", D))], l)

        def at(total, i, per, k):
            return l * total + i * per + k if not isinstance(i, int) else l * total + (i * per + k)

        def need(e, name, total, i, per, k, alone=False):
            if isinstance(i, int) and i * per + k <= 0:
                return
            wait(e, s[name], at(total, i, per, k), alone or e is nc.sync)

        def tile_exists(i, j):
            return not isinstance(i, int) or 0 <= 4 * i + j < NT

        def loop(e, body):
            body(0)
            with e.Fori(1, NI - 1) as i:
                body(i)
            body(NI - 1)

        with nc.Block() as block:
            @block.sync
            def _(e):
                for a, name in enumerate(("q_scale", "k_scale")):
                    src = io[name][bass.ds(l, 1), :]
                    e.dma_start(qk_scale[:, 2 * a, :], src.to_broadcast([P, DH])).then_inc(s["ld_small"], 16)
                    for half in range(2):
                        e.dma_start(qk_scale[:, 2 * a + 1, half * DH // 2:(half + 1) * DH // 2],
                                    src[:, (1 - half) * DH // 2:(2 - half) * DH // 2].to_broadcast([P, DH // 2])).then_inc(s["ld_small"], 16)
                e.dma_start(mask[:], io["mask"]).then_inc(s["ld_small"], 16)
                for u in range(2):
                    e.dma_start(mask01[:, u, 2 * P:KEYS], io["mask"][:, 2 * P:KEYS]).then_inc(s["ld_small"], 16)

                def load_h(i, j):
                    if tile_exists(i, j):
                        r = i * 4 * P + j * P
                        r = r if isinstance(r, int) else e.snap(r)
                        need(e, "pe_h", NT, i, 4, j - 3)
                        e.dma_start(h_in[:, j % 4, 0:HALF], dram["src"][bass.ds(r, P), 0:HALF]).then_inc(s["ld_h"][j % 4], 16)
                        e.dma_start(h_in[:, j % 4, HALF:D], dram["src_late"][bass.ds(r, P), :]).then_inc(s["ld_h"][j % 4], 16)

                def load_tables(i, j):
                    if tile_exists(i, j):
                        r = i * 4 * P + j * P
                        r = r if isinstance(r, int) else e.snap(r)
                        need(e, "pl_rot", 2 * NT, i, 8, 2 * (j - 3))
                        e.dma_start(rot[:, j % 4], io["rot"][bass.ds(r, P), :].rearrange("p (a d) -> p a d", a=4)).then_inc(s["ld_rot"][j % 4], 16)

                def load_masks(i):
                    for u in range(2):
                        r = i * 2 * P + u * P
                        r = r if isinstance(r, int) else e.snap(r)
                        need(e, "dv_s", LH, i, 4 * HEADS, -2 * HEADS)
                        e.dma_start(mask01[:, u, 0:2 * P], io["mask01"][bass.ds(r, P), :]).then_inc(s["ld_mask"], 16)

                def store(i, j):
                    if tile_exists(i, j):
                        r = i * 4 * P + j * P
                        r2 = i * 4 * P + (j * P + 1)
                        if not isinstance(i, int):
                            r, r2 = e.snap(r), e.snap(r2)
                        need(e, "dv_y", NT, i, 4, j + 1)
                        e.dma_start(dram["dst"][bass.ds(r, P), :], y_in[:, j % 4, :]).then_inc(s["st"][j % 4], 16)
                        e.dma_start(dram["dst_late"][bass.ds(r2, P), :], y_in[:, j % 4, HALF:D]).then_inc(s["st"][j % 4], 16)

                def body(i):
                    for u in range(4):
                        r = i * 4 * P + u * P
                        r = r if isinstance(r, int) else e.snap(r)
                        if not isinstance(i, int) or i:
                            wait(e, s["st"][u], 32 * (l * NI) + i * 32, alone=True)
                        e.dma_start(y_in[:, u, :], dram["src"][bass.ds(r, P), :]).then_inc(s["ld_y"][u], 16)
                        load_h(i, u + 3)
                        load_tables(i, u + 2)
                        if u >= 2:
                            need(e, "dv_r", 2 * NT, i, 8, 2 * u + 2)
                            need(e, "pe_s", LH, i, 4 * HEADS, HEADS * (u - 1))
                            for part in range(2):
                                e.dma_start(kT[part][:, :, u - 2, :].bitcast(F32), kT[part][:, :, u + 2, :].bitcast(F32)).then_inc(s["k_copy"], 16)
                        if u == 2 and not (isinstance(i, int) and i == NI - 1):
                            load_masks(i + 1)
                        store(i, u - 1)

                load_h(0, 0)
                load_h(0, 1)
                load_h(0, 2)
                load_tables(0, 0)
                load_tables(0, 1)
                w.loads(e)
                load_masks(0)
                wait(e, s["pl_init"], 4 * l + 4, alone=True)
                loop(e, body)
                store(NI - 1, 3)
                wait(e, s["k_copy"], 64 * (l * NI) + 64 * NI, alone=True)
                for u in range(4):
                    wait(e, s["st"][u], 32 * (l * NI) + 32 * NI)
                e.dma_start(dram["dst_late"][N:N + 1, :], zero_row[:]).then_inc(s["ld_small"], 16)
                wait(e, s["ld_small"], 16 * 10 * l + 16 * 10)

            def token_major_heads(ap):
                return ap.rearrange("p (h d) -> p h d", h=HEADS)

            @block.gpsimd
            def _(e):
                for part in range(2):
                    e.memset(kT[part][:, :, 0:2, :].bitcast(F32), 0.0).then_inc(s["pl_init"], 1)
                    e.memset(v[part][:, 2:4, :].bitcast(F32), 0.0).then_inc(s["pl_init"], 1)
                wait(e, s["ld_small"], 16 * 10 * l + 16 * 9)

                def rotate(i, j):
                    if not tile_exists(i, j):
                        return
                    u = j % 4
                    if isinstance(i, int):
                        base = l * NI + (i + j // 4) + 1
                    else:
                        base = l * NI + i + (j // 4 + 1)
                    wait(e, s["ld_rot"][u], 16 * base)
                    e.tensor_tensor(rot[:, u], rot[:, u], qk_scale[:], ALU.mult).then_inc(s["pl_tab"], 1)
                    need(e, "pl_tab", NT, i, 4, j + 1)
                    hd = DH // 2
                    parts = [[token_major_heads(m[:, a, :]) for m in (qk, m1, m2)] for a in range(2)]
                    tabs = [rot[:, u, a, :].rearrange("p (o d) -> p o d", o=1) for a in range(4)]

                    def root(a):
                        need(e, "dv_ssq", 2 * NT, i, 8, 2 * j + a + 1)
                        e.tensor_tensor(rn[:, a, :], ssq[:, a, :], neg_half[:, 0:HEADS], ALU.pow).then_inc(s["pl_rn"], 1)

                    def times_cos(a):
                        need(e, "dv_norm", 2 * NT, i, 8, 2 * j + a + 1)
                        need(e, "pe_r", 2 * NT, i, 8, 2 * j + a - 1)
                        e.tensor_tensor(parts[a][1], parts[a][0], tabs[2 * a].to_broadcast([P, HEADS, DH]), ALU.mult).then_inc(s["pl_m1"], 1)

                    def plus_sin(a):
                        x, y1, y2 = parts[a]
                        for half in range(2):
                            here, there = (slice(z * hd, z * hd + hd) for z in (half, 1 - half))
                            e.tensor_tensor(y2[:, :, here], x[:, :, there], tabs[2 * a + 1][:, :, here].to_broadcast([P, HEADS, hd]),
                                            ALU.mult).then_inc(s["pl_m2"], 1)
                        need(e, "pl_m1", 2 * NT, i, 8, 2 * j + a + 1)
                        need(e, "pl_m2", 4 * NT, i, 16, 4 * j + 2 * a + 2)
                        e.tensor_tensor(y1, y1, y2, ALU.add).then_inc(s["pl_rot"], 1)

                    root(0)
                    times_cos(0)
                    root(1)
                    plus_sin(0)
                    times_cos(1)
                    plus_sin(1)

                rotate(0, 0)

                def body(i):
                    for u in range(4):
                        rotate(i, u + 1)

                loop(e, body)

            @block.tensor
            def _(e):
                def transpose_h(i, j):
                    if not tile_exists(i, j):
                        return
                    if isinstance(i, int):
                        base = l * NI + (i + j // 4) + 1
                    else:
                        base = l * NI + i + (j // 4 + 1)
                    wait(e, s["ld_h"][j % 4], 32 * base)
                    need(e, "dv_v", NT, i, 4, j)
                    for k in range(DC):
                        last = e.transpose(ps[:, 0, k * P:(k + 1) * P], h_in[:, j % 4, k * P:(k + 1) * P], ident[:])
                    last.then_inc(s["pe_h"], 1)

                def project(i, j, a):
                    if not tile_exists(i, j):
                        return
                    if a == 0:
                        need(e, "dv_h", NT, i, 4, j + 1)
                        need(e, "dv_r", 2 * NT, i, 8, 2 * j)
                    elif a == 1:
                        need(e, "dv_r", 2 * NT, i, 8, 2 * j)
                    else:
                        need(e, "dv_norm", 2 * NT, i, 8, 2 * j + 1)
                    for k in range(DC):
                        last = split_matmul(e, ps[:, a % 2, :], [x[:, k, :] for x in hT],
                                            [x[:, k, a * D:(a + 1) * D] for x in wqkv], k == 0, k == DC - 1)
                    last.then_inc(s["pe_qkv"], 1)

                def transpose_qk(i, j):
                    if not tile_exists(i, j):
                        return
                    for a in range(2):
                        need(e, "pl_rot", 2 * NT, i, 8, 2 * j + a + 1)
                        if a == 0:
                            need(e, "dv_norm", 2 * NT, i, 8, 2 * j + 2)
                            need(e, "dv_y", NT, i, 4, j - 1)
                        else:
                            need(e, "dv_v", NT, i, 4, j + 1)
                            if tile_exists(i, j + 1):
                                need(e, "dv_h", NT, i, 4, j + 2)
                        for c in range(DC):
                            last = e.transpose(ps[:, 1 - a, c * P:(c + 1) * P], m1[:, a, c * P:(c + 1) * P], ident[:])
                        last.then_inc(s["pe_r"], 1)

                def scores(i, u, h):
                    if not tile_exists(i, u):
                        return
                    n = HEADS * u + h
                    if h == 0:
                        need(e, "dv_r", 2 * NT, i, 8, 2 * u + 2)
                        if u % 4 == 0 and not (isinstance(i, int) and 4 * i + u == 0):
                            if isinstance(i, int):
                                wait(e, s["k_copy"], 64 * (l * NI) + 64 * (i + u // 4))
                            else:
                                wait(e, s["k_copy"], 64 * (l * NI) + i * 64 + 64 * (u // 4))
                    need(e, "dv_s", LH, i, 4 * HEADS, n - 1)
                    r = slice(DH * (h % 2), DH * (h % 2) + DH)
                    uu = u % 4
                    split_matmul(e, ps[:, 2 + h % 2, 0:KEYS], [x[r, uu % 2, h // 2, :] for x in qT],
                                 [x[r, h // 2, uu:uu + 3, :].rearrange("p a k -> p (a k)") for x in kT],
                                 True, True).then_inc(s["pe_s"], 1)

                def transpose_p(i, u, h):
                    n = HEADS * u + h
                    need(e, "dv_p", LH, i, 4 * HEADS, n + 1)
                    need(e, "dv_t", LH, i, 4 * HEADS, n - 1)
                    for k in range(3):
                        last = e.transpose(ps[:, 4 + h % 2, k * P:(k + 1) * P], prob[:, n % 4, k * P:(k + 1) * P], ident[:])
                    last.then_inc(s["pe_t"], 1)

                def values(i, u, h):
                    n = HEADS * u + h
                    need(e, "dv_t", LH, i, 4 * HEADS, n + 1)
                    if h == 0:
                        need(e, "dv_v", NT, i, 4, u + 1)
                    if h % 4 == 0:
                        need(e, "dv_o", 2 * NT, i, 8, 2 * u + h // 4 - 1)
                    for k in range(3):
                        slot = (u + 2 + k) % 4
                        last = split_matmul(e, ps[0:DH, 6 + h // 4, (h % 4) * P:(h % 4 + 1) * P],
                                            [x[:, slot, h * DH:(h + 1) * DH] for x in v],
                                            [x[:, n % 4, k * P:(k + 1) * P] for x in pT], k == 0, k == 2)
                    last.then_inc(s["pe_o"], 1)

                def output(i, u):
                    if u < 0 and isinstance(i, int) and i == 0:
                        return
                    need(e, "dv_o", 2 * NT, i, 8, 2 * u + 2)
                    if tile_exists(i, u + 2):
                        need(e, "dv_norm", 2 * NT, i, 8, 2 * u + 6)
                    else:
                        need(e, "dv_y", NT, i, 4, u)
                    for c in range(DC):
                        last = split_matmul(e, ps[:, 1, :], [x[:, c, :] for x in oT], [x[:, c, :] for x in wo], c == 0, c == DC - 1)
                    last.then_inc(s["pe_w"], 1)

                transpose_h(0, 0)
                w.done(e, 3 * DC)
                for a in range(3):
                    project(0, 0, a)
                transpose_h(0, 1)
                transpose_qk(0, 0)
                wait(e, s["pl_init"], 4 * l + 4)
                w.done(e)
                scores(0, 0, 0)
                scores(0, 0, 1)

                def body(i):
                    for u in range(4):
                        for h in range(HEADS):
                            if h < 6:
                                scores(i, u, h + 2)
                            else:
                                scores(i, u + 1, h - 6)
                            transpose_p(i, u, h)
                            if h:
                                values(i, u, h - 1)
                            elif not (isinstance(i, int) and i == 0 and u == 0):
                                values(i, u - 1, HEADS - 1)
                            if h < 3:
                                project(i, u + 1, h)
                            elif h == 3:
                                output(i, u - 1)
                            elif h == 4:
                                transpose_h(i, u + 2)
                            elif h == 5:
                                transpose_qk(i, u + 1)

                loop(e, body)
                values(NI - 1, 3, HEADS - 1)
                output(NI - 1, 3)

            @block.scalar
            def _(e):
                w.his(e)
                wait(e, s["pl_init"], 4 * l + 4)

                def hi_h(i, j):
                    if tile_exists(i, j):
                        need(e, "pe_h", NT, i, 4, j + 1)
                        e.activation(hT[0][:].rearrange("p c t -> p (c t)"), ps[:, 0, :], ACT.Copy).then_inc(s["ac_h"], 1)

                def squares(i, j, a):
                    if tile_exists(i, j):
                        need(e, "pe_qkv", 3 * NT, i, 12, 3 * j + a + 1)
                        e.activation(sq[:, a, :], ps[:, a, :], ACT.Square).then_inc(s["ac_sq"], 1)

                def hi_v(i, j):
                    if tile_exists(i, j):
                        need(e, "pe_qkv", 3 * NT, i, 12, 3 * j + 3)
                        need(e, "pe_o", LH, i, 4 * HEADS, HEADS * (j - 1))
                        e.activation(v[0][:, j % 4, :], ps[:, 0, :], ACT.Copy).then_inc(s["ac_v"], 1)

                def hi_qk(i, j):
                    if tile_exists(i, j):
                        for a in range(2):
                            need(e, "pe_r", 2 * NT, i, 8, 2 * j + a + 1)
                            if a == 0:
                                dst = qT[0][:, j % 2]
                            else:
                                dst = kT[0][:, :, 2 + j % 4, :]
                                if j % 4 >= 2:
                                    wait_copy(e, i, j)
                            e.activation(dst, ps[:, 1 - a, :].rearrange("p (c t) -> p c t", c=DC), ACT.Copy).then_inc(s["ac_r"], 1)

                def wait_copy(e, i, j):
                    if isinstance(i, int):
                        if i + j // 4 > 0:
                            wait(e, s["k_copy"], 64 * (l * NI) + 64 * (i + j // 4))
                    else:
                        wait(e, s["k_copy"], 64 * (l * NI) + i * 64 + 64 * (j // 4))

                def exponent(i, u, h):
                    if tile_exists(i, u):
                        n = HEADS * u + h
                        need(e, "dv_s", LH, i, 4 * HEADS, n + 1)
                        need(e, "pe_t", LH, i, 4 * HEADS, n - 3)
                        need(e, "dv_p", LH, i, 4 * HEADS, n - 3)
                        m = n % 4
                        e.activation(prob[:, m, :], neg_s[:, m, :], ACT.Exp, bias=neg_m[:, n % 4:n % 4 + 1], scale=-1.0,
                                     accum_out=sm[:, n % 4:n % 4 + 1]).then_inc(s["ac_exp"], 1)

                def hi_p(i, u, h):
                    n = HEADS * u + h
                    need(e, "pe_t", LH, i, 4 * HEADS, n + 1)
                    need(e, "pe_o", LH, i, 4 * HEADS, n - 3)
                    e.activation(pT[0][:, n % 4, :], ps[:, 4 + h % 2, 0:KEYS], ACT.Copy).then_inc(s["ac_t"], 1)

                def hi_o(i, u, half):
                    need(e, "pe_o", LH, i, 4 * HEADS, HEADS * u + 4 * half + 4)
                    if half == 0:
                        need(e, "pe_w", NT, i, 4, u)
                    for odd in range(2):
                        src = ps[0:DH, 6 + half, :].rearrange("p (c o t) -> p c o t", c=2, o=2)[:, :, odd, :]
                        e.activation(oT[0][DH * odd:DH * odd + DH, 2 * half:2 * half + 2, :], src, ACT.Copy).then_inc(s["ac_o"], 1)

                hi_h(0, 0)
                squares(0, 0, 0)
                squares(0, 0, 1)
                hi_v(0, 0)
                hi_h(0, 1)
                hi_qk(0, 0)
                exponent(0, 0, 0)
                exponent(0, 0, 1)

                def body(i):
                    for u in range(4):
                        for h in range(HEADS):
                            if h == 1:
                                squares(i, u + 1, 0)
                            elif h == 2:
                                squares(i, u + 1, 1)
                            elif h == 3:
                                hi_v(i, u + 1)
                            elif h == 5:
                                hi_h(i, u + 2)
                            elif h == 6:
                                hi_qk(i, u + 1)
                            hi_p(i, u, h)
                            if h < 6:
                                exponent(i, u, h + 2)
                            else:
                                exponent(i, u + 1, h - 6)
                            if h == 1 and not (isinstance(i, int) and i == 0 and u == 0):
                                hi_o(i, u - 1, 1)
                            elif h == 5:
                                hi_o(i, u, 0)

                loop(e, body)
                hi_o(NI - 1, 3, 1)

            @block.vector
            def _(e):
                w.los(e)
                wait(e, s["ld_small"], 16 * 10 * l + 16 * 9)
                wait(e, s["pl_init"], 4 * l + 4)

                def lo(out, bank, hi, done):
                    return e.tensor_tensor(out, bank, hi.bitcast(F32), ALU.subtract).then_inc(s[done], 1)

                def lo_h(i, j):
                    if tile_exists(i, j):
                        need(e, "ac_h", NT, i, 4, j + 1)
                        lo(hT[1][:].rearrange("p c t -> p (c t)"), ps[:, 0, :], hT[0][:].rearrange("p c t -> p (c t)"), "dv_h")

                def norms(i, j, a):
                    if tile_exists(i, j):
                        need(e, "ac_sq", 2 * NT, i, 8, 2 * j + a + 1)
                        e.tensor_reduce(ssq[:, a, :], token_major_heads(sq[:, a, :]), AX.X, ALU.add).then_inc(s["dv_own"], 1)
                        need(e, "dv_own", 2 * NT, i, 8, 2 * j + a + 1)
                        e.tensor_scalar(ssq[:, a, :], ssq[:, a, :], 1e-24, None, ALU.max).then_inc(s["dv_ssq"], 1)

                def normalise(i, j, a):
                    if tile_exists(i, j):
                        need(e, "pl_rn", 2 * NT, i, 8, 2 * j + a + 1)
                        need(e, "pl_rot", 2 * NT, i, 8, 2 * j + a - 1)
                        e.tensor_tensor(token_major_heads(qk[:, a, :]), token_major_heads(ps[:, a, :]),
                                        rn[:, a, :].rearrange("p (h o) -> p h o", o=1).to_broadcast([P, HEADS, DH]),
                                        ALU.mult).then_inc(s["dv_norm"], 1)

                def lo_v(i, j):
                    if tile_exists(i, j):
                        need(e, "ac_v", NT, i, 4, j + 1)
                        lo(v[1][:, j % 4, :], ps[:, 0, :], v[0][:, j % 4, :], "dv_v")

                def lo_qk(i, j):
                    if tile_exists(i, j):
                        for a in range(2):
                            need(e, "ac_r", 2 * NT, i, 8, 2 * j + a + 1)
                            hi, out = ((qT[x][:, j % 2] if a == 0 else kT[x][:, :, 2 + j % 4, :]) for x in range(2))
                            lo(out, ps[:, 1 - a, :].rearrange("p (c t) -> p c t", c=DC), hi, "dv_r")

                def masked(i, u, h):
                    if tile_exists(i, u):
                        n = HEADS * u + h
                        if h == 0 and u % 4 == 0:
                            if isinstance(i, int):
                                wait(e, s["ld_mask"], 32 * (l * NI) + 32 * (i + u // 4 + 1), alone=True)
                            else:
                                wait(e, s["ld_mask"], 32 * (l * NI) + i * 32 + 32 * (u // 4 + 1), alone=True)
                        need(e, "pe_s", LH, i, 4 * HEADS, n + 1, alone=True)
                        need(e, "ac_exp", LH, i, 4 * HEADS, n - 3, alone=True)
                        mk = mask01[:, u % 4, :] if u % 4 < 2 else mask[:]
                        e.tensor_tensor_reduce(out=neg_s[:, n % 4, :], in0=ps[:, 2 + h % 2, 0:KEYS], in1=mk, scale=-1.0,
                                               scalar=3.0e38, op0=ALU.add, op1=ALU.min, accum_out=neg_m[:, n % 4:n % 4 + 1]
                                               ).then_inc(s["dv_s"], 1)

                def divide(i, u, h):
                    if tile_exists(i, u):
                        n = HEADS * u + h
                        need(e, "ac_exp", LH, i, 4 * HEADS, n + 1)
                        e.reciprocal(rc[:, n % 4:n % 4 + 1], sm[:, n % 4:n % 4 + 1]).then_inc(s["dv_rc"], 1)
                        need(e, "dv_rc", LH, i, 4 * HEADS, n + 1)
                        e.tensor_scalar(prob[:, n % 4, :], prob[:, n % 4, :], rc[:, n % 4:n % 4 + 1], None, ALU.mult).then_inc(s["dv_p"], 1)

                def lo_p(i, u, h):
                    n = HEADS * u + h
                    need(e, "ac_t", LH, i, 4 * HEADS, n + 1)
                    lo(pT[1][:, n % 4, :], ps[:, 4 + h % 2, 0:KEYS], pT[0][:, n % 4, :], "dv_t")

                def lo_o(i, u, half):
                    need(e, "ac_o", 4 * NT, i, 16, 4 * u + 2 * half + 2)
                    for odd in range(2):
                        src = ps[0:DH, 6 + half, :].rearrange("p (c o t) -> p c o t", c=2, o=2)[:, :, odd, :]
                        r = slice(DH * odd, DH * odd + DH)
                        ins = e.tensor_tensor(oT[1][r, 2 * half:2 * half + 2, :], src,
                                              oT[0][r, 2 * half:2 * half + 2, :].bitcast(F32), ALU.subtract)
                    ins.then_inc(s["dv_o"], 1)

                def residual(i, u):
                    if isinstance(i, int):
                        if 4 * i + u < 0:
                            return
                        base = l * NI + (i + (u // 4)) + 1
                    else:
                        base = l * NI + i + (u // 4 + 1)
                    need(e, "pe_w", NT, i, 4, u + 1)
                    wait(e, s["ld_y"][u % 4], 16 * base)
                    e.tensor_tensor(y_in[:, u % 4, :], ps[:, 1, :], y_in[:, u % 4, :], ALU.add).then_inc(s["dv_y"], 1)

                lo_h(0, 0)
                for a in range(2):
                    norms(0, 0, a)
                    normalise(0, 0, a)
                lo_v(0, 0)
                lo_h(0, 1)
                lo_qk(0, 0)
                masked(0, 0, 0)
                masked(0, 0, 1)
                divide(0, 0, 0)

                def body(i):
                    for u in range(4):
                        for h in range(HEADS):
                            if h == 1:
                                norms(i, u + 1, 0)
                            elif h == 2:
                                normalise(i, u + 1, 0)
                                norms(i, u + 1, 1)
                            elif h == 3:
                                normalise(i, u + 1, 1)
                                lo_v(i, u + 1)
                            elif h == 4:
                                residual(i, u - 1)
                            elif h == 5:
                                lo_h(i, u + 2)
                            elif h == 6:
                                lo_qk(i, u + 1)
                            if h < 6:
                                masked(i, u, h + 2)
                            else:
                                masked(i, u + 1, h - 6)
                            if h < 7:
                                divide(i, u, h + 1)
                            else:
                                divide(i, u + 1, 0)
                            lo_p(i, u, h)
                            if h == 1 and not (isinstance(i, int) and i == 0 and u == 0):
                                lo_o(i, u - 1, 1)
                            elif h == 5:
                                lo_o(i, u, 0)

                loop(e, body)
                lo_o(NI - 1, 3, 1)
                residual(NI - 1, 3)


def ffn_sems(sem):
    return {n: sem(f"f_{n}") for n in (
        "ld_small", "ld_in", "ld_res", "st", "dv_own", "dv_ve", "pl_rs", "dv_z", "pe_x", "ac_x", "dv_xh", "dv_x",
        "pe_a", "pe_g", "ac_g", "dv_u", "ac_u", "dv_ul", "pe_y", "pl_res", "dv_y", "pl_o")}


def ffn_phase(nc, io, ps, ident, s, wait, Split, neg_half, l, dram, zero_row):
    rows_of = [P] * (MC - 1) + [TAIL]
    cols = [[(x * HID + m * P, x * HID + m * P + rows_of[m]) for x in range(2)] for m in range(MC)]
    OWN = 1 + GT

    with ExitStack() as st:
        def sb(name, shape, dt=F32):
            return st.enter_context(nc.sbuf_tensor(name, shape, dt))

        w1 = [sb(f"w1_{x}", [P, DC, 2 * HID], F32R) for x in "hl"]
        w2 = [sb(f"w2_{x}", [P, MC, D], F32R) for x in "hl"]
        xT = [sb(f"fxT_{x}", [P, DC, G], F32R) for x in "hl"]
        u = [sb(f"u_{x}", [P, 2, G], F32R) for x in "hl"]
        x_full = sb("x_full", [P, G])
        gate = sb("gate", [P, G])
        u_full = sb("u_full", [P, 2, G])
        h_in = sb("f_in", [P, GT, D])
        res = sb("f_res", [P, GT, D])
        x1 = sb("f_x1", [P, GT, D])
        lg, lb = sb("lg", [P, DC]), sb("lb", [P, DC])
        b1 = sb("b1_cols", [P, MC, 2])
        b2 = sb("b2_rows", [P, D])
        stats, mv = sb("f_stats", [P, GT, 6]), sb("f_mv", [P, GT, 2])
        ve, rs = sb("f_ve", [P, GT]), sb("f_rs", [P, GT])

        src1 = io["w1"].rearrange("l k n -> (l k) n")
        src2 = io["w2"].rearrange("l k n -> (l k) n")
        cuts = [0, 3 * P, 7 * P, HID]
        pieces = []
        for c0, c1 in zip(cuts, cuts[1:]):
            for x in range(2):
                for k in range(DC):
                    c = slice(x * HID + c0, x * HID + c1)
                    pieces.append((src1[bass.ds(l * D + k * P, P), c], w1[0][:, k, c], w1[1][:, k, c]))
        W1_FIRST = 2 * DC
        for m in range(MC):
            pieces.append((src2[bass.ds(l * HID + m * P, rows_of[m]), :], w2[0][0:rows_of[m], m, :], w2[1][0:rows_of[m], m, :]))
        w = Split("w_ffn", st, max(b - a for a, b in zip(cuts, cuts[1:])), pieces, l)

        def need(e, name, per, g, k, alone=False):
            if isinstance(g, int) and g * per + k <= 0:
                return
            value = l * (NG * per) + g * per + k if not isinstance(g, int) else l * (NG * per) + (g * per + k)
            wait(e, s[name], value, alone)

        def loop(e, body):
            with e.Fori(0, NG - 1) as g:
                body(g)
            body(NG - 1)

        SMALL = 6

        with nc.Block() as block:
            @block.sync
            def _(e):
                for name, t in (("ln_g", lg), ("ln_b", lb)):
                    e.dma_start(t[:], io[name][bass.ds(l * P, P), :]).then_inc(s["ld_small"], 16)
                e.dma_start(b1[:, 0:MC - 1, :], io["b1_main"][bass.ds(l * P, P), :].rearrange("p (m x) -> p m x", x=2)).then_inc(s["ld_small"], 16)
                e.dma_start(b1[0:TAIL, MC - 1, :], io["b1_tail"][bass.ds(l * TAIL, TAIL), :]).then_inc(s["ld_small"], 16)
                e.dma_start(b2[:], io["b2"][bass.ds(l, 1), :].to_broadcast([P, D])).then_inc(s["ld_small"], 16)

                def rows(ap, g, late=0):
                    r = g * G + late
                    r = r if isinstance(r, int) else e.snap(r)
                    return ap[bass.ds(r, G), :].rearrange("(t p) d -> p t d", p=P)

                def load_in(g, behind):
                    a, b = rows(dram["src"], g)[:, :, 0:HALF], rows(dram["src_late"], g)
                    need(e, "pe_x", DC, behind, DC) if behind is not None else None
                    e.dma_start(h_in[:, :, 0:HALF], a).then_inc(s["ld_in"], 16)
                    e.dma_start(h_in[:, :, HALF:D], b).then_inc(s["ld_in"], 16)

                def body(g):
                    a, b = rows(dram["src"], g), rows(dram["x1"], g)
                    if isinstance(g, int):
                        wait(e, s["st"], l * (48 * NG) + 48 * g)
                    else:
                        wait(e, s["st"], l * (48 * NG) + g * 48)
                    e.dma_start(res[:], a).then_inc(s["ld_res"], 16)
                    e.dma_start(x1[:], b).then_inc(s["ld_res"], 16)
                    if not isinstance(g, int):
                        load_in(g + 1, g)
                    d = [rows(dram["dst"], g), rows(dram["dst_late"], g, 1), rows(io["out"], g)]
                    need(e, "dv_y", GT, g, GT)
                    e.dma_start(d[0], res[:]).then_inc(s["st"], 16)
                    e.dma_start(d[1], res[:, :, HALF:D]).then_inc(s["st"], 16)
                    need(e, "pl_o", GT, g, GT)
                    e.dma_start(d[2], x1[:]).then_inc(s["st"], 16)

                load_in(0, None)
                w.loads(e)
                loop(e, body)
                wait(e, s["st"], l * (48 * NG) + 48 * NG)
                e.dma_start(dram["dst_late"][N:N + 1, :], zero_row[:]).then_inc(s["ld_small"], 16)
                wait(e, s["ld_small"], 16 * SMALL * l + 16 * SMALL)

            @block.gpsimd
            def _(e):
                def root(g):
                    need(e, "dv_ve", 1, g, 1)
                    e.tensor_tensor(rs[:], ve[:], neg_half[:, 0:GT], ALU.pow).then_inc(s["pl_rs"], 1)

                def body(g):
                    if isinstance(g, int):
                        wait(e, s["ld_res"], l * (32 * NG) + (32 * g + 32))
                    else:
                        wait(e, s["ld_res"], l * (32 * NG) + g * 32 + 32)
                    for tt in range(GT):
                        e.tensor_tensor(res[:, tt, :], res[:, tt, :], b2[:], ALU.add).then_inc(s["pl_res"], 1)
                    if not isinstance(g, int):
                        root(g + 1)
                    for tt in range(GT):
                        need(e, "dv_y", GT, g, tt + 1)
                        e.tensor_tensor(x1[:, tt, :], x1[:, tt, :], res[:, tt, :], ALU.add).then_inc(s["pl_o"], 1)

                wait(e, s["ld_small"], 16 * SMALL * l + 16 * (SMALL - 1))
                root(0)
                loop(e, body)

            @block.tensor
            def _(e):
                def transpose_x(g, k, behind):
                    need(e, "dv_z", GT, g, GT)
                    if k >= 2:
                        need(e, "dv_x", DC, g, k - 1)
                    elif behind is not None:
                        need(e, "dv_u", MC, behind, MC - 1)
                    for tt in range(GT):
                        last = e.transpose(ps[:, 2 + k % 2, tt * P:(tt + 1) * P], h_in[:, tt, k * P:(k + 1) * P], ident[:])
                    last.then_inc(s["pe_x"], 1)

                def hidden(g, m, peeled_first):
                    if m == 0:
                        need(e, "dv_x", DC, g, DC)
                    need(e, "dv_u", MC, g, m - 1 if m >= 2 else 0)
                    for x in range(2):
                        c = slice(*cols[m][x])
                        for k in range(DC):
                            last = split_matmul(e, ps[0:rows_of[m], 2 * (m % 2) + x, :], [y[:, k, c] for y in w1],
                                                [y[:, k, :] for y in xT], k == 0, k == DC - 1)
                        last.then_inc(s["pe_g" if x else "pe_a"], 1)

                def output(g, m, tts=range(GT)):
                    need(e, "dv_ul", MC, g, m + 1)
                    if m == 0:
                        need(e, "dv_y", GT, g, 0)
                    for tt in tts:
                        r = slice(0, rows_of[m])
                        last = split_matmul(e, ps[:, 4 + tt, :], [y[r, m % 2, tt * P:(tt + 1) * P] for y in u],
                                            [y[r, m, :] for y in w2], m == 0, m == MC - 1)
                        if m == MC - 1 or tt == GT - 1:
                            last.then_inc(s["pe_y"], 1)

                def body(g):
                    for m in range(MC):
                        hidden(g, m, False)
                        if m:
                            output(g, m - 1)
                    more = not isinstance(g, int)
                    if more:
                        transpose_x(g + 1, 0, g)
                        transpose_x(g + 1, 1, g)
                    output(g, MC - 1, range(2))
                    if more:
                        transpose_x(g + 1, 2, g)
                        transpose_x(g + 1, 3, g)
                    output(g, MC - 1, range(2, GT))

                for k in range(DC):
                    transpose_x(0, k, None)
                w.done(e)
                loop(e, body)

            @block.scalar
            def _(e):
                w.his(e)
                wait(e, s["ld_small"], 16 * SMALL * l + 16 * (SMALL - 1))

                def affine(g, k):
                    need(e, "pe_x", DC, g, k + 1)
                    need(e, "dv_x", DC, g, k)
                    e.activation(x_full[:], ps[:, 2 + k % 2, :], ACT.Identity, bias=lb[:, k:k + 1], scale=lg[:, k:k + 1]).then_inc(s["ac_x"], 1)

                def body(g):
                    for m in range(MC):
                        r = slice(0, rows_of[m])
                        need(e, "pe_g", MC, g, m + 1)
                        need(e, "dv_u", MC, g, m)
                        e.activation(gate[r, :], ps[r, 2 * (m % 2) + 1, :], ACT.Gelu, bias=b1[r, m, 1:2]).then_inc(s["ac_g"], 1)
                        need(e, "dv_u", MC, g, m + 1)
                        need(e, "pe_y", MC - 1 + GT, g, m - 1 if m >= 2 else 0)
                        e.activation(u[0][r, m % 2, :], u_full[r, m % 2, :], ACT.Copy).then_inc(s["ac_u"], 1)
                    if not isinstance(g, int):
                        for k in range(DC):
                            affine(g + 1, k)

                for k in range(DC):
                    affine(0, k)
                loop(e, body)

            @block.vector
            def _(e):
                w.los(e)
                wait(e, s["ld_small"], 16 * SMALL * l + 16 * (SMALL - 1))

                def normalise(g):
                    if isinstance(g, int):
                        wait(e, s["ld_in"], l * (32 * NG) + (32 * g + 32))
                    else:
                        wait(e, s["ld_in"], l * (32 * NG) + g * 32 + 32)
                    for tt in range(GT):
                        ins = e.bn_stats(stats[:, tt, :], h_in[:, tt, :])
                    ins.then_inc(s["dv_own"], 1)
                    need(e, "dv_own", OWN, g, 1, alone=True)
                    for tt in range(GT):
                        e.bn_aggr(mv[:, tt, :], stats[:, tt, :]).then_inc(s["dv_own"], 1)
                    need(e, "dv_own", OWN, g, OWN, alone=True)
                    e.tensor_scalar(ve[:].rearrange("p (t o) -> p t o", o=1), mv[:, :, 1:2], EPS, None, ALU.add).then_inc(s["dv_ve"], 1)
                    need(e, "pl_rs", 1, g, 1)
                    for tt in range(GT):
                        e.tensor_scalar(h_in[:, tt, :], h_in[:, tt, :], mv[:, tt, 0:1], rs[:, tt:tt + 1],
                                        ALU.subtract, ALU.mult).then_inc(s["dv_z"], 1)

                def split_x(g, k):
                    need(e, "ac_x", DC, g, k + 1)
                    e.tensor_copy(xT[0][:, k, :], x_full[:]).then_inc(s["dv_xh"], 1)
                    need(e, "dv_xh", DC, g, k + 1)
                    e.tensor_tensor(xT[1][:, k, :], x_full[:], xT[0][:, k, :].bitcast(F32), ALU.subtract).then_inc(s["dv_x"], 1)

                def body(g):
                    for m in range(MC):
                        r = slice(0, rows_of[m])
                        need(e, "pe_a", MC, g, m + 1)
                        need(e, "ac_g", MC, g, m + 1)
                        need(e, "dv_ul", MC, g, max(m - 1, 0))
                        e.scalar_tensor_tensor(out=u_full[r, m % 2, :], in0=ps[r, 2 * (m % 2), :], scalar=b1[r, m, 0:1],
                                               in1=gate[r, :], op0=ALU.add, op1=ALU.mult).then_inc(s["dv_u"], 1)
                        need(e, "ac_u", MC, g, m + 1)
                        e.tensor_tensor(u[1][r, m % 2, :], u_full[r, m % 2, :], u[0][r, m % 2, :].bitcast(F32), ALU.subtract).then_inc(s["dv_ul"], 1)
                        if m == 5 and not isinstance(g, int):
                            normalise(g + 1)
                    if not isinstance(g, int):
                        for k in range(2):
                            split_x(g + 1, k)
                    need(e, "pl_res", GT, g, GT)
                    for tt in range(GT):
                        need(e, "pe_y", MC - 1 + GT, g, MC + tt)
                        e.tensor_tensor(res[:, tt, :], ps[:, 4 + tt, :], res[:, tt, :], ALU.add).then_inc(s["dv_y"], 1)
                        if tt == 1 and not isinstance(g, int):
                            for k in range(2, DC):
                                split_x(g + 1, k)

                normalise(0)
                for k in range(DC):
                    split_x(0, k)
                loop(e, body)


def rotary_tables():
    half_idx = np.arange(0, DH, 2, dtype=np.float32)
    inv_freq = (np.float32(1.0) / np.float32(10000.0) ** (half_idx / np.float32(DH))).astype(np.float32)
    t = np.arange(N, dtype=np.float32)
    freqs = t[:, None] * inv_freq[None, :]
    freqs = np.concatenate([freqs, freqs], -1)
    base = (half_idx + np.float32(0.4 * DH)) / np.float32(1.4 * DH)
    power = (t - np.float32(N // 2)) / np.float32(WIN // 2)
    scale = base[None, :] ** power[:, None]
    scale = np.concatenate([scale, scale], -1)
    cos, sin = np.cos(freqs), np.sin(freqs)
    sin[:, :DH // 2] = -sin[:, :DH // 2]
    tab = np.concatenate([cos * scale * 8, sin * scale * 8, cos / scale, sin / scale], -1).astype(np.float32)
    return np.concatenate([tab] * B, 0)


def window_masks():
    q, k = np.arange(P)[:, None], np.arange(KEYS)[None, :] - 2 * P
    mask = np.where((k <= q) & (q <= k + WIN), np.float32(0), np.float32(MASKED)).astype(np.float32)
    first = np.repeat(mask[None, None, :, 0:2 * P], NI, 0).repeat(2, 1)
    for i in range(0, NI, NI // B):
        first[i, 0] = MASKED
        first[i, 1, :, 0:P] = MASKED
    return mask, np.ascontiguousarray(first.reshape(NI * 2 * P, 2 * P))


def kernel(**inputs):
    import concourse.bacc as bacc
    from concourse.bass_utils import run_bass_kernel_spmd

    a = {k: np.asarray(v) for k, v in inputs.items()}
    x_, f_ = "L0_xattn_", "L0_ffn_"
    mask, mask01 = window_masks()
    b1 = a[f_ + "b1"].reshape(DEPTH, 2, HID)
    main = (MC - 1) * P
    arrays = {
        "x": a["x"].reshape(T, D), "ctx": a["ctx_1024"].reshape(B * SC, D),
        "WqT": a[x_ + "Wq"].T, "WkT": a[x_ + "Wk"].T, "WvT": a[x_ + "Wv"].T, "WoT": a[x_ + "Wo"].T,
        "bq": a[x_ + "bq"].reshape(DC, P).T, "bk": a[x_ + "bk"].reshape(DC, P).T,
        "bv": a[x_ + "bv"].reshape(1, D), "bo": a[x_ + "bo"].reshape(1, D),
        "wqkv": a[f_ + "wqkv"], "q_scale": a[f_ + "q_scale"], "k_scale": a[f_ + "k_scale"], "wo": a[f_ + "wo"],
        "ln_g": a[f_ + "ln_g"].reshape(DEPTH, DC, P).transpose(0, 2, 1).reshape(DEPTH * P, DC),
        "ln_b": a[f_ + "ln_b"].reshape(DEPTH, DC, P).transpose(0, 2, 1).reshape(DEPTH * P, DC),
        "w1": a[f_ + "w1"], "w2": a[f_ + "w2"],
        "b1_main": b1[:, :, :main].reshape(DEPTH, 2, MC - 1, P).transpose(0, 3, 2, 1).reshape(DEPTH * P, 2 * (MC - 1)),
        "b1_tail": b1[:, :, main:].transpose(0, 2, 1).reshape(DEPTH * TAIL, 2),
        "b2": a[f_ + "b2"], "rot": rotary_tables(), "mask": mask, "mask01": mask01,
    }
    arrays = {k: np.ascontiguousarray(v) for k, v in arrays.items()}
    nc = bacc.Bacc("TRN2", target_bir_lowering=False, num_devices=1)
    io = {k: nc.dram_tensor(f"in_{k}", v.shape, mybir.dt.from_np(v.dtype), kind="ExternalInput").ap()
          for k, v in arrays.items()}
    io["out"] = nc.dram_tensor("out_rows", (T, D), F32, kind="ExternalOutput").ap()
    build(nc, io)
    r = run_bass_kernel_spmd(nc, [{f"in_{k}": v for k, v in arrays.items()}], core_ids=[0])
    return r.results[0]["out_rows"].reshape(B, N, D)
```

```python
from contextlib import ExitStack

import numpy as np

import concourse.bass as bass
from concourse import mybir

F32 = mybir.dt.float32
F32R = mybir.dt.float32r
ACT = mybir.ActivationFunctionType
ALU = mybir.AluOpType
AX = mybir.AxisListType

P = 128
B, N, D = 2, 2048, 512
T = B * N
DC = D // P
HALF = D // 2
SC, XH = 154, 16
XD = D // XH
SCH = SC // 2
QUAD = P // XD
QW = QUAD * SC
QK = -(-QW // P)
DEPTH, HEADS, DH, WIN = 2, 8, 64, 256
HID = int(D * 4 * 2 / 3)
MC = -(-HID // P)
TAIL = HID - (MC - 1) * P
GT = 4
G = GT * P
NT = T // P
NG = T // G
NI = NT // 4
KEYS = 3 * P
EPS = 1e-5
MASKED = -3.0e38
SLOTS = 4


FROM_ONE = ("c_ac_k", "c_dv_t", "c_dv_vf", "c_out", "c_pe_t", "x_ac_exp", "x_dv_x1", "x_pe_o", "x_st_x1",
            "x_st_y", "f_dv_u", "f_dv_ul", "f_dv_y", "f_pe_y", "f_st")


def split_matmul(pe, out, a, b, start, stop):
    (a_h, a_l), (b_h, b_l) = a, b
    pe.matmul(out, a_h, b_h, start=start, stop=False)
    pe.matmul(out, a_h, b_l, start=False, stop=False)
    return pe.matmul(out, a_l, b_h, start=False, stop=stop)


def build(nc, io):
    ctx = ExitStack()

    from_one = {name: nc.alloc_semaphore(name) for name in FROM_ONE}

    def sem(name):
        return from_one[name] if name in from_one else nc.alloc_semaphore(name)

    passed = sem("passed")

    def wait(e, s, value, alone=False):
        if isinstance(value, int) and value <= 0:
            return
        if any(s is one for one in from_one.values()):
            value = value + 1
        assert isinstance(value, int) or value.min_val > 0, s
        e.wait_ge(s, value)
        if (alone or e is nc.sync) and not isinstance(value, int):
            e.sem_inc(passed, 1)

    def scratch(name, shape, dt=F32):
        return nc.dram_tensor(name, shape, dt, kind="Internal").ap()

    x1_rows = scratch("x1_rows", (T, D))
    y_rows = scratch("y_rows", (T, D))
    y_late = scratch("y_late", (T + 1, HALF))
    z_rows = scratch("z_rows", (T, D))
    z_late = scratch("z_late", (T + 1, HALF))
    ctx_k = scratch("ctx_k", (B * 2 * P, DC * SC))
    ctx_v = scratch("ctx_v", (B * 2 * SC, D))

    ps = ctx.enter_context(nc.psum_tensor("banks", [P, 8, 512], F32))
    ident = ctx.enter_context(nc.sbuf_tensor("ident", [P, P], F32))
    neg_half = ctx.enter_context(nc.sbuf_tensor("neg_half", [P, 2 * HEADS], F32))
    zero_row = ctx.enter_context(nc.sbuf_tensor("zero_row", [1, HALF], F32))
    consts_done = sem("consts_done")

    class Split:

        def __init__(self, name, stack, width, pieces, l=0):
            self.l, self.pieces = l, pieces
            self.stage = stack.enter_context(nc.sbuf_tensor(f"{name}_stage", [P, SLOTS, width], F32))
            self.loaded = split_sems[name][0:SLOTS]
            self.hi_done, self.lo_done = split_sems[name][SLOTS:]

        def slot(self, n):
            shape = self.pieces[n][0].shape
            at = self.stage[0:shape[0], n % SLOTS, 0:int(np.prod(shape[1:]))]
            return at if len(shape) == 2 else at.rearrange("p (a b) -> p a b", a=shape[1])

        def each(self, n0, n1):
            return range(n0, len(self.pieces) if n1 is None else n1)

        def loads(self, e, n0=0, n1=None):
            for n in self.each(n0, n1):
                wait(e, self.lo_done, self.l * len(self.pieces) + n - SLOTS + 1 if n >= SLOTS else 0)
                e.dma_start(self.slot(n), self.pieces[n][0]).then_inc(self.loaded[n % SLOTS], 16)

        def his(self, e, n0=0, n1=None):
            for n in self.each(n0, n1):
                total = len(range(n % SLOTS, len(self.pieces), SLOTS))
                wait(e, self.loaded[n % SLOTS], 16 * (self.l * total + n // SLOTS + 1))
                e.activation(self.pieces[n][1], self.slot(n), ACT.Copy).then_inc(self.hi_done, 1)

        def los(self, e, n0=0, n1=None):
            for n in self.each(n0, n1):
                wait(e, self.hi_done, self.l * len(self.pieces) + n + 1)
                e.tensor_tensor(self.pieces[n][2], self.slot(n), self.pieces[n][1].bitcast(F32),
                                ALU.subtract).then_inc(self.lo_done, 1)

        def done(self, e, n=None):
            n = len(self.pieces) if n is None else n
            wait(e, self.lo_done, self.l * len(self.pieces) + n, alone=True)

    split_sems = {name: [sem(f"{name}_{x}") for x in (*range(SLOTS), "hi", "lo")]
                  for name in ("w_ctx", "w_attn", "w_ffn")}

    with nc.Block() as block:
        @block.gpsimd
        def _(e):
            for one in from_one.values():
                e.sem_inc(one, 1)

    with ExitStack() as shared:
        def sb(name, shape):
            return [shared.enter_context(nc.sbuf_tensor(f"{name}_{x}", shape, F32R)) for x in "hl"]

        keep = dict(wq=sb("wq", [P, DC, D]), wo=sb("xwo", [P, DC, D]),
                    k_bd=sb("k_bd", [P, DC, 2, SC]),
                    v_bd=sb("v_bd", [P, DC, QK, P]))
        context_phase(nc, io, ps, ident, sem, wait, Split, dict(ctx_k=ctx_k, ctx_v=ctx_v),
                      neg_half, zero_row, consts_done, (y_late, z_late), keep)
        cross_phase(nc, io, ps, ident, sem, wait, neg_half,
                    dict(ctx_k=ctx_k, ctx_v=ctx_v, x1=x1_rows, y=y_rows, late=y_late), zero_row, keep)
    attn_sems = attention_sems(sem)
    ffn_s = ffn_sems(sem)
    with nc.Fori(0, DEPTH) as l:
        attention_phase(nc, io, ps, ident, attn_sems, wait, Split, neg_half, l,
                        dict(src=y_rows, src_late=y_late, dst=z_rows, dst_late=z_late), zero_row)
        ffn_phase(nc, io, ps, ident, ffn_s, wait, Split, neg_half, l,
                  dict(src=z_rows, src_late=z_late, dst=y_rows, dst_late=y_late, x1=x1_rows),
                  zero_row)
    ctx.close()


def context_phase(nc, io, ps, ident, sem, wait, Split, dram, neg_half, zero_row, consts_done,
                  lates, keep):
    ld_small, ld_ctx, out_done, zero_done = sem("c_small"), sem("c_ctx"), sem("c_out"), sem("c_zero")
    ident_zeroed = sem("ident_zeroed")
    pe_t, ac_t, dv_t = sem("c_pe_t"), sem("c_ac_t"), sem("c_dv_t")
    pe_k, ac_k, ac_kh, dv_k = sem("c_pe_k"), sem("c_ac_k"), sem("c_ac_kh"), sem("c_dv_k")
    pe_v, dv_vf, ac_v, dv_v = sem("c_pe_v"), sem("c_dv_vf"), sem("c_ac_v"), sem("c_dv_v")
    with ExitStack() as st:
        def sb(name, shape, dt=F32):
            return st.enter_context(nc.sbuf_tensor(name, shape, dt))

        wk = [sb(f"wk_{x}", [P, DC, D], F32R) for x in "hl"]
        wv = [sb(f"wv_{x}", [P, DC, D], F32R) for x in "hl"]
        bk = sb("bk_cols", [P, DC])
        bv = sb("bv_rows", [SCH, D])
        c_in = sb("c_in", [SCH, 2, D])
        cT = [sb(f"cT_{x}", [P, DC, SC], F32R) for x in "hl"]
        k_full = sb("k_full", [P, DC, SC])
        kT = [sb(f"ctx_kT_{x}", [P, DC, SC], F32R) for x in "hl"]
        v_full = sb("v_full", [SCH, 2, D])
        v = [sb(f"ctx_v_{x}", [SCH, 2, D], F32R) for x in "hl"]
        w = Split("w_ctx", st, D, [(io[name][k * P:(k + 1) * P, :], t[0][:, k, :], t[1][:, k, :])
                                   for name, t in (("WkT", wk), ("WvT", wv), ("WqT", keep["wq"]), ("WoT", keep["wo"]))
                                   for k in range(DC)])
        NOW = 2 * DC
        k_dram = dram["ctx_k"].rearrange("r (c s) -> r c s", c=DC)

        with nc.Block() as block:
            @block.sync
            def _(e):
                e.dma_start(bk[:], io["bk"]).then_inc(ld_small, 16)
                e.dma_start(bv[:], io["bv"].to_broadcast([SCH, D])).then_inc(ld_small, 16)
                w.loads(e, 0, NOW + SLOTS)
                wait(e, consts_done, 3)
                for late in lates:
                    for b in range(B):
                        e.dma_start(late[b * N:b * N + 1, :], zero_row[:]).then_inc(zero_done, 16)
                with e.Fori(0, B) as b:
                    wait(e, pe_t, b * DC)
                    e.dma_start(c_in[:], io["ctx"][bass.ds(b * SC, SC), :]
                                .rearrange("(h p) d -> p h d", p=SCH)).then_inc(ld_ctx, 16)
                    wait(e, dv_k, b + 1)
                    for part in range(2):
                        e.dma_start(k_dram[bass.ds(b * 2 * P + part * P, P)], kT[part][:].bitcast(F32)).then_inc(out_done, 16)
                    wait(e, dv_v, b + 1)
                    for part in range(2):
                        e.dma_start(dram["ctx_v"][bass.ds(b * 2 * SC + part * SC, SC), :]
                                    .rearrange("(h p) d -> p h d", p=SCH), v[part][:].bitcast(F32)).then_inc(out_done, 16)
                w.loads(e, NOW + SLOTS)
                wait(e, out_done, 16 * 4 * B)
                wait(e, zero_done, 16 * 2 * B)

            @block.gpsimd
            def _(e):
                e.memset(neg_half[:], -0.5).then_inc(consts_done, 1)
                e.memset(zero_row[:], 0.0).then_inc(consts_done, 1)
                e.memset(ident[:], 0.0).then_inc(ident_zeroed, 1)
                wait(e, ident_zeroed, 1)
                e.affine_select(out=ident[:], in_=ident[:], compare_op=ALU.not_equal, fill=1.0, base=0,
                                pattern=[[-1, P]], channel_multiplier=1).then_inc(consts_done, 1)
                for t in keep["k_bd"] + keep["v_bd"]:
                    e.memset(t[:].bitcast(F32), 0.0)

            @block.tensor
            def _(e):
                wait(e, consts_done, 3)
                with e.Fori(0, B) as b:
                    wait(e, ld_ctx, 16 * b + 16)
                    for c in range(DC):
                        if c == 0:
                            wait(e, dv_t, 2 * b)
                        for h in range(2):
                            last = e.transpose(ps[:, c // 2, (c % 2) * SC + h * SCH:(c % 2) * SC + (h + 1) * SCH],
                                               c_in[:, h, c * P:(c + 1) * P], ident[0:SCH, 0:SCH])
                        last.then_inc(pe_t, 1)
                    w.done(e, NOW)
                    wait(e, dv_t, 2 * b + 2)
                    wait(e, ac_k, 2 * b)
                    for c in range(DC):
                        for k in range(DC):
                            last = split_matmul(e, ps[:, 2 + c // 2, (c % 2) * SC:(c % 2 + 1) * SC],
                                                [x[:, k, c * P:(c + 1) * P] for x in wk],
                                                [x[:, k, :] for x in cT], k == 0, k == DC - 1)
                        last.then_inc(pe_k, 1)
                    wait(e, dv_vf, 2 * b)
                    for h in range(2):
                        for k in range(DC):
                            last = split_matmul(e, ps[0:SCH, 4 + h, :],
                                                [x[:, k, h * SCH:(h + 1) * SCH] for x in cT],
                                                [x[:, k, :] for x in wv], k == 0, k == DC - 1)
                        last.then_inc(pe_v, 1)

            @block.scalar
            def _(e):
                w.his(e, 0, NOW)
                wait(e, ld_small, 32)
                with e.Fori(0, B) as b:
                    for j in range(2):
                        wait(e, pe_t, b * DC + 2 * j + 2)
                        e.activation(cT[0][:, 2 * j:2 * j + 2, :],
                                     ps[:, j, 0:2 * SC].rearrange("p (c s) -> p c s", c=2), ACT.Copy).then_inc(ac_t, 1)
                    wait(e, pe_k, DC * b + DC)
                    for c in range(DC):
                        ins = e.activation(k_full[:, c, :], ps[:, 2 + c // 2, (c % 2) * SC:(c % 2 + 1) * SC],
                                           ACT.Identity, bias=bk[:, c:c + 1])
                        if c % 2:
                            ins.then_inc(ac_k, 1)
                    wait(e, ac_k, 2 * b + 2)
                    wait(e, out_done, 64 * b, alone=True)
                    e.activation(kT[0][:], k_full[:], ACT.Copy).then_inc(ac_kh, 1)
                    wait(e, dv_vf, 2 * b + 2)
                    e.activation(v[0][:], v_full[:], ACT.Copy).then_inc(ac_v, 1)
                w.his(e, NOW)

            @block.vector
            def _(e):
                w.los(e, 0, NOW)
                wait(e, ld_small, 32)
                with e.Fori(0, B) as b:
                    for j in range(2):
                        wait(e, ac_t, 2 * b + j + 1)
                        e.tensor_tensor(cT[1][:, 2 * j:2 * j + 2, :],
                                        ps[:, j, 0:2 * SC].rearrange("p (c s) -> p c s", c=2),
                                        cT[0][:, 2 * j:2 * j + 2, :].bitcast(F32), ALU.subtract).then_inc(dv_t, 1)
                    wait(e, ac_kh, b + 1)
                    e.tensor_tensor(kT[1][:], k_full[:], kT[0][:].bitcast(F32), ALU.subtract).then_inc(dv_k, 1)
                    for h in range(2):
                        wait(e, pe_v, 2 * b + h + 1)
                        e.tensor_tensor(v_full[:, h, :], ps[0:SCH, 4 + h, :], bv[:], ALU.add).then_inc(dv_vf, 1)
                    wait(e, ac_v, b + 1)
                    e.tensor_tensor(v[1][:], v_full[:], v[0][:].bitcast(F32), ALU.subtract).then_inc(dv_v, 1)
                w.los(e, NOW)


def cross_phase(nc, io, ps, ident, sem, wait, neg_half, dram, zero_row, keep):
    ld_small, ld_kv = sem("x_small"), sem("x_kv")
    ld_x = [sem(f"x_ld{s}") for s in range(2)]
    st_x1, st_y = sem("x_st_x1"), sem("x_st_y")
    dv_own, dv_ve, pl_rs, dv_xn, pl_xb = sem("x_dv_own"), sem("x_dv_ve"), sem("x_pl_rs"), sem("x_dv_xn"), sem("x_pl_xb")
    pe_x, ac_x, dv_x = sem("x_pe_x"), sem("x_ac_x"), sem("x_dv_x")
    pe_q, ac_q, dv_q = sem("x_pe_q"), sem("x_ac_q"), sem("x_dv_q")
    pe_s, dv_max, ac_exp, dv_rc, pl_p = sem("x_pe_s"), sem("x_dv_max"), sem("x_ac_exp"), sem("x_dv_rc"), sem("x_pl_p")
    pe_t, ac_t, dv_t = sem("x_pe_t"), sem("x_ac_t"), sem("x_dv_t")
    pe_o, ac_o, dv_o = sem("x_pe_o"), sem("x_ac_o"), sem("x_dv_o")
    pe_w, dv_x1, dv_y = sem("x_pe_w"), sem("x_dv_x1"), sem("x_dv_y")
    dv_vy, pl_ry = sem("x_dv_vy"), sem("x_pl_ry")
    NS = DC * GT
    NM = DC * QK
    SCALE = float(XD) ** -0.5
    rows_of = [min(P, QW - k * P) for k in range(QK)]
    segments = [(r, k, max(SC * r, P * k), min(SC * (r + 1), P * (k + 1)))
                for r in range(QUAD) for k in range(QK) if max(SC * r, P * k) < min(SC * (r + 1), P * (k + 1))]
    KV_LOADS = 2 * (QUAD + len(segments))
    LEAD = 1 + GT
    OWN = LEAD + 2 * GT + NS
    wq, wo, k_bd, v_bd = keep["wq"], keep["wo"], keep["k_bd"], keep["v_bd"]

    with ExitStack() as st:
        def sb(name, shape, dt=F32):
            return st.enter_context(nc.sbuf_tensor(name, shape, dt))

        bq = sb("bq_cols", [P, DC])
        bo = sb("bo_rows", [P, D])
        x_in = sb("x_in", [P, 2, GT, D])
        xn = sb("xn", [P, GT, D])
        stats, stats_y = sb("x_stats", [P, GT, 6]), sb("y_stats", [P, GT, 6])
        mv, mv_y = sb("x_mv", [P, GT, 2]), sb("y_mv", [P, GT, 2])
        ve, ve_y = sb("x_ve", [P, GT]), sb("y_ve", [P, GT])
        rs, rs_y = sb("x_rs", [P, GT]), sb("y_rs", [P, GT])
        xT = [sb(f"xT_{x}", [P, DC, G], F32R) for x in "hl"]
        qT = [sb(f"xqT_{x}", [P, DC, G], F32R) for x in "hl"]
        mx = sb("x_mx", [P, NS, QUAD])
        nmx = sb("x_nmx", [P, NS, QUAD])
        sm = sb("x_sm", [P, NS, QUAD])
        rc = sb("x_rc", [P, NS, QUAD])
        prob = sb("x_prob", [P, 2, GT, QW])
        pT = [sb(f"xpT_{x}", [P, QK, G], F32R) for x in "hl"]
        oT = [sb(f"xoT_{x}", [P, DC, G], F32R) for x in "hl"]
        x1 = sb("x1_t", [P, GT, D])
        y = sb("y0_t", [P, GT, D])
        k_dram = dram["ctx_k"].rearrange("r (c s) -> r c s", c=DC)

        def run(e, per_group, per_batch=lambda b: None):
            with e.Fori(0, B) as b:
                per_batch(b)
                with e.Fori(0, NG // B // 2) as gg:
                    for s in range(2):
                        pair = e.snap(b * (NG // B // 2) + gg)
                        it = e.snap(b * (NG // B) + gg * 2 + s)
                        per_group(it, s, pair)

        with nc.Block() as block:
            @block.sync
            def _(e):
                def rows(ap, it, late=0):
                    return ap[bass.ds(it * G + late, G), :].rearrange("(t p) d -> p t d", p=P)

                for s in range(2):
                    e.dma_start(x_in[:, s], rows(io["x"], s)).then_inc(ld_x[s], 16)
                e.dma_start(bq[:], io["bq"]).then_inc(ld_small, 16)
                e.dma_start(bo[:], io["bo"].to_broadcast([P, D])).then_inc(ld_small, 16)

                def per_batch(b):
                    src_k = [k_dram[bass.ds(b * 2 * P + part * P, P)] for part in range(2)]
                    src_v = [dram["ctx_v"][bass.ds(b * 2 * SC + part * SC, SC), :]
                             .rearrange("s (c n) -> s c n", c=DC) for part in range(2)]
                    wait(e, pe_o, b * (NG // B) * DC)
                    for part in range(2):
                        for r in range(QUAD):
                            e.dma_start(k_bd[part][r * XD:(r + 1) * XD, :, r % 2, :].bitcast(F32),
                                        src_k[part][r * XD:(r + 1) * XD]).then_inc(ld_kv, 16)
                    for part in range(2):
                        for r, k, f0, f1 in segments:
                            e.dma_start(v_bd[part][f0 - k * P:f1 - k * P, :, k, r * XD:(r + 1) * XD].bitcast(F32),
                                        src_v[part][f0 - r * SC:f1 - r * SC, :, r * XD:(r + 1) * XD]).then_inc(ld_kv, 16)

                def per_group(it, s, pair):
                    dst = [rows(dram["x1"], it), rows(dram["y"], it), rows(dram["late"], it, 1)]
                    nxt = e.snap((it + 2) % NG)
                    src = rows(io["x"], nxt)
                    wait(e, dv_x1, GT * it + GT)
                    e.dma_start(dst[0], x1[:]).then_inc(st_x1, 16)
                    e.dma_start(x_in[:, s], src).then_inc(ld_x[s], 16)
                    wait(e, dv_y, GT * it + GT)
                    e.dma_start(dst[1], y[:]).then_inc(st_y, 16)
                    e.dma_start(dst[2], y[:, :, HALF:D]).then_inc(st_y, 16)

                run(e, per_group, per_batch)
                wait(e, st_x1, 16 * NG)
                wait(e, st_y, 32 * NG)
                for s in range(2):
                    wait(e, ld_x[s], 16 * (NG // 2 + 1))
                e.dma_start(dram["late"][N:N + 1, :], zero_row[:]).then_inc(st_y, 16)
                wait(e, st_y, 32 * NG + 16)

            @block.gpsimd
            def _(e):
                wait(e, ld_small, 32)

                def root(count):
                    wait(e, dv_ve, count)
                    e.tensor_tensor(rs[:], ve[:], neg_half[:, 0:GT], ALU.pow).then_inc(pl_rs, 1)

                def per_group(it, s, pair):
                    wait(e, dv_xn, GT * it + GT)
                    for tt in range(GT):
                        e.tensor_tensor(x_in[:, s, tt, :], x_in[:, s, tt, :], bo[:], ALU.add).then_inc(pl_xb, 1)
                    for n in range(NS):
                        c, tt = divmod(n, GT)
                        p4 = prob[:, c % 2, tt, :].rearrange("p (r s) -> p r s", r=QUAD)
                        wait(e, dv_rc, NS * it + n + 1)
                        e.tensor_tensor(p4, p4, rc[:, n, :].rearrange("p (r o) -> p r o", o=1)
                                        .to_broadcast([P, QUAD, SC]), ALU.mult).then_inc(pl_p, 1)
                    root(it + 2)
                    for tt in range(GT):
                        wait(e, dv_vy, GT * it + tt + 1)
                        e.tensor_tensor(rs_y[:, tt:tt + 1], ve_y[:, tt:tt + 1], neg_half[:, 0:1], ALU.pow).then_inc(pl_ry, 1)

                root(1)
                run(e, per_group)

            @block.tensor
            def _(e):
                def transpose_x(it):
                    wait(e, dv_xn, GT * it + GT)
                    for k in range(DC):
                        for tt in range(GT):
                            last = e.transpose(ps[:, k, tt * P:(tt + 1) * P], xn[:, tt, k * P:(k + 1) * P], ident[:])
                        last.then_inc(pe_x, 1)

                def per_batch(b):
                    wait(e, ld_kv, 16 * KV_LOADS * b + 16 * KV_LOADS, alone=True)

                def per_group(it, s, pair):
                    def queries(c):
                        for k in range(DC):
                            last = split_matmul(e, ps[:, 4 + c, :], [x[:, k, c * P:(c + 1) * P] for x in wq],
                                                [x[:, k, :] for x in xT], k == 0, k == DC - 1)
                        last.then_inc(pe_q, 1)

                    def scores(n):
                        c, tt = divmod(n, GT)
                        if tt == 0:
                            wait(e, dv_q, DC * it + c + 1)
                        wait(e, ac_exp, NS * it + n - 1 if n >= 2 else NS * it)
                        for pair_ in range(2):
                            r = slice(64 * pair_, 64 * pair_ + 64)
                            last = split_matmul(e, ps[:, 2 * (n % 2) + pair_, 0:2 * SC],
                                                [x[r, c, tt * P:(tt + 1) * P] for x in qT],
                                                [x[r, c, :, :].rearrange("p a s -> p (a s)") for x in k_bd], True, True)
                        last.then_inc(pe_s, 1)

                    def transpose_p(m):
                        c, k = divmod(m, QK)
                        if k == 0:
                            wait(e, pl_p, NS * it + GT * (c + 1))
                        wait(e, dv_q if m < 2 else dv_t, DC * it + m + 1 if m < 2 else NM * it + m - 1)
                        for tt in range(GT):
                            last = e.transpose(ps[0:rows_of[k], 4 + m % 2, tt * P:(tt + 1) * P],
                                               prob[:, c % 2, tt, k * P:k * P + rows_of[k]], ident[:])
                        last.then_inc(pe_t, 1)

                    def values(m):
                        c, k = divmod(m, QK)
                        if m == 0:
                            wait(e, dv_q, DC * it + DC)
                        if k == 0 and c >= 2:
                            wait(e, dv_o, DC * it + c - 1)
                        wait(e, dv_t, NM * it + m + 1)
                        last = split_matmul(e, ps[:, 6 + c % 2, :], [x[0:rows_of[k], c, k, :] for x in v_bd],
                                            [x[0:rows_of[k], k, :] for x in pT], k == 0, k == QK - 1)
                        if k == QK - 1:
                            last.then_inc(pe_o, 1)

                    wait(e, dv_x, DC * it + DC)
                    wait(e, dv_x1, GT * it)
                    queries(0)
                    queries(1)
                    scores(0)
                    scores(1)
                    queries(2)
                    scores(2)
                    scores(3)
                    queries(3)
                    for m in range(NM):
                        c, k = divmod(m, QK)
                        transpose_p(m)
                        if c + 1 < DC and k < GT:
                            scores(GT * (c + 1) + k)
                        if m >= 2:
                            values(m - 2)
                    values(NM - 2)
                    values(NM - 1)
                    transpose_x(it + 1)
                    wait(e, dv_o, DC * it + DC)
                    for tt in range(GT):
                        for c in range(DC):
                            last = split_matmul(e, ps[:, 4 + tt, :], [x[:, c, tt * P:(tt + 1) * P] for x in oT],
                                                [x[:, c, :] for x in wo], c == 0, c == DC - 1)
                        last.then_inc(pe_w, 1)

                transpose_x(0)
                run(e, per_group, per_batch)

            @block.scalar
            def _(e):
                wait(e, ld_small, 32)

                def hi_x(it):
                    for k in range(DC):
                        wait(e, pe_x, DC * it + k + 1)
                        e.activation(xT[0][:, k, :], ps[:, k, :], ACT.Copy).then_inc(ac_x, 1)

                def per_group(it, s, pair):
                    def hi_q(c):
                        wait(e, pe_q, DC * it + c + 1)
                        e.activation(qT[0][:, c, :], ps[:, 4 + c, :], ACT.Identity, bias=bq[:, c:c + 1]).then_inc(ac_q, 1)

                    def exps(n):
                        c, tt = divmod(n, GT)
                        wait(e, dv_max, NS * it + n + 1)
                        for r in range(QUAD):
                            ins = e.activation(prob[:, c % 2, tt, r * SC:(r + 1) * SC],
                                               ps[:, 2 * (n % 2) + r // 2, (r % 2) * SC:(r % 2 + 1) * SC], ACT.Exp,
                                               bias=nmx[:, n, r:r + 1], scale=SCALE, accum_out=sm[:, n, r:r + 1])
                        ins.then_inc(ac_exp, 1)

                    def hi_o(c):
                        wait(e, pe_o, DC * it + c + 1)
                        e.activation(oT[0][:, c, :], ps[:, 6 + c % 2, :], ACT.Copy).then_inc(ac_o, 1)

                    hi_q(0)
                    hi_q(1)
                    exps(0)
                    exps(1)
                    hi_q(2)
                    exps(2)
                    exps(3)
                    hi_q(3)
                    for m in range(NM):
                        c, k = divmod(m, QK)
                        wait(e, pe_t, NM * it + m + 1)
                        e.activation(pT[0][0:rows_of[k], k, :], ps[0:rows_of[k], 4 + m % 2, :], ACT.Copy).then_inc(ac_t, 1)
                        if c + 1 < DC and k < GT:
                            exps(GT * (c + 1) + k)
                        if c and k == 1:
                            hi_o(c - 1)
                    hi_o(DC - 1)
                    hi_x(it + 1)

                hi_x(0)
                run(e, per_group)

            @block.vector
            def _(e):
                wait(e, ld_small, 32)
                own = [0, 0]

                def mark(ins):
                    ins.then_inc(dv_own, 1)
                    own[0] += 1

                def settle():
                    wait(e, dv_own, own[1] + own[0], alone=True)

                def moments(s, tiles):
                    for tt in tiles:
                        ins = e.bn_stats(stats[:, tt, :], x_in[:, s, tt, :])
                    if GT - 1 in tiles:
                        mark(ins)
                        settle()
                        for tt in range(GT):
                            mark(e.bn_aggr(mv[:, tt, :], stats[:, tt, :]))
                        settle()
                        e.tensor_scalar(ve[:].rearrange("p (t o) -> p t o", o=1), mv[:, :, 1:2], EPS, None, ALU.add).then_inc(dv_ve, 1)

                def normalise(it, s):
                    wait(e, pl_rs, it + 1, alone=True)
                    for tt in range(GT):
                        e.tensor_scalar(xn[:, tt, :], x_in[:, s, tt, :], mv[:, tt, 0:1], rs[:, tt:tt + 1],
                                        ALU.subtract, ALU.mult).then_inc(dv_xn, 1)

                def lo_x(it):
                    for k in range(DC):
                        wait(e, ac_x, DC * it + k + 1)
                        e.tensor_tensor(xT[1][:, k, :], ps[:, k, :], xT[0][:, k, :].bitcast(F32), ALU.subtract).then_inc(dv_x, 1)

                def per_group(it, s, pair):
                    own[0], own[1] = LEAD, OWN * it

                    def lo_q(c):
                        wait(e, ac_q, DC * it + c + 1)
                        e.scalar_tensor_tensor(out=qT[1][:, c, :], in0=ps[:, 4 + c, :], scalar=bq[:, c:c + 1],
                                               in1=qT[0][:, c, :].bitcast(F32), op0=ALU.add, op1=ALU.subtract).then_inc(dv_q, 1)

                    def maxima(n):
                        wait(e, pe_s, NS * it + n + 1)
                        b0 = 2 * (n % 2)
                        mark(e.tensor_reduce(mx[:, n, :].rearrange("p (a r) -> p a r", a=2),
                                             ps[:, b0:b0 + 2, 0:2 * SC].rearrange("p a (r s) -> p a r s", r=2), AX.X, ALU.max))
                        settle()
                        e.tensor_scalar(nmx[:, n, :], mx[:, n, :], -SCALE, None, ALU.mult).then_inc(dv_max, 1)

                    def recip(n):
                        wait(e, ac_exp, NS * it + n + 1)
                        e.reciprocal(rc[:, n, :], sm[:, n, :]).then_inc(dv_rc, 1)

                    def lo_o(c):
                        wait(e, ac_o, DC * it + c + 1)
                        e.tensor_tensor(oT[1][:, c, :], ps[:, 6 + c % 2, :], oT[0][:, c, :].bitcast(F32), ALU.subtract).then_inc(dv_o, 1)

                    lo_q(0)
                    lo_q(1)
                    maxima(0)
                    maxima(1)
                    recip(0)
                    lo_q(2)
                    maxima(2)
                    recip(1)
                    maxima(3)
                    recip(2)
                    lo_q(3)
                    recip(3)
                    for m in range(NM):
                        c, k = divmod(m, QK)
                        n = GT * (c + 1) + k
                        if c + 1 < DC:
                            if k < GT:
                                maxima(n)
                            if k:
                                recip(n - 1)
                        wait(e, ac_t, NM * it + m + 1)
                        e.tensor_tensor(pT[1][0:rows_of[k], k, :], ps[0:rows_of[k], 4 + m % 2, :],
                                        pT[0][0:rows_of[k], k, :].bitcast(F32), ALU.subtract).then_inc(dv_t, 1)
                        if c and k == 1:
                            lo_o(c - 1)
                        if c == DC - 1:
                            if k == 0:
                                wait(e, ld_x[1 - s], 16 * pair + 16 * (s + 1), alone=True)
                                moments(1 - s, (0, 1))
                            elif k == 2:
                                moments(1 - s, (2, 3))
                            elif k == 3:
                                normalise(it + 1, 1 - s)
                    lo_o(DC - 1)
                    lo_x(it + 1)
                    wait(e, st_x1, 16 * it, alone=True)
                    wait(e, st_y, 32 * it, alone=True)
                    wait(e, pl_xb, GT * it + GT, alone=True)

                    def finish(tt):
                        wait(e, pl_ry, GT * it + tt + 1)
                        e.tensor_scalar(y[:, tt, :], x1[:, tt, :], mv_y[:, tt, 0:1], rs_y[:, tt:tt + 1],
                                        ALU.subtract, ALU.mult).then_inc(dv_y, 1)

                    for tt in range(GT):
                        wait(e, pe_w, GT * it + tt + 1)
                        e.tensor_tensor(x1[:, tt, :], ps[:, 4 + tt, :], x_in[:, s, tt, :], ALU.add).then_inc(dv_x1, 1)
                        if tt:
                            finish(tt - 1)
                        wait(e, dv_x1, GT * it + tt + 1, alone=True)
                        mark(e.bn_stats(stats_y[:, tt, :], x1[:, tt, :]))
                        settle()
                        mark(e.bn_aggr(mv_y[:, tt, :], stats_y[:, tt, :]))
                        settle()
                        e.tensor_scalar(ve_y[:, tt:tt + 1], mv_y[:, tt, 1:2], EPS, None, ALU.add).then_inc(dv_vy, 1)
                    finish(GT - 1)
                    assert own[0] == LEAD + OWN, own[0]

                wait(e, ld_x[0], 16)
                moments(0, range(GT))
                normalise(0, 0)
                lo_x(0)
                run(e, per_group)


def attention_sems(sem):
    s = {n: [sem(f"a_{n}{u}") for u in range(4)] for n in ("ld_h", "ld_rot", "ld_y", "st")}
    for n in ("ld_small", "ld_mask", "k_copy", "dv_own", "pe_h", "ac_h", "dv_h", "pe_qkv", "ac_sq", "dv_ssq", "pl_rn", "dv_norm",
              "pl_tab", "pl_m1", "pl_m2", "pl_rot", "ac_v", "dv_v", "pe_r", "ac_r", "dv_r", "pe_s", "dv_s", "ac_exp", "dv_rc", "dv_p",
              "pe_t", "ac_t", "dv_t", "pe_o", "ac_o", "dv_o", "pe_w", "dv_y", "pl_init"):
        s[n] = sem(f"a_{n}")
    return s


def attention_phase(nc, io, ps, ident, s, wait, Split, neg_half, l, dram, zero_row):
    LH = NT * HEADS

    with ExitStack() as st:
        def sb(name, shape, dt=F32):
            return st.enter_context(nc.sbuf_tensor(name, shape, dt))

        wqkv = [sb(f"wqkv_{x}", [P, DC, 3 * D], F32R) for x in "hl"]
        wo = [sb(f"wo_{x}", [P, DC, D], F32R) for x in "hl"]
        hT = [sb(f"hT_{x}", [P, DC, P], F32R) for x in "hl"]
        qT = [sb(f"qT_{x}", [P, 2, DC, P], F32R) for x in "hl"]
        kT = [sb(f"kT_{x}", [P, DC, 6, P], F32R) for x in "hl"]
        v = [sb(f"v_{x}", [P, 4, D], F32R) for x in "hl"]
        pT = [sb(f"pT_{x}", [P, 4, KEYS], F32R) for x in "hl"]
        oT = [sb(f"oT_{x}", [P, DC, P], F32R) for x in "hl"]
        h_in = sb("h_in", [P, 4, D])
        y_in = sb("y_in", [P, 4, D])
        rot = sb("rot", [P, 4, 4, DH])
        qk_scale = sb("qk_scale", [P, 4, DH])
        sq = sb("sq", [P, 2, D])
        ssq = sb("ssq", [P, 2, HEADS])
        rn = sb("rn", [P, 2, HEADS])
        qk = sb("qk", [P, 2, D])
        m1 = sb("m1", [P, 2, D])
        m2 = sb("m2", [P, 2, D])
        mask = sb("mask", [P, KEYS])
        mask01 = sb("mask01", [P, 2, KEYS])
        neg_s = sb("neg_s", [P, 4, KEYS])
        neg_m = sb("neg_m", [P, 4])
        prob = sb("prob", [P, 4, KEYS])
        sm = sb("sm", [P, 4])
        rc = sb("rc", [P, 4])

        def weight(name, width):
            src = io[name].rearrange("l k n -> (l k) n")
            return [src[bass.ds(l * D + k * P, P), :] for k in range(DC)]

        w = Split("w_attn", st, D,
                  [(a[:, j * D:(j + 1) * D], wqkv[0][:, k, j * D:(j + 1) * D], wqkv[1][:, k, j * D:(j + 1) * D])
                   for k, a in enumerate(weight("wqkv", 3 * D)) for j in range(3)]
                  + [(a, wo[0][:, k, :], wo[1][:, k, :]) for k, a in enumerate(weight("wo", D))], l)

        def at(total, i, per, k):
            return l * total + i * per + k if not isinstance(i, int) else l * total + (i * per + k)

        def need(e, name, total, i, per, k, alone=False):
            if isinstance(i, int) and i * per + k <= 0:
                return
            wait(e, s[name], at(total, i, per, k), alone or e is nc.sync)

        def tile_exists(i, j):
            return not isinstance(i, int) or 0 <= 4 * i + j < NT

        def loop(e, body):
            body(0)
            with e.Fori(1, NI - 1) as i:
                body(i)
            body(NI - 1)

        with nc.Block() as block:
            @block.sync
            def _(e):
                for a, name in enumerate(("q_scale", "k_scale")):
                    src = io[name][bass.ds(l, 1), :]
                    e.dma_start(qk_scale[:, 2 * a, :], src.to_broadcast([P, DH])).then_inc(s["ld_small"], 16)
                    for half in range(2):
                        e.dma_start(qk_scale[:, 2 * a + 1, half * DH // 2:(half + 1) * DH // 2],
                                    src[:, (1 - half) * DH // 2:(2 - half) * DH // 2].to_broadcast([P, DH // 2])).then_inc(s["ld_small"], 16)
                e.dma_start(mask[:], io["mask"]).then_inc(s["ld_small"], 16)
                for u in range(2):
                    e.dma_start(mask01[:, u, 2 * P:KEYS], io["mask"][:, 2 * P:KEYS]).then_inc(s["ld_small"], 16)

                def load_h(i, j):
                    if tile_exists(i, j):
                        r = i * 4 * P + j * P
                        r = r if isinstance(r, int) else e.snap(r)
                        need(e, "pe_h", NT, i, 4, j - 3)
                        e.dma_start(h_in[:, j % 4, 0:HALF], dram["src"][bass.ds(r, P), 0:HALF]).then_inc(s["ld_h"][j % 4], 16)
                        e.dma_start(h_in[:, j % 4, HALF:D], dram["src_late"][bass.ds(r, P), :]).then_inc(s["ld_h"][j % 4], 16)

                def load_tables(i, j):
                    if tile_exists(i, j):
                        r = i * 4 * P + j * P
                        r = r if isinstance(r, int) else e.snap(r)
                        need(e, "pl_rot", 2 * NT, i, 8, 2 * (j - 3))
                        e.dma_start(rot[:, j % 4], io["rot"][bass.ds(r, P), :].rearrange("p (a d) -> p a d", a=4)).then_inc(s["ld_rot"][j % 4], 16)

                def load_masks(i):
                    for u in range(2):
                        r = i * 2 * P + u * P
                        r = r if isinstance(r, int) else e.snap(r)
                        need(e, "dv_s", LH, i, 4 * HEADS, -2 * HEADS)
                        e.dma_start(mask01[:, u, 0:2 * P], io["mask01"][bass.ds(r, P), :]).then_inc(s["ld_mask"], 16)

                def store(i, j):
                    if tile_exists(i, j):
                        r = i * 4 * P + j * P
                        r2 = i * 4 * P + (j * P + 1)
                        if not isinstance(i, int):
                            r, r2 = e.snap(r), e.snap(r2)
                        need(e, "dv_y", NT, i, 4, j + 1)
                        e.dma_start(dram["dst"][bass.ds(r, P), :], y_in[:, j % 4, :]).then_inc(s["st"][j % 4], 16)
                        e.dma_start(dram["dst_late"][bass.ds(r2, P), :], y_in[:, j % 4, HALF:D]).then_inc(s["st"][j % 4], 16)

                def body(i):
                    for u in range(4):
                        r = i * 4 * P + u * P
                        r = r if isinstance(r, int) else e.snap(r)
                        if not isinstance(i, int) or i:
                            wait(e, s["st"][u], 32 * (l * NI) + i * 32, alone=True)
                        e.dma_start(y_in[:, u, :], dram["src"][bass.ds(r, P), :]).then_inc(s["ld_y"][u], 16)
                        load_h(i, u + 3)
                        load_tables(i, u + 2)
                        if u >= 2:
                            need(e, "dv_r", 2 * NT, i, 8, 2 * u + 2)
                            need(e, "pe_s", LH, i, 4 * HEADS, HEADS * (u - 1))
                            for part in range(2):
                                e.dma_start(kT[part][:, :, u - 2, :].bitcast(F32), kT[part][:, :, u + 2, :].bitcast(F32)).then_inc(s["k_copy"], 16)
                        if u == 2 and not (isinstance(i, int) and i == NI - 1):
                            load_masks(i + 1)
                        store(i, u - 1)

                load_h(0, 0)
                load_h(0, 1)
                load_h(0, 2)
                load_tables(0, 0)
                load_tables(0, 1)
                w.loads(e)
                load_masks(0)
                wait(e, s["pl_init"], 4 * l + 4, alone=True)
                loop(e, body)
                store(NI - 1, 3)
                wait(e, s["k_copy"], 64 * (l * NI) + 64 * NI, alone=True)
                for u in range(4):
                    wait(e, s["st"][u], 32 * (l * NI) + 32 * NI)
                e.dma_start(dram["dst_late"][N:N + 1, :], zero_row[:]).then_inc(s["ld_small"], 16)
                wait(e, s["ld_small"], 16 * 10 * l + 16 * 10)

            def token_major_heads(ap):
                return ap.rearrange("p (h d) -> p h d", h=HEADS)

            @block.gpsimd
            def _(e):
                for part in range(2):
                    e.memset(kT[part][:, :, 0:2, :].bitcast(F32), 0.0).then_inc(s["pl_init"], 1)
                    e.memset(v[part][:, 2:4, :].bitcast(F32), 0.0).then_inc(s["pl_init"], 1)
                wait(e, s["ld_small"], 16 * 10 * l + 16 * 9)

                def rotate(i, j):
                    if not tile_exists(i, j):
                        return
                    u = j % 4
                    if isinstance(i, int):
                        base = l * NI + (i + j // 4) + 1
                    else:
                        base = l * NI + i + (j // 4 + 1)
                    wait(e, s["ld_rot"][u], 16 * base)
                    e.tensor_tensor(rot[:, u], rot[:, u], qk_scale[:], ALU.mult).then_inc(s["pl_tab"], 1)
                    need(e, "pl_tab", NT, i, 4, j + 1)
                    hd = DH // 2
                    parts = [[token_major_heads(m[:, a, :]) for m in (qk, m1, m2)] for a in range(2)]
                    tabs = [rot[:, u, a, :].rearrange("p (o d) -> p o d", o=1) for a in range(4)]

                    def root(a):
                        need(e, "dv_ssq", 2 * NT, i, 8, 2 * j + a + 1)
                        e.tensor_tensor(rn[:, a, :], ssq[:, a, :], neg_half[:, 0:HEADS], ALU.pow).then_inc(s["pl_rn"], 1)

                    def times_cos(a):
                        need(e, "dv_norm", 2 * NT, i, 8, 2 * j + a + 1)
                        need(e, "pe_r", 2 * NT, i, 8, 2 * j + a - 1)
                        e.tensor_tensor(parts[a][1], parts[a][0], tabs[2 * a].to_broadcast([P, HEADS, DH]), ALU.mult).then_inc(s["pl_m1"], 1)

                    def plus_sin(a):
                        x, y1, y2 = parts[a]
                        for half in range(2):
                            here, there = (slice(z * hd, z * hd + hd) for z in (half, 1 - half))
                            e.tensor_tensor(y2[:, :, here], x[:, :, there], tabs[2 * a + 1][:, :, here].to_broadcast([P, HEADS, hd]),
                                            ALU.mult).then_inc(s["pl_m2"], 1)
                        need(e, "pl_m1", 2 * NT, i, 8, 2 * j + a + 1)
                        need(e, "pl_m2", 4 * NT, i, 16, 4 * j + 2 * a + 2)
                        e.tensor_tensor(y1, y1, y2, ALU.add).then_inc(s["pl_rot"], 1)

                    root(0)
                    times_cos(0)
                    root(1)
                    plus_sin(0)
                    times_cos(1)
                    plus_sin(1)

                rotate(0, 0)

                def body(i):
                    for u in range(4):
                        rotate(i, u + 1)

                loop(e, body)

            @block.tensor
            def _(e):
                def transpose_h(i, j):
                    if not tile_exists(i, j):
                        return
                    if isinstance(i, int):
                        base = l * NI + (i + j // 4) + 1
                    else:
                        base = l * NI + i + (j // 4 + 1)
                    wait(e, s["ld_h"][j % 4], 32 * base)
                    need(e, "dv_r", 2 * NT, i, 8, 2 * j)
                    for k in range(DC):
                        last = e.transpose(ps[:, 0, k * P:(k + 1) * P], h_in[:, j % 4, k * P:(k + 1) * P], ident[:])
                    last.then_inc(s["pe_h"], 1)

                def project(i, j, a):
                    if not tile_exists(i, j):
                        return
                    if a == 0:
                        need(e, "dv_h", NT, i, 4, j + 1)
                        need(e, "dv_r", 2 * NT, i, 8, 2 * j)
                    elif a == 1:
                        need(e, "dv_r", 2 * NT, i, 8, 2 * j)
                    else:
                        need(e, "dv_norm", 2 * NT, i, 8, 2 * j + 1)
                    for k in range(DC):
                        last = split_matmul(e, ps[:, a % 2, :], [x[:, k, :] for x in hT],
                                            [x[:, k, a * D:(a + 1) * D] for x in wqkv], k == 0, k == DC - 1)
                    last.then_inc(s["pe_qkv"], 1)

                def transpose_qk(i, j):
                    if not tile_exists(i, j):
                        return
                    for a in range(2):
                        need(e, "pl_rot", 2 * NT, i, 8, 2 * j + a + 1)
                        if a == 0:
                            need(e, "dv_norm", 2 * NT, i, 8, 2 * j + 2)
                            need(e, "dv_y", NT, i, 4, j - 1)
                        else:
                            need(e, "dv_v", NT, i, 4, j + 1)
                        for c in range(DC):
                            last = e.transpose(ps[:, 1 - a, c * P:(c + 1) * P], m1[:, a, c * P:(c + 1) * P], ident[:])
                        last.then_inc(s["pe_r"], 1)

                def scores(i, u, h):
                    if not tile_exists(i, u):
                        return
                    n = HEADS * u + h
                    if h == 0:
                        need(e, "dv_r", 2 * NT, i, 8, 2 * u + 2)
                        if u % 4 == 0 and not (isinstance(i, int) and 4 * i + u == 0):
                            if isinstance(i, int):
                                wait(e, s["k_copy"], 64 * (l * NI) + 64 * (i + u // 4))
                            else:
                                wait(e, s["k_copy"], 64 * (l * NI) + i * 64 + 64 * (u // 4))
                    need(e, "dv_s", LH, i, 4 * HEADS, n - 1)
                    r = slice(DH * (h % 2), DH * (h % 2) + DH)
                    uu = u % 4
                    split_matmul(e, ps[:, 2 + h % 2, 0:KEYS], [x[r, uu % 2, h // 2, :] for x in qT],
                                 [x[r, h // 2, uu:uu + 3, :].rearrange("p a k -> p (a k)") for x in kT],
                                 True, True).then_inc(s["pe_s"], 1)

                def transpose_p(i, u, h):
                    n = HEADS * u + h
                    need(e, "dv_p", LH, i, 4 * HEADS, n + 1)
                    need(e, "dv_t", LH, i, 4 * HEADS, n - 1)
                    for k in range(3):
                        last = e.transpose(ps[:, 4 + h % 2, k * P:(k + 1) * P], prob[:, n % 4, k * P:(k + 1) * P], ident[:])
                    last.then_inc(s["pe_t"], 1)

                def values(i, u, h):
                    n = HEADS * u + h
                    need(e, "dv_t", LH, i, 4 * HEADS, n + 1)
                    if h == 0:
                        need(e, "dv_v", NT, i, 4, u + 1)
                    if h % 4 == 0:
                        need(e, "dv_o", 2 * NT, i, 8, 2 * u + h // 4 - 1)
                    for k in range(3):
                        slot = (u + 2 + k) % 4
                        last = split_matmul(e, ps[0:DH, 6 + h // 4, (h % 4) * P:(h % 4 + 1) * P],
                                            [x[:, slot, h * DH:(h + 1) * DH] for x in v],
                                            [x[:, n % 4, k * P:(k + 1) * P] for x in pT], k == 0, k == 2)
                    last.then_inc(s["pe_o"], 1)

                def output(i, u):
                    if u < 0 and isinstance(i, int) and i == 0:
                        return
                    need(e, "dv_o", 2 * NT, i, 8, 2 * u + 2)
                    if tile_exists(i, u + 2):
                        need(e, "dv_norm", 2 * NT, i, 8, 2 * u + 6)
                    else:
                        need(e, "dv_y", NT, i, 4, u)
                    for c in range(DC):
                        last = split_matmul(e, ps[:, 1, :], [x[:, c, :] for x in oT], [x[:, c, :] for x in wo], c == 0, c == DC - 1)
                    last.then_inc(s["pe_w"], 1)

                transpose_h(0, 0)
                w.done(e, 3 * DC)
                for a in range(3):
                    project(0, 0, a)
                transpose_qk(0, 0)
                transpose_h(0, 1)
                project(0, 1, 0)
                wait(e, s["pl_init"], 4 * l + 4)
                w.done(e)
                scores(0, 0, 0)
                scores(0, 0, 1)

                def body(i):
                    for u in range(4):
                        for h in range(HEADS):
                            if h < 6:
                                scores(i, u, h + 2)
                            else:
                                scores(i, u + 1, h - 6)
                            transpose_p(i, u, h)
                            if h == 4:
                                transpose_qk(i, u + 1)
                            if h:
                                values(i, u, h - 1)
                            elif not (isinstance(i, int) and i == 0 and u == 0):
                                values(i, u - 1, HEADS - 1)
                            if h < 2:
                                project(i, u + 1, h + 1)
                            elif h == 3:
                                output(i, u - 1)
                            elif h == 5:
                                transpose_h(i, u + 2)
                            elif h == 7:
                                project(i, u + 2, 0)

                loop(e, body)
                values(NI - 1, 3, HEADS - 1)
                output(NI - 1, 3)

            @block.scalar
            def _(e):
                w.his(e)
                wait(e, s["pl_init"], 4 * l + 4)

                def hi_h(i, j):
                    if tile_exists(i, j):
                        need(e, "pe_h", NT, i, 4, j + 1)
                        e.activation(hT[0][:].rearrange("p c t -> p (c t)"), ps[:, 0, :], ACT.Copy).then_inc(s["ac_h"], 1)

                def squares(i, j, a):
                    if tile_exists(i, j):
                        need(e, "pe_qkv", 3 * NT, i, 12, 3 * j + a + 1)
                        e.activation(sq[:, a, :], ps[:, a, :], ACT.Square).then_inc(s["ac_sq"], 1)

                def hi_v(i, j):
                    if tile_exists(i, j):
                        need(e, "pe_qkv", 3 * NT, i, 12, 3 * j + 3)
                        need(e, "pe_o", LH, i, 4 * HEADS, HEADS * (j - 1))
                        e.activation(v[0][:, j % 4, :], ps[:, 0, :], ACT.Copy).then_inc(s["ac_v"], 1)

                def hi_qk(i, j):
                    if tile_exists(i, j):
                        for a in range(2):
                            need(e, "pe_r", 2 * NT, i, 8, 2 * j + a + 1)
                            if a == 0:
                                dst = qT[0][:, j % 2]
                            else:
                                dst = kT[0][:, :, 2 + j % 4, :]
                                if j % 4 >= 2:
                                    wait_copy(e, i, j)
                            e.activation(dst, ps[:, 1 - a, :].rearrange("p (c t) -> p c t", c=DC), ACT.Copy).then_inc(s["ac_r"], 1)

                def wait_copy(e, i, j):
                    if isinstance(i, int):
                        if i + j // 4 > 0:
                            wait(e, s["k_copy"], 64 * (l * NI) + 64 * (i + j // 4))
                    else:
                        wait(e, s["k_copy"], 64 * (l * NI) + i * 64 + 64 * (j // 4))

                def exponent(i, u, h):
                    if tile_exists(i, u):
                        n = HEADS * u + h
                        need(e, "dv_s", LH, i, 4 * HEADS, n + 1)
                        need(e, "pe_t", LH, i, 4 * HEADS, n - 3)
                        need(e, "dv_p", LH, i, 4 * HEADS, n - 3)
                        m = n % 4
                        e.activation(prob[:, m, :], neg_s[:, m, :], ACT.Exp, bias=neg_m[:, n % 4:n % 4 + 1], scale=-1.0,
                                     accum_out=sm[:, n % 4:n % 4 + 1]).then_inc(s["ac_exp"], 1)

                def hi_p(i, u, h):
                    n = HEADS * u + h
                    need(e, "pe_t", LH, i, 4 * HEADS, n + 1)
                    need(e, "pe_o", LH, i, 4 * HEADS, n - 3)
                    e.activation(pT[0][:, n % 4, :], ps[:, 4 + h % 2, 0:KEYS], ACT.Copy).then_inc(s["ac_t"], 1)

                def hi_o(i, u, half):
                    need(e, "pe_o", LH, i, 4 * HEADS, HEADS * u + 4 * half + 4)
                    if half == 0:
                        need(e, "pe_w", NT, i, 4, u)
                    for odd in range(2):
                        src = ps[0:DH, 6 + half, :].rearrange("p (c o t) -> p c o t", c=2, o=2)[:, :, odd, :]
                        e.activation(oT[0][DH * odd:DH * odd + DH, 2 * half:2 * half + 2, :], src, ACT.Copy).then_inc(s["ac_o"], 1)

                hi_h(0, 0)
                squares(0, 0, 0)
                squares(0, 0, 1)
                hi_v(0, 0)
                hi_qk(0, 0)
                hi_h(0, 1)
                exponent(0, 0, 0)
                exponent(0, 0, 1)

                def body(i):
                    for u in range(4):
                        for h in range(HEADS):
                            if h == 0:
                                squares(i, u + 1, 0)
                            elif h == 1:
                                squares(i, u + 1, 1)
                            elif h == 2:
                                hi_v(i, u + 1)
                            elif h == 5:
                                hi_qk(i, u + 1)
                            elif h == 6:
                                hi_h(i, u + 2)
                            hi_p(i, u, h)
                            if h < 6:
                                exponent(i, u, h + 2)
                            else:
                                exponent(i, u + 1, h - 6)
                            if h == 1 and not (isinstance(i, int) and i == 0 and u == 0):
                                hi_o(i, u - 1, 1)
                            elif h == 6:
                                hi_o(i, u, 0)

                loop(e, body)
                hi_o(NI - 1, 3, 1)

            @block.vector
            def _(e):
                w.los(e)
                wait(e, s["ld_small"], 16 * 10 * l + 16 * 9)
                wait(e, s["pl_init"], 4 * l + 4)

                def lo(out, bank, hi, done):
                    return e.tensor_tensor(out, bank, hi.bitcast(F32), ALU.subtract).then_inc(s[done], 1)

                def lo_h(i, j):
                    if tile_exists(i, j):
                        need(e, "ac_h", NT, i, 4, j + 1)
                        lo(hT[1][:].rearrange("p c t -> p (c t)"), ps[:, 0, :], hT[0][:].rearrange("p c t -> p (c t)"), "dv_h")

                def norms(i, j, a):
                    if tile_exists(i, j):
                        need(e, "ac_sq", 2 * NT, i, 8, 2 * j + a + 1)
                        e.tensor_reduce(ssq[:, a, :], token_major_heads(sq[:, a, :]), AX.X, ALU.add).then_inc(s["dv_own"], 1)
                        need(e, "dv_own", 2 * NT, i, 8, 2 * j + a + 1)
                        e.tensor_scalar(ssq[:, a, :], ssq[:, a, :], 1e-24, None, ALU.max).then_inc(s["dv_ssq"], 1)

                def normalise(i, j, a):
                    if tile_exists(i, j):
                        need(e, "pl_rn", 2 * NT, i, 8, 2 * j + a + 1)
                        need(e, "pl_rot", 2 * NT, i, 8, 2 * j + a - 1)
                        e.tensor_tensor(token_major_heads(qk[:, a, :]), token_major_heads(ps[:, a, :]),
                                        rn[:, a, :].rearrange("p (h o) -> p h o", o=1).to_broadcast([P, HEADS, DH]),
                                        ALU.mult).then_inc(s["dv_norm"], 1)

                def lo_v(i, j):
                    if tile_exists(i, j):
                        need(e, "ac_v", NT, i, 4, j + 1)
                        lo(v[1][:, j % 4, :], ps[:, 0, :], v[0][:, j % 4, :], "dv_v")

                def lo_qk(i, j):
                    if tile_exists(i, j):
                        for a in range(2):
                            need(e, "ac_r", 2 * NT, i, 8, 2 * j + a + 1)
                            hi, out = ((qT[x][:, j % 2] if a == 0 else kT[x][:, :, 2 + j % 4, :]) for x in range(2))
                            lo(out, ps[:, 1 - a, :].rearrange("p (c t) -> p c t", c=DC), hi, "dv_r")

                def masked(i, u, h):
                    if tile_exists(i, u):
                        n = HEADS * u + h
                        if h == 0 and u % 4 == 0:
                            if isinstance(i, int):
                                wait(e, s["ld_mask"], 32 * (l * NI) + 32 * (i + u // 4 + 1), alone=True)
                            else:
                                wait(e, s["ld_mask"], 32 * (l * NI) + i * 32 + 32 * (u // 4 + 1), alone=True)
                        need(e, "pe_s", LH, i, 4 * HEADS, n + 1, alone=True)
                        need(e, "ac_exp", LH, i, 4 * HEADS, n - 3, alone=True)
                        mk = mask01[:, u % 4, :] if u % 4 < 2 else mask[:]
                        e.tensor_tensor_reduce(out=neg_s[:, n % 4, :], in0=ps[:, 2 + h % 2, 0:KEYS], in1=mk, scale=-1.0,
                                               scalar=3.0e38, op0=ALU.add, op1=ALU.min, accum_out=neg_m[:, n % 4:n % 4 + 1]
                                               ).then_inc(s["dv_s"], 1)

                def divide(i, u, h):
                    if tile_exists(i, u):
                        n = HEADS * u + h
                        need(e, "ac_exp", LH, i, 4 * HEADS, n + 1)
                        e.reciprocal(rc[:, n % 4:n % 4 + 1], sm[:, n % 4:n % 4 + 1]).then_inc(s["dv_rc"], 1)
                        need(e, "dv_rc", LH, i, 4 * HEADS, n + 1)
                        e.tensor_scalar(prob[:, n % 4, :], prob[:, n % 4, :], rc[:, n % 4:n % 4 + 1], None, ALU.mult).then_inc(s["dv_p"], 1)

                def lo_p(i, u, h):
                    n = HEADS * u + h
                    need(e, "ac_t", LH, i, 4 * HEADS, n + 1)
                    lo(pT[1][:, n % 4, :], ps[:, 4 + h % 2, 0:KEYS], pT[0][:, n % 4, :], "dv_t")

                def lo_o(i, u, half):
                    need(e, "ac_o", 4 * NT, i, 16, 4 * u + 2 * half + 2)
                    for odd in range(2):
                        src = ps[0:DH, 6 + half, :].rearrange("p (c o t) -> p c o t", c=2, o=2)[:, :, odd, :]
                        r = slice(DH * odd, DH * odd + DH)
                        ins = e.tensor_tensor(oT[1][r, 2 * half:2 * half + 2, :], src,
                                              oT[0][r, 2 * half:2 * half + 2, :].bitcast(F32), ALU.subtract)
                    ins.then_inc(s["dv_o"], 1)

                def residual(i, u):
                    if isinstance(i, int):
                        if 4 * i + u < 0:
                            return
                        base = l * NI + (i + (u // 4)) + 1
                    else:
                        base = l * NI + i + (u // 4 + 1)
                    need(e, "pe_w", NT, i, 4, u + 1)
                    wait(e, s["ld_y"][u % 4], 16 * base)
                    e.tensor_tensor(y_in[:, u % 4, :], ps[:, 1, :], y_in[:, u % 4, :], ALU.add).then_inc(s["dv_y"], 1)

                lo_h(0, 0)
                for a in range(2):
                    norms(0, 0, a)
                    normalise(0, 0, a)
                lo_v(0, 0)
                lo_qk(0, 0)
                lo_h(0, 1)
                masked(0, 0, 0)
                masked(0, 0, 1)
                divide(0, 0, 0)

                def body(i):
                    for u in range(4):
                        for h in range(HEADS):
                            if h == 0:
                                norms(i, u + 1, 0)
                            elif h == 1:
                                normalise(i, u + 1, 0)
                                norms(i, u + 1, 1)
                            elif h == 2:
                                normalise(i, u + 1, 1)
                            elif h == 4:
                                residual(i, u - 1)
                            elif h == 5:
                                lo_qk(i, u + 1)
                            if h < 6:
                                masked(i, u, h + 2)
                            else:
                                masked(i, u + 1, h - 6)
                            if h < 7:
                                divide(i, u, h + 1)
                            else:
                                divide(i, u + 1, 0)
                            lo_p(i, u, h)
                            if h == 1 and not (isinstance(i, int) and i == 0 and u == 0):
                                lo_o(i, u - 1, 1)
                            elif h == 2:
                                lo_v(i, u + 1)
                            elif h == 6:
                                lo_h(i, u + 2)
                            elif h == 7:
                                lo_o(i, u, 0)

                loop(e, body)
                lo_o(NI - 1, 3, 1)
                residual(NI - 1, 3)


def ffn_sems(sem):
    return {n: sem(f"f_{n}") for n in (
        "ld_small", "ld_in", "ld_res", "st", "dv_own", "dv_ve", "pl_rs", "dv_z", "pe_x", "ac_x", "dv_xh", "dv_x",
        "pe_a", "pe_g", "ac_g", "dv_u", "ac_u", "dv_ul", "pe_y", "pl_res", "dv_y", "pl_o")}


def ffn_phase(nc, io, ps, ident, s, wait, Split, neg_half, l, dram, zero_row):
    rows_of = [P] * (MC - 1) + [TAIL]
    cols = [[(x * HID + m * P, x * HID + m * P + rows_of[m]) for x in range(2)] for m in range(MC)]
    OWN = 1 + GT

    with ExitStack() as st:
        def sb(name, shape, dt=F32):
            return st.enter_context(nc.sbuf_tensor(name, shape, dt))

        w1 = [sb(f"w1_{x}", [P, DC, 2 * HID], F32R) for x in "hl"]
        w2 = [sb(f"w2_{x}", [P, MC, D], F32R) for x in "hl"]
        xT = [sb(f"fxT_{x}", [P, DC, G], F32R) for x in "hl"]
        u = [sb(f"u_{x}", [P, 2, G], F32R) for x in "hl"]
        x_full = sb("x_full", [P, G])
        gate = sb("gate", [P, G])
        u_full = sb("u_full", [P, 2, G])
        h_in = sb("f_in", [P, GT, D])
        res = sb("f_res", [P, GT, D])
        x1 = sb("f_x1", [P, GT, D])
        lg, lb = sb("lg", [P, DC]), sb("lb", [P, DC])
        b1 = sb("b1_cols", [P, MC, 2])
        b2 = sb("b2_rows", [P, D])
        stats, mv = sb("f_stats", [P, GT, 6]), sb("f_mv", [P, GT, 2])
        ve, rs = sb("f_ve", [P, GT]), sb("f_rs", [P, GT])

        src1 = io["w1"].rearrange("l k n -> (l k) n")
        src2 = io["w2"].rearrange("l k n -> (l k) n")
        pieces = []
        for c0 in range(0, HID, 2 * P):
            m, n = c0 // P, min(2 * P, HID - c0)
            for x in range(2):
                c = slice(x * HID + c0, x * HID + c0 + n)
                pieces.append((src1[bass.ds(l * D, D), c].rearrange("(k p) c -> p k c", p=P), w1[0][:, :, c], w1[1][:, :, c]))
            if n == 2 * P:
                pieces.append((src2[bass.ds(l * HID + c0, n), :].rearrange("(m p) d -> p m d", p=P),
                               w2[0][:, m:m + 2, :], w2[1][:, m:m + 2, :]))
            else:
                pieces.append((src2[bass.ds(l * HID + c0, n), :], w2[0][0:n, m, :], w2[1][0:n, m, :]))
        PAIR = 3
        w = Split("w_ffn", st, DC * 2 * P, pieces, l)

        def is_first(g):
            return isinstance(g, int) and g == 0

        def is_last(g):
            return isinstance(g, int) and g == NG - 1

        def need(e, name, per, g, k, alone=False):
            if isinstance(g, int) and g * per + k <= 0:
                return
            value = l * (NG * per) + g * per + k if not isinstance(g, int) else l * (NG * per) + (g * per + k)
            wait(e, s[name], value, alone)

        def loop(e, body):
            body(0)
            with e.Fori(1, NG - 1) as g:
                body(g)
            body(NG - 1)

        SMALL = 6

        with nc.Block() as block:
            @block.sync
            def _(e):
                for name, t in (("ln_g", lg), ("ln_b", lb)):
                    e.dma_start(t[:], io[name][bass.ds(l * P, P), :]).then_inc(s["ld_small"], 16)
                e.dma_start(b1[:, 0:MC - 1, :], io["b1_main"][bass.ds(l * P, P), :].rearrange("p (m x) -> p m x", x=2)).then_inc(s["ld_small"], 16)
                e.dma_start(b1[0:TAIL, MC - 1, :], io["b1_tail"][bass.ds(l * TAIL, TAIL), :]).then_inc(s["ld_small"], 16)
                e.dma_start(b2[:], io["b2"][bass.ds(l, 1), :].to_broadcast([P, D])).then_inc(s["ld_small"], 16)

                def rows(ap, g, late=0):
                    r = g * G + late
                    r = r if isinstance(r, int) else e.snap(r)
                    return ap[bass.ds(r, G), :].rearrange("(t p) d -> p t d", p=P)

                def load_in(g, behind):
                    a, b = rows(dram["src"], g)[:, :, 0:HALF], rows(dram["src_late"], g)
                    need(e, "pe_x", DC, behind, DC) if behind is not None else None
                    e.dma_start(h_in[:, :, 0:HALF], a).then_inc(s["ld_in"], 16)
                    e.dma_start(h_in[:, :, HALF:D], b).then_inc(s["ld_in"], 16)

                def body(g):
                    a, b = rows(dram["src"], g), rows(dram["x1"], g)
                    if not is_first(g):
                        wait(e, s["st"], l * (48 * NG) + g * 48)
                    e.dma_start(res[:], a).then_inc(s["ld_res"], 16)
                    e.dma_start(x1[:], b).then_inc(s["ld_res"], 16)
                    if not is_last(g):
                        load_in(g + 1, g)
                    if is_first(g):
                        w.loads(e, 4 * PAIR)
                    d = [rows(dram["dst"], g), rows(dram["dst_late"], g, 1), rows(io["out"], g)]
                    need(e, "dv_y", GT, g, GT)
                    e.dma_start(d[0], res[:]).then_inc(s["st"], 16)
                    e.dma_start(d[1], res[:, :, HALF:D]).then_inc(s["st"], 16)
                    need(e, "pl_o", GT, g, GT)
                    e.dma_start(d[2], x1[:]).then_inc(s["st"], 16)

                load_in(0, None)
                w.loads(e, 0, 4 * PAIR)
                loop(e, body)
                wait(e, s["st"], l * (48 * NG) + 48 * NG)
                e.dma_start(dram["dst_late"][N:N + 1, :], zero_row[:]).then_inc(s["ld_small"], 16)
                wait(e, s["ld_small"], 16 * SMALL * l + 16 * SMALL)

            @block.gpsimd
            def _(e):
                def root(g):
                    need(e, "dv_ve", 1, g, 1)
                    e.tensor_tensor(rs[:], ve[:], neg_half[:, 0:GT], ALU.pow).then_inc(s["pl_rs"], 1)

                def body(g):
                    wait(e, s["ld_res"], l * (32 * NG) + g * 32 + 32)
                    for tt in range(GT):
                        e.tensor_tensor(res[:, tt, :], res[:, tt, :], b2[:], ALU.add).then_inc(s["pl_res"], 1)
                    if not is_last(g):
                        root(g + 1)
                    for tt in range(GT):
                        need(e, "dv_y", GT, g, tt + 1)
                        e.tensor_tensor(x1[:, tt, :], x1[:, tt, :], res[:, tt, :], ALU.add).then_inc(s["pl_o"], 1)

                wait(e, s["ld_small"], 16 * SMALL * l + 16 * (SMALL - 1))
                root(0)
                loop(e, body)

            @block.tensor
            def _(e):
                def transpose_x(g, k, behind):
                    need(e, "dv_z", GT, g, GT)
                    if k >= 2:
                        need(e, "dv_x", DC, g, k - 1)
                    elif behind is not None:
                        need(e, "dv_u", MC, behind, MC - 1)
                    for tt in range(GT):
                        last = e.transpose(ps[:, 2 + k % 2, tt * P:(tt + 1) * P], h_in[:, tt, k * P:(k + 1) * P], ident[:])
                    last.then_inc(s["pe_x"], 1)

                def hidden(g, m):
                    if m == 0:
                        need(e, "dv_x", DC, g, DC)
                    if is_first(g) and m % 2 == 0:
                        w.done(e, PAIR * (m // 2) + 2)
                    need(e, "dv_u", MC, g, m - 1 if m >= 2 else 0)
                    for x in range(2):
                        c = slice(*cols[m][x])
                        for k in range(DC):
                            last = split_matmul(e, ps[0:rows_of[m], 2 * (m % 2) + x, :], [y[:, k, c] for y in w1],
                                                [y[:, k, :] for y in xT], k == 0, k == DC - 1)
                        last.then_inc(s["pe_g" if x else "pe_a"], 1)

                def output(g, m, tts=range(GT)):
                    if is_first(g) and m % 2 == 0:
                        w.done(e, PAIR * (m // 2 + 1))
                    need(e, "dv_ul", MC, g, m + 1)
                    if m == 0:
                        need(e, "dv_y", GT, g, 0)
                    for tt in tts:
                        r = slice(0, rows_of[m])
                        last = split_matmul(e, ps[:, 4 + tt, :], [y[r, m % 2, tt * P:(tt + 1) * P] for y in u],
                                            [y[r, m, :] for y in w2], m == 0, m == MC - 1)
                        if m == MC - 1 or tt == GT - 1:
                            last.then_inc(s["pe_y"], 1)

                def body(g):
                    for m in range(MC):
                        hidden(g, m)
                        if m:
                            output(g, m - 1)
                    more = not is_last(g)
                    if more:
                        transpose_x(g + 1, 0, g)
                        transpose_x(g + 1, 1, g)
                    output(g, MC - 1, range(2))
                    if more:
                        transpose_x(g + 1, 2, g)
                        transpose_x(g + 1, 3, g)
                    output(g, MC - 1, range(2, GT))

                for k in range(DC):
                    transpose_x(0, k, None)
                loop(e, body)

            @block.scalar
            def _(e):
                wait(e, s["ld_small"], 16 * SMALL * l + 16 * (SMALL - 1))

                def affine(g, k):
                    need(e, "pe_x", DC, g, k + 1)
                    need(e, "dv_x", DC, g, k)
                    e.activation(x_full[:], ps[:, 2 + k % 2, :], ACT.Identity, bias=lb[:, k:k + 1], scale=lg[:, k:k + 1]).then_inc(s["ac_x"], 1)

                def body(g):
                    for m in range(MC):
                        r = slice(0, rows_of[m])
                        need(e, "pe_g", MC, g, m + 1)
                        need(e, "dv_u", MC, g, m)
                        e.activation(gate[r, :], ps[r, 2 * (m % 2) + 1, :], ACT.Gelu, bias=b1[r, m, 1:2]).then_inc(s["ac_g"], 1)
                        need(e, "dv_u", MC, g, m + 1)
                        need(e, "pe_y", MC - 1 + GT, g, m - 1 if m >= 2 else 0)
                        e.activation(u[0][r, m % 2, :], u_full[r, m % 2, :], ACT.Copy).then_inc(s["ac_u"], 1)
                        if is_first(g) and m % 2 == 0 and m < MC - 1:
                            w.his(e, PAIR * (m // 2 + 1), PAIR * (m // 2 + 2))
                    if not is_last(g):
                        for k in range(DC):
                            affine(g + 1, k)

                for k in range(DC):
                    affine(0, k)
                w.his(e, 0, PAIR)
                loop(e, body)

            @block.vector
            def _(e):
                wait(e, s["ld_small"], 16 * SMALL * l + 16 * (SMALL - 1))

                def normalise(g):
                    wait(e, s["ld_in"], l * (32 * NG) + g * 32 + 32)
                    for tt in range(GT):
                        ins = e.bn_stats(stats[:, tt, :], h_in[:, tt, :])
                    ins.then_inc(s["dv_own"], 1)
                    need(e, "dv_own", OWN, g, 1, alone=True)
                    for tt in range(GT):
                        e.bn_aggr(mv[:, tt, :], stats[:, tt, :]).then_inc(s["dv_own"], 1)
                    need(e, "dv_own", OWN, g, OWN, alone=True)
                    e.tensor_scalar(ve[:].rearrange("p (t o) -> p t o", o=1), mv[:, :, 1:2], EPS, None, ALU.add).then_inc(s["dv_ve"], 1)
                    need(e, "pl_rs", 1, g, 1)
                    for tt in range(GT):
                        e.tensor_scalar(h_in[:, tt, :], h_in[:, tt, :], mv[:, tt, 0:1], rs[:, tt:tt + 1],
                                        ALU.subtract, ALU.mult).then_inc(s["dv_z"], 1)

                def split_x(g, k):
                    need(e, "ac_x", DC, g, k + 1)
                    e.tensor_copy(xT[0][:, k, :], x_full[:]).then_inc(s["dv_xh"], 1)
                    need(e, "dv_xh", DC, g, k + 1)
                    e.tensor_tensor(xT[1][:, k, :], x_full[:], xT[0][:, k, :].bitcast(F32), ALU.subtract).then_inc(s["dv_x"], 1)

                def body(g):
                    for m in range(MC):
                        r = slice(0, rows_of[m])
                        need(e, "pe_a", MC, g, m + 1)
                        need(e, "ac_g", MC, g, m + 1)
                        need(e, "dv_ul", MC, g, max(m - 1, 0))
                        e.scalar_tensor_tensor(out=u_full[r, m % 2, :], in0=ps[r, 2 * (m % 2), :], scalar=b1[r, m, 0:1],
                                               in1=gate[r, :], op0=ALU.add, op1=ALU.mult).then_inc(s["dv_u"], 1)
                        need(e, "ac_u", MC, g, m + 1)
                        e.tensor_tensor(u[1][r, m % 2, :], u_full[r, m % 2, :], u[0][r, m % 2, :].bitcast(F32), ALU.subtract).then_inc(s["dv_ul"], 1)
                        if is_first(g) and m % 2 == 0 and m < MC - 1:
                            w.los(e, PAIR * (m // 2 + 1), PAIR * (m // 2 + 2))
                        if m == 5 and not is_last(g):
                            normalise(g + 1)
                    if not is_last(g):
                        for k in range(2):
                            split_x(g + 1, k)
                    need(e, "pl_res", GT, g, GT)
                    for tt in range(GT):
                        need(e, "pe_y", MC - 1 + GT, g, MC + tt)
                        e.tensor_tensor(res[:, tt, :], ps[:, 4 + tt, :], res[:, tt, :], ALU.add).then_inc(s["dv_y"], 1)
                        if tt == 1 and not is_last(g):
                            for k in range(2, DC):
                                split_x(g + 1, k)

                normalise(0)
                for k in range(DC):
                    split_x(0, k)
                w.los(e, 0, PAIR)
                loop(e, body)


def rotary_tables():
    half_idx = np.arange(0, DH, 2, dtype=np.float32)
    inv_freq = (np.float32(1.0) / np.float32(10000.0) ** (half_idx / np.float32(DH))).astype(np.float32)
    t = np.arange(N, dtype=np.float32)
    freqs = t[:, None] * inv_freq[None, :]
    freqs = np.concatenate([freqs, freqs], -1)
    base = (half_idx + np.float32(0.4 * DH)) / np.float32(1.4 * DH)
    power = (t - np.float32(N // 2)) / np.float32(WIN // 2)
    scale = base[None, :] ** power[:, None]
    scale = np.concatenate([scale, scale], -1)
    cos, sin = np.cos(freqs), np.sin(freqs)
    sin[:, :DH // 2] = -sin[:, :DH // 2]
    tab = np.concatenate([cos * scale * 8, sin * scale * 8, cos / scale, sin / scale], -1).astype(np.float32)
    return np.concatenate([tab] * B, 0)


def window_masks():
    q, k = np.arange(P)[:, None], np.arange(KEYS)[None, :] - 2 * P
    mask = np.where((k <= q) & (q <= k + WIN), np.float32(0), np.float32(MASKED)).astype(np.float32)
    first = np.repeat(mask[None, None, :, 0:2 * P], NI, 0).repeat(2, 1)
    for i in range(0, NI, NI // B):
        first[i, 0] = MASKED
        first[i, 1, :, 0:P] = MASKED
    return mask, np.ascontiguousarray(first.reshape(NI * 2 * P, 2 * P))


def kernel(**inputs):
    import concourse.bacc as bacc
    from concourse.bass_utils import run_bass_kernel_spmd

    a = {k: np.asarray(v) for k, v in inputs.items()}
    x_, f_ = "L0_xattn_", "L0_ffn_"
    mask, mask01 = window_masks()
    b1 = a[f_ + "b1"].reshape(DEPTH, 2, HID)
    main = (MC - 1) * P
    arrays = {
        "x": a["x"].reshape(T, D), "ctx": a["ctx_1024"].reshape(B * SC, D),
        "WqT": a[x_ + "Wq"].T, "WkT": a[x_ + "Wk"].T, "WvT": a[x_ + "Wv"].T, "WoT": a[x_ + "Wo"].T,
        "bq": a[x_ + "bq"].reshape(DC, P).T, "bk": a[x_ + "bk"].reshape(DC, P).T,
        "bv": a[x_ + "bv"].reshape(1, D), "bo": a[x_ + "bo"].reshape(1, D),
        "wqkv": a[f_ + "wqkv"], "q_scale": a[f_ + "q_scale"], "k_scale": a[f_ + "k_scale"], "wo": a[f_ + "wo"],
        "ln_g": a[f_ + "ln_g"].reshape(DEPTH, DC, P).transpose(0, 2, 1).reshape(DEPTH * P, DC),
        "ln_b": a[f_ + "ln_b"].reshape(DEPTH, DC, P).transpose(0, 2, 1).reshape(DEPTH * P, DC),
        "w1": a[f_ + "w1"], "w2": a[f_ + "w2"],
        "b1_main": b1[:, :, :main].reshape(DEPTH, 2, MC - 1, P).transpose(0, 3, 2, 1).reshape(DEPTH * P, 2 * (MC - 1)),
        "b1_tail": b1[:, :, main:].transpose(0, 2, 1).reshape(DEPTH * TAIL, 2),
        "b2": a[f_ + "b2"], "rot": rotary_tables(), "mask": mask, "mask01": mask01,
    }
    arrays = {k: np.ascontiguousarray(v) for k, v in arrays.items()}
    nc = bacc.Bacc("TRN2", target_bir_lowering=False, num_devices=1)
    io = {k: nc.dram_tensor(f"in_{k}", v.shape, mybir.dt.from_np(v.dtype), kind="ExternalInput").ap()
          for k, v in arrays.items()}
    io["out"] = nc.dram_tensor("out_rows", (T, D), F32, kind="ExternalOutput").ap()
    build(nc, io)
    r = run_bass_kernel_spmd(nc, [{f"in_{k}": v for k, v in arrays.items()}], core_ids=[0])
    return r.results[0]["out_rows"].reshape(B, N, D)
```

```python
from contextlib import ExitStack

import numpy as np

import concourse.bass as bass
from concourse import mybir

F32 = mybir.dt.float32
F32R = mybir.dt.float32r
ACT = mybir.ActivationFunctionType
ALU = mybir.AluOpType
AX = mybir.AxisListType

P = 128
B, N, D = 2, 2048, 512
T = B * N
DC = D // P
HALF = D // 2
SC, XH = 154, 16
XD = D // XH
SCH = SC // 2
QUAD = P // XD
QW = QUAD * SC
QK = -(-QW // P)
DEPTH, HEADS, DH, WIN = 2, 8, 64, 256
HID = int(D * 4 * 2 / 3)
MC = -(-HID // P)
TAIL = HID - (MC - 1) * P
GT = 4
G = GT * P
NT = T // P
NG = T // G
NI = NT // 4
KEYS = 3 * P
EPS = 1e-5
MASKED = -3.0e38
XSLOTS = 3
SLOTS = {"w_ctx": 4, "w_attn": 8, "w_ffn": 4}


FROM_ONE = ("x_ac_exp", "x_dv_x1", "x_pe_o", "x_st_x1",
            "x_st_y", "f_dv_u", "f_dv_ul", "f_dv_y", "f_pe_y", "f_st")


def split_matmul(pe, out, a, b, start, stop):
    (a_h, a_l), (b_h, b_l) = a, b
    pe.matmul(out, a_h, b_h, start=start, stop=False)
    pe.matmul(out, a_h, b_l, start=False, stop=False)
    return pe.matmul(out, a_l, b_h, start=False, stop=stop)


def build(nc, io):
    ctx = ExitStack()

    from_one = {name: nc.alloc_semaphore(name) for name in FROM_ONE}

    def sem(name):
        return from_one[name] if name in from_one else nc.alloc_semaphore(name)

    passed = sem("passed")

    def wait(e, s, value, alone=False):
        if isinstance(value, int) and value <= 0:
            return
        if any(s is one for one in from_one.values()):
            value = value + 1
        assert isinstance(value, int) or value.min_val > 0, s
        e.wait_ge(s, value)
        if (alone or e is nc.sync) and not isinstance(value, int):
            e.sem_inc(passed, 1)

    def scratch(name, shape, dt=F32):
        return nc.dram_tensor(name, shape, dt, kind="Internal").ap()

    x1_rows = scratch("x1_rows", (T, D))
    y_rows = scratch("y_rows", (T, D))
    y_late = scratch("y_late", (T + 1, HALF))
    z_rows = scratch("z_rows", (T, D))
    z_late = scratch("z_late", (T + 1, HALF))
    ctx_k = scratch("ctx_k", (B * 2 * P, DC * SC))
    ctx_v = scratch("ctx_v", (B * 2 * SC, D))

    ps = ctx.enter_context(nc.psum_tensor("banks", [P, 8, 512], F32))
    ident = ctx.enter_context(nc.sbuf_tensor("ident", [P, P], F32))
    neg_half = ctx.enter_context(nc.sbuf_tensor("neg_half", [P, 2 * HEADS], F32))
    zero_row = ctx.enter_context(nc.sbuf_tensor("zero_row", [1, HALF], F32))
    consts_done = sem("consts_done")

    class Split:

        def __init__(self, name, stack, width, pieces, l=0):
            self.l, self.pieces = l, pieces
            *self.loaded, self.hi_done, self.lo_done = split_sems[name]
            self.slots = len(self.loaded)
            self.stage = stack.enter_context(nc.sbuf_tensor(f"{name}_stage", [P, self.slots, width], F32))

        def slot(self, n):
            shape = self.pieces[n][0].shape
            at = self.stage[0:shape[0], n % self.slots, 0:int(np.prod(shape[1:]))]
            return at if len(shape) == 2 else at.rearrange("p (a b) -> p a b", a=shape[1])

        def each(self, n0, n1):
            return range(n0, len(self.pieces) if n1 is None else n1)

        def loads(self, e, n0=0, n1=None):
            for n in self.each(n0, n1):
                wait(e, self.lo_done, self.l * len(self.pieces) + n - self.slots + 1 if n >= self.slots else 0)
                e.dma_start(self.slot(n), self.pieces[n][0]).then_inc(self.loaded[n % self.slots], 16)

        def his(self, e, n0=0, n1=None):
            for n in self.each(n0, n1):
                total = len(range(n % self.slots, len(self.pieces), self.slots))
                wait(e, self.loaded[n % self.slots], 16 * (self.l * total + n // self.slots + 1))
                e.activation(self.pieces[n][1], self.slot(n), ACT.Copy).then_inc(self.hi_done, 1)

        def los(self, e, n0=0, n1=None):
            for n in self.each(n0, n1):
                wait(e, self.hi_done, self.l * len(self.pieces) + n + 1)
                e.tensor_tensor(self.pieces[n][2], self.slot(n), self.pieces[n][1].bitcast(F32),
                                ALU.subtract).then_inc(self.lo_done, 1)

        def done(self, e, n=None):
            n = len(self.pieces) if n is None else n
            wait(e, self.lo_done, self.l * len(self.pieces) + n, alone=True)

    split_sems = {name: [sem(f"{name}_{x}") for x in (*range(slots), "hi", "lo")]
                  for name, slots in SLOTS.items()}

    with nc.Block() as block:
        @block.gpsimd
        def _(e):
            for one in from_one.values():
                e.sem_inc(one, 1)

    with ExitStack() as shared:
        def sb(name, shape):
            return [shared.enter_context(nc.sbuf_tensor(f"{name}_{x}", shape, F32R)) for x in "hl"]

        keep = dict(wq=sb("wq", [P, DC, D]), wo=sb("xwo", [P, DC, D]),
                    k_bd=sb("k_bd", [P, DC, 2, SC]),
                    v_bd=sb("v_bd", [P, DC, QK, P]),
                    x_in=shared.enter_context(nc.sbuf_tensor("x_in", [P, XSLOTS, GT, D], F32)),
                    ld_x=[sem(f"x_ld{s}") for s in range(XSLOTS)])
        context_phase(nc, io, ps, ident, sem, wait, Split, dict(ctx_k=ctx_k, ctx_v=ctx_v),
                      neg_half, zero_row, consts_done, (y_late, z_late), keep)
        cross_phase(nc, io, ps, ident, sem, wait, neg_half,
                    dict(ctx_k=ctx_k, ctx_v=ctx_v, x1=x1_rows, y=y_rows, late=y_late), zero_row, keep)
    attn_sems = attention_sems(sem)
    ffn_s = ffn_sems(sem)
    with nc.Fori(0, DEPTH) as l:
        attention_phase(nc, io, ps, ident, attn_sems, wait, Split, neg_half, l,
                        dict(src=y_rows, src_late=y_late, dst=z_rows, dst_late=z_late), zero_row)
        ffn_phase(nc, io, ps, ident, ffn_s, wait, Split, neg_half, l,
                  dict(src=z_rows, src_late=z_late, dst=y_rows, dst_late=y_late, x1=x1_rows),
                  zero_row)
    ctx.close()


def context_phase(nc, io, ps, ident, sem, wait, Split, dram, neg_half, zero_row, consts_done,
                  lates, keep):
    ld_small, ld_ctx, out_done, zero_done = sem("c_small"), sem("c_ctx"), sem("c_out"), sem("c_zero")
    ident_zeroed = sem("ident_zeroed")
    pe_t, ac_t, dv_t = sem("c_pe_t"), sem("c_ac_t"), sem("c_dv_t")
    pe_k, ac_k, ac_kh, dv_k = sem("c_pe_k"), sem("c_ac_k"), sem("c_ac_kh"), sem("c_dv_k")
    pe_v, dv_vf, ac_v, dv_v = sem("c_pe_v"), sem("c_dv_vf"), sem("c_ac_v"), sem("c_dv_v")
    TT = 2 * B
    BSC = B * SC
    with ExitStack() as st:
        def sb(name, shape, dt=F32):
            return st.enter_context(nc.sbuf_tensor(name, shape, dt))

        wk = [sb(f"wk_{x}", [P, DC, D], F32R) for x in "hl"]
        wv = [sb(f"wv_{x}", [P, DC, D], F32R) for x in "hl"]
        bk = sb("bk_cols", [P, DC])
        bv = sb("bv_rows", [SCH, D])
        c_in = sb("c_in", [SCH, TT, D])
        cT = [sb(f"cT_{x}", [P, DC, BSC], F32R) for x in "hl"]
        k_full = sb("k_full", [P, DC, BSC])
        kT = [sb(f"ctx_kT_{x}", [P, DC, BSC], F32R) for x in "hl"]
        v_full = sb("v_full", [SCH, TT, D])
        v = [sb(f"ctx_v_{x}", [SCH, TT, D], F32R) for x in "hl"]
        w = Split("w_ctx", st, D, [(io[name][k * P:(k + 1) * P, :], t[0][:, k, :], t[1][:, k, :])
                                   for name, t in (("WkT", wk), ("WvT", wv), ("WqT", keep["wq"]), ("WoT", keep["wo"]))
                                   for k in range(DC)])
        KEYS_W, VALUES_W, QUERIES_W = DC, 2 * DC, 3 * DC

        with nc.Block() as block:
            @block.sync
            def _(e):
                e.dma_start(c_in[:], io["ctx"].rearrange("(t p) d -> p t d", p=SCH)).then_inc(ld_ctx, 16)
                w.loads(e, 0, w.slots)
                e.dma_start(bk[:], io["bk"]).then_inc(ld_small, 16)
                e.dma_start(bv[:], io["bv"].to_broadcast([SCH, D])).then_inc(ld_small, 16)
                w.loads(e, w.slots, VALUES_W + w.slots)
                wait(e, consts_done, 3)
                for late in lates:
                    for b in range(B):
                        e.dma_start(late[b * N:b * N + 1, :], zero_row[:]).then_inc(zero_done, 16)
                for s in range(XSLOTS):
                    e.dma_start(keep["x_in"][:, s], io["x"][s * G:(s + 1) * G, :].rearrange("(t p) d -> p t d", p=P)
                                ).then_inc(keep["ld_x"][s], 16)
                wait(e, dv_k, 1)
                for b in range(B):
                    for part in range(2):
                        e.dma_start(dram["ctx_k"][(b * 2 + part) * P:(b * 2 + part + 1) * P, :].rearrange("r (c s) -> r c s", c=DC),
                                    kT[part][:, :, b * SC:(b + 1) * SC].bitcast(F32)).then_inc(out_done, 16)
                w.loads(e, VALUES_W + w.slots)
                wait(e, dv_v, TT)
                for b in range(B):
                    for part in range(2):
                        e.dma_start(dram["ctx_v"][(b * 2 + part) * SC:(b * 2 + part + 1) * SC, :].rearrange("(h p) d -> p h d", p=SCH),
                                    v[part][:, 2 * b:2 * b + 2, :].bitcast(F32)).then_inc(out_done, 16)
                wait(e, out_done, 16 * 4 * B)
                wait(e, zero_done, 16 * 2 * B)

            @block.gpsimd
            def _(e):
                e.memset(neg_half[:], -0.5).then_inc(consts_done, 1)
                e.memset(zero_row[:], 0.0).then_inc(consts_done, 1)
                e.memset(ident[:], 0.0).then_inc(ident_zeroed, 1)
                wait(e, ident_zeroed, 1)
                e.affine_select(out=ident[:], in_=ident[:], compare_op=ALU.not_equal, fill=1.0, base=0,
                                pattern=[[-1, P]], channel_multiplier=1).then_inc(consts_done, 1)
                for t in keep["k_bd"] + keep["v_bd"]:
                    e.memset(t[:].bitcast(F32), 0.0)

            @block.tensor
            def _(e):
                wait(e, consts_done, 3)
                wait(e, ld_ctx, 16)
                for c in range(DC):
                    for t in range(TT):
                        last = e.transpose(ps[:, c, t * SCH:(t + 1) * SCH], c_in[:, t, c * P:(c + 1) * P], ident[0:SCH, 0:SCH])
                    last.then_inc(pe_t, 1)
                wait(e, dv_t, DC)
                w.done(e, KEYS_W)
                for c in range(DC):
                    for k in range(DC):
                        last = split_matmul(e, ps[:, 4 + c, 0:BSC], [x[:, k, c * P:(c + 1) * P] for x in wk],
                                            [x[:, k, :] for x in cT], k == 0, k == DC - 1)
                    last.then_inc(pe_k, 1)
                w.done(e, VALUES_W)
                for t in range(TT):
                    for k in range(DC):
                        last = split_matmul(e, ps[0:SCH, t, :], [x[:, k, t * SCH:(t + 1) * SCH] for x in cT],
                                            [x[:, k, :] for x in wv], k == 0, k == DC - 1)
                    last.then_inc(pe_v, 1)

            @block.scalar
            def _(e):
                for c in range(DC):
                    wait(e, pe_t, c + 1)
                    e.activation(cT[0][:, c, :], ps[:, c, 0:BSC], ACT.Copy).then_inc(ac_t, 1)
                w.his(e, 0, VALUES_W)
                wait(e, ld_small, 32)
                for c in range(DC):
                    wait(e, pe_k, c + 1)
                    e.activation(k_full[:, c, :], ps[:, 4 + c, 0:BSC], ACT.Identity, bias=bk[:, c:c + 1]).then_inc(ac_k, 1)
                wait(e, ac_k, DC)
                e.activation(kT[0][:], k_full[:], ACT.Copy).then_inc(ac_kh, 1)
                w.his(e, VALUES_W, QUERIES_W)
                for t in range(TT):
                    wait(e, dv_vf, t + 1)
                    e.activation(v[0][:, t, :], v_full[:, t, :], ACT.Copy).then_inc(ac_v, 1)
                w.his(e, QUERIES_W)

            @block.vector
            def _(e):
                for c in range(DC):
                    wait(e, ac_t, c + 1)
                    e.tensor_tensor(cT[1][:, c, :], ps[:, c, 0:BSC], cT[0][:, c, :].bitcast(F32), ALU.subtract).then_inc(dv_t, 1)
                w.los(e, 0, VALUES_W)
                wait(e, ld_small, 32)
                wait(e, ac_kh, 1)
                e.tensor_tensor(kT[1][:], k_full[:], kT[0][:].bitcast(F32), ALU.subtract).then_inc(dv_k, 1)
                w.los(e, VALUES_W, QUERIES_W)
                for t in range(TT):
                    wait(e, pe_v, t + 1)
                    e.tensor_tensor(v_full[:, t, :], ps[0:SCH, t, :], bv[:], ALU.add).then_inc(dv_vf, 1)
                    wait(e, ac_v, t + 1)
                    e.tensor_tensor(v[1][:, t, :], v_full[:, t, :], v[0][:, t, :].bitcast(F32), ALU.subtract).then_inc(dv_v, 1)
                w.los(e, QUERIES_W)


def cross_phase(nc, io, ps, ident, sem, wait, neg_half, dram, zero_row, keep):
    ld_small = sem("x_small")
    ld_k, ld_v = ([sem(f"x_ld_{x}{half}") for half in range(2)] for x in "kv")
    st_x1, st_y = sem("x_st_x1"), sem("x_st_y")
    dv_own, dv_ve, pl_rs, dv_xn, pl_xb = sem("x_dv_own"), sem("x_dv_ve"), sem("x_pl_rs"), sem("x_dv_xn"), sem("x_pl_xb")
    pe_x, ac_x, dv_x = sem("x_pe_x"), sem("x_ac_x"), sem("x_dv_x")
    pe_q, ac_q, dv_q = sem("x_pe_q"), sem("x_ac_q"), sem("x_dv_q")
    pe_s, dv_max, ac_exp, dv_rc, pl_p = sem("x_pe_s"), sem("x_dv_max"), sem("x_ac_exp"), sem("x_dv_rc"), sem("x_pl_p")
    pe_t, ac_t, dv_t = sem("x_pe_t"), sem("x_ac_t"), sem("x_dv_t")
    pe_o, ac_o, dv_o = sem("x_pe_o"), sem("x_ac_o"), sem("x_dv_o")
    pe_w, dv_x1, dv_y = sem("x_pe_w"), sem("x_dv_x1"), sem("x_dv_y")
    dv_vy, pl_ry = sem("x_dv_vy"), sem("x_pl_ry")
    NS = DC * GT
    NM = DC * QK
    SCALE = float(XD) ** -0.5
    V_BANK, TURNS = 6, 7
    rows_of = [min(P, QW - k * P) for k in range(QK)]
    segments = [(r, k, max(SC * r, P * k), min(SC * (r + 1), P * (k + 1)))
                for r in range(QUAD) for k in range(QK) if max(SC * r, P * k) < min(SC * (r + 1), P * (k + 1))]
    K_HALVES, V_HALVES = ((0, 2), (2, DC)), ((0, DC - 1), (DC - 1, DC))
    K_LOADED, V_LOADED = 16 * 2 * QUAD, 16 * 2 * len(segments)
    LEAD = 1 + GT
    OWN_BEFORE, OWN_FIRST, OWN = 2 * LEAD + GT, LEAD + NS, LEAD + NS + 2 * GT
    wq, wo, k_bd, v_bd, x_in, ld_x = (keep[name] for name in ("wq", "wo", "k_bd", "v_bd", "x_in", "ld_x"))

    with ExitStack() as st:
        def sb(name, shape, dt=F32):
            return st.enter_context(nc.sbuf_tensor(name, shape, dt))

        bq = sb("bq_cols", [P, DC])
        bo = sb("bo_rows", [P, D])
        xn = sb("xn", [P, GT, D])
        stats, stats_y = sb("x_stats", [P, GT, 6]), sb("y_stats", [P, GT, 6])
        mv, mv_y = sb("x_mv", [P, GT, 2]), sb("y_mv", [P, GT, 2])
        ve, ve_y = sb("x_ve", [P, GT]), sb("y_ve", [P, GT])
        rs, rs_y = sb("x_rs", [P, GT]), sb("y_rs", [P, GT])
        xT = [sb(f"xT_{x}", [P, DC, G], F32R) for x in "hl"]
        qT = [sb(f"xqT_{x}", [P, DC, G], F32R) for x in "hl"]
        mx = sb("x_mx", [P, NS, QUAD])
        nmx = sb("x_nmx", [P, NS, QUAD])
        sm = sb("x_sm", [P, NS, QUAD])
        rc = sb("x_rc", [P, NS, QUAD])
        prob = sb("x_prob", [P, 2, GT, QW])
        pT = [sb(f"xpT_{x}", [P, QK, G], F32R) for x in "hl"]
        oT = [sb(f"xoT_{x}", [P, DC, G], F32R) for x in "hl"]
        y = sb("y0_t", [P, GT, D])
        k_dram = dram["ctx_k"].rearrange("r (c s) -> r c s", c=DC)

        class Group:

            def __init__(self, it, before, turn):
                self.it, self.before, self.turn = it, before, turn
                self.known = isinstance(it, int)
                self.first, self.last = self.known and it == 0, self.known and it == NG - 1

            def slot(self, off):
                return (self.before + off) % XSLOTS

            def round(self, off):
                return self.turn + (self.before + off) // XSLOTS

            def row(self, e, off, late=0):
                r = (self.it + off) * G + late
                return r if self.known else e.snap(r)

        def run(e, body):
            body(Group(0, 0, 0), None)
            with e.Fori(0, (NG - 2) // XSLOTS) as turn:
                for s in range(XSLOTS):
                    body(Group(e.snap(turn * XSLOTS + (1 + s)), 1 + s, turn), s)
            body(Group(NG - 1, NG - 1, 0), None)

        with nc.Block() as block:
            @block.sync
            def _(e):
                def rows(ap, r):
                    return ap[bass.ds(r, G), :].rearrange("(t p) d -> p t d", p=P)

                e.dma_start(bq[:], io["bq"]).then_inc(ld_small, 16)
                e.dma_start(bo[:], io["bo"].to_broadcast([P, D])).then_inc(ld_small, 16)

                def load_keys(b, half):
                    c = slice(*K_HALVES[half])
                    for part in range(2):
                        src = k_dram[(b * 2 + part) * P:(b * 2 + part + 1) * P]
                        for r in range(QUAD):
                            e.dma_start(k_bd[part][r * XD:(r + 1) * XD, c, r % 2, :].bitcast(F32),
                                        src[r * XD:(r + 1) * XD, c]).then_inc(ld_k[half], 16)

                def load_values(b, half):
                    c = slice(*V_HALVES[half])
                    for part in range(2):
                        src = dram["ctx_v"][(b * 2 + part) * SC:(b * 2 + part + 1) * SC, :].rearrange("s (c n) -> s c n", c=DC)
                        for r, k, f0, f1 in segments:
                            e.dma_start(v_bd[part][f0 - k * P:f1 - k * P, c, k, r * XD:(r + 1) * XD].bitcast(F32),
                                        src[f0 - r * SC:f1 - r * SC, c, r * XD:(r + 1) * XD]).then_inc(ld_v[half], 16)

                def store_before(g, it):
                    r, r_late = g.row(e, -1), g.row(e, -1, 1)
                    if it is g.it and not g.last:
                        src = rows(io["x"], e.snap(e.snap((it + 2) % NG) * G))
                    wait(e, dv_x1, GT * it)
                    e.dma_start(rows(dram["x1"], r), x_in[:, g.slot(-1)]).then_inc(st_x1, 16)
                    wait(e, dv_y, GT * it)
                    if it is g.it and not g.last:
                        wait(e, st_x1, 16 * it)
                        e.dma_start(x_in[:, g.slot(2)], src).then_inc(ld_x[g.slot(2)], 16)
                    e.dma_start(rows(dram["y"], r), y[:]).then_inc(st_y, 16)
                    e.dma_start(rows(dram["late"], r_late), y[:, :, HALF:D]).then_inc(st_y, 16)

                def body(g, s):
                    if g.first:
                        return
                    store_before(g, g.it)
                    if s == XSLOTS - 1:
                        for half, (_, c1) in enumerate(K_HALVES):
                            wait(e, pe_s, NS * g.it + GT * c1)
                            load_keys(1, half)
                        for half, (_, c1) in enumerate(V_HALVES):
                            wait(e, pe_o, DC * g.it + c1)
                            load_values(1, half)

                for load in (load_keys, load_values):
                    for half in range(2):
                        load(0, half)
                run(e, body)
                store_before(Group(NG, NG, 0), NG)
                wait(e, st_x1, 16 * NG)
                wait(e, st_y, 32 * NG)
                for s in range(XSLOTS):
                    wait(e, ld_x[s], 16 * len(range(s, NG + 1, XSLOTS)))
                e.dma_start(dram["late"][N:N + 1, :], zero_row[:]).then_inc(st_y, 16)
                wait(e, st_y, 32 * NG + 16)

            @block.gpsimd
            def _(e):
                def root(it):
                    wait(e, dv_ve, it + 1)
                    e.tensor_tensor(rs[:], ve[:], neg_half[:, 0:GT], ALU.pow).then_inc(pl_rs, 1)

                def root_y(it):
                    wait(e, dv_vy, it + 1)
                    e.tensor_tensor(rs_y[:], ve_y[:], neg_half[:, 0:GT], ALU.pow).then_inc(pl_ry, 1)

                def divide(it, c, tt):
                    p4 = prob[:, c % 2, tt, :].rearrange("p (r s) -> p r s", r=QUAD)
                    wait(e, dv_rc, NS * it + (GT * c + tt + 1))
                    e.tensor_tensor(p4, p4, rc[:, (GT * c + tt) % NS, :].rearrange("p (r o) -> p r o", o=1)
                                    .to_broadcast([P, QUAD, SC]), ALU.mult).then_inc(pl_p, 1)

                def add_bias(it, slot, tt):
                    wait(e, dv_xn, GT * it + GT)
                    e.tensor_tensor(x_in[:, slot, tt, :], x_in[:, slot, tt, :], bo[:], ALU.add).then_inc(pl_xb, 1)

                def body(g, s):
                    for q in range(DC):
                        for k in range(GT):
                            if not (g.last and q == DC - 1):
                                divide(g.it, q + 1, k)
                            if q >= 2 and k < 2 and not g.last:
                                add_bias(g.it + 1, g.slot(1), 2 * (q - 2) + k)
                            if q == 0 and k == 0 and not (g.first or g.last):
                                root(g.it + 1)
                            if q == 1 and k == 1 and not g.first:
                                root_y(g.it - 1)

                root(0)
                root(1)
                wait(e, ld_small, 32)
                for k in range(GT):
                    add_bias(0, 0, k)
                for k in range(GT):
                    divide(0, 0, k)
                run(e, body)
                root_y(NG - 1)

            @block.tensor
            def _(e):
                def transpose_x(it, k, bank, free):
                    wait(e, dv_xn, GT * it + GT)
                    free()
                    for tt in range(GT):
                        last = e.transpose(ps[:, bank, tt * P:(tt + 1) * P], xn[:, tt, k * P:(k + 1) * P], ident[:])
                    last.then_inc(pe_x, 1)

                def queries(c, free):
                    free()
                    for k in range(DC):
                        last = split_matmul(e, ps[:, TURNS, :], [x[:, k, c * P:(c + 1) * P] for x in wq],
                                            [x[:, k, :] for x in xT], k == 0, k == DC - 1)
                    last.then_inc(pe_q, 1)

                def scores(it, c, tt):
                    n = GT * c + tt
                    if tt == 0:
                        wait(e, dv_q, DC * it + (c + 1))
                    wait(e, ac_exp, NS * it + (n - 1))
                    for pair in range(2):
                        r = slice(64 * pair, 64 * pair + 64)
                        last = split_matmul(e, ps[:, 2 * (n % 2) + pair, 0:2 * SC],
                                            [x[r, c % DC, tt * P:(tt + 1) * P] for x in qT],
                                            [x[r, c % DC, :, :].rearrange("p a s -> p (a s)") for x in k_bd], True, True)
                    last.then_inc(pe_s, 1)

                def transpose_p(it, m):
                    c, k = divmod(m, QK)
                    if k == 0:
                        wait(e, pl_p, NS * it + GT * (c + 1))
                    wait(e, dv_t, NM * it + (m - 1))
                    for tt in range(GT):
                        last = e.transpose(ps[0:rows_of[k], 4 + m % 2, tt * P:(tt + 1) * P],
                                           prob[:, c % 2, tt, k * P:k * P + rows_of[k]], ident[:])
                    last.then_inc(pe_t, 1)

                def values(it, m):
                    c, k = divmod(m, QK)
                    if k == 0:
                        wait(e, dv_o, DC * it + c)
                    wait(e, dv_t, NM * it + (m + 1))
                    last = split_matmul(e, ps[:, V_BANK, :], [x[0:rows_of[k], c % DC, k, :] for x in v_bd],
                                        [x[0:rows_of[k], k, :] for x in pT], k == 0, k == QK - 1)
                    if k == QK - 1:
                        last.then_inc(pe_o, 1)

                def project(tt, bank, free):
                    free()
                    for c in range(DC):
                        last = split_matmul(e, ps[:, bank, :], [x[:, c, tt * P:(tt + 1) * P] for x in oT],
                                            [x[:, c, :] for x in wo], c == 0, c == DC - 1)
                    last.then_inc(pe_w, 1)

                def body(g, s):
                    it = g.it

                    def q_out(n):
                        return lambda: wait(e, dv_q, DC * it + n)

                    def w_out(n):
                        return lambda: wait(e, dv_x1, GT * it + (n - GT))

                    def x_out(n):
                        return lambda: wait(e, dv_x, DC * it + (DC + n))

                    def reloaded(half, loaded):
                        if s == 0 or g.last:
                            wait(e, half, 3 * loaded if g.last else g.turn * loaded + loaded, alone=True)

                    for q in range(DC):
                        for k in range(QK):
                            m = QK * q + k
                            if k < GT and not (g.last and q == DC - 1):
                                if (q, k, s) == (DC - 1, 0, XSLOTS - 1):
                                    wait(e, ld_k[0], g.turn * K_LOADED + 2 * K_LOADED, alone=True)
                                if (q, k) == (1, 0):
                                    reloaded(ld_k[1], K_LOADED)
                                scores(it, q + 1, k)
                            transpose_p(it, m)
                            if (q, k) == (0, 1) and not g.first:
                                wait(e, dv_o, DC * it)
                                project(0, TURNS, q_out(2))
                            elif (q, k) == (0, 2) and not g.first:
                                project(1, TURNS, w_out(1))
                            elif (q, k) == (0, 3):
                                queries(2, q_out(2) if g.first else w_out(2))
                            elif (q, k) == (0, 4) and not g.first:
                                project(2, TURNS, q_out(3))
                            elif (q, k) == (1, 0) and not g.first:
                                project(3, TURNS, w_out(3))
                            elif (q, k) == (1, 3):
                                queries(3, q_out(3) if g.first else w_out(4))
                            elif q == 2 and k < 3 and not g.last:
                                transpose_x(it + 1, k + 1, TURNS, x_out(k + 1))
                            elif (q, k) == (2, 3) and not g.last:
                                queries(0, x_out(4))
                            elif (q, k) == (3, 3) and not g.last:
                                queries(1, q_out(5))
                            if k == 0 and not (g.first and q == 0):
                                values(it, m - 2)
                                values(it, m - 1)
                            elif k >= 2:
                                if k == 2 and q in (0, DC - 1):
                                    reloaded(ld_v[q // (DC - 1)], V_LOADED)
                                values(it, m - 2)
                            if (q, k) == (1, 4) and not g.last:
                                transpose_x(it + 1, 0, TURNS, q_out(4))

                def nothing():
                    pass

                for k in range(DC):
                    transpose_x(0, k, k, nothing)
                queries(0, lambda: wait(e, dv_x, DC))
                for half in ld_k:
                    wait(e, half, K_LOADED)
                scores(0, 0, 0)
                scores(0, 0, 1)
                queries(1, nothing)
                scores(0, 0, 2)
                scores(0, 0, 3)
                for half in ld_v:
                    wait(e, half, V_LOADED)
                run(e, body)
                values(NG, -2)
                values(NG, -1)
                wait(e, dv_o, DC * NG)
                for tt in range(GT):
                    project(tt, tt, nothing)

            @block.scalar
            def _(e):
                def hi_x(it, k, bank):
                    wait(e, pe_x, DC * it + k + 1)
                    e.activation(xT[0][:, k, :], ps[:, bank, :], ACT.Copy).then_inc(ac_x, 1)

                def hi_q(it, c):
                    wait(e, pe_q, DC * it + (c + 1))
                    e.activation(qT[0][:, c % DC, :], ps[:, TURNS, :], ACT.Identity, bias=bq[:, c % DC:c % DC + 1]).then_inc(ac_q, 1)

                def exps(it, c, tt):
                    n = (GT * c + tt) % NS
                    wait(e, dv_max, NS * it + (GT * c + tt + 1))
                    for r in range(QUAD):
                        ins = e.activation(prob[:, c % 2, tt, r * SC:(r + 1) * SC],
                                           ps[:, 2 * (n % 2) + r // 2, (r % 2) * SC:(r % 2 + 1) * SC], ACT.Exp,
                                           bias=nmx[:, n, r:r + 1], scale=SCALE, accum_out=sm[:, n, r:r + 1])
                    ins.then_inc(ac_exp, 1)

                def hi_p(it, m):
                    k = m % QK
                    wait(e, pe_t, NM * it + m + 1)
                    e.activation(pT[0][0:rows_of[k], k, :], ps[0:rows_of[k], 4 + m % 2, :], ACT.Copy).then_inc(ac_t, 1)

                def hi_o(it, c):
                    wait(e, pe_o, DC * it + (c + 1))
                    e.activation(oT[0][:, c % DC, :], ps[:, V_BANK, :], ACT.Copy).then_inc(ac_o, 1)

                def body(g, s):
                    it = g.it
                    for q in range(DC):
                        more = not (g.last and q == DC - 1)
                        for k in range(QK):
                            if k == 0 and q != 2 and more:
                                exps(it, q + 1, k)
                            if k == 1 and not (g.first and q == 0):
                                hi_o(it, q - 1)
                            hi_p(it, QK * q + k)
                            if (q, k) == (1, 4) and not g.last:
                                hi_x(it + 1, 0, TURNS)
                            elif q == 2 and k < 3 and not g.last:
                                hi_x(it + 1, k + 1, TURNS)
                            if (0 < k < GT or (q, k) == (2, 0)) and more:
                                exps(it, q + 1, k)
                            if k == 3 and (q < 2 or not g.last):
                                hi_q(it, q + 2)

                for k in range(DC):
                    hi_x(0, k, k)
                wait(e, ld_small, 32)
                hi_q(0, 0)
                exps(0, 0, 0)
                exps(0, 0, 1)
                hi_q(0, 1)
                exps(0, 0, 2)
                exps(0, 0, 3)
                run(e, body)
                hi_o(NG, -1)

            @block.vector
            def _(e):
                own = [0, 0]

                def mark(ins):
                    ins.then_inc(dv_own, 1)
                    own[0] += 1

                def settle():
                    wait(e, dv_own, own[1] + own[0], alone=True)

                def moments(slot, times, tiles):
                    if 0 in tiles:
                        wait(e, ld_x[slot], times * 16 + 16, alone=True)
                    for tt in tiles:
                        ins = e.bn_stats(stats[:, tt, :], x_in[:, slot, tt, :])
                    if GT - 1 in tiles:
                        mark(ins)
                        settle()
                        for tt in range(GT):
                            mark(e.bn_aggr(mv[:, tt, :], stats[:, tt, :]))
                        settle()
                        e.tensor_scalar(ve[:].rearrange("p (t o) -> p t o", o=1), mv[:, :, 1:2], EPS, None, ALU.add).then_inc(dv_ve, 1)

                def normalise(it, slot, tiles):
                    wait(e, pl_rs, it + 1, alone=True)
                    for tt in tiles:
                        e.tensor_scalar(xn[:, tt, :], x_in[:, slot, tt, :], mv[:, tt, 0:1], rs[:, tt:tt + 1],
                                        ALU.subtract, ALU.mult).then_inc(dv_xn, 1)

                def lo_x(it, k, bank):
                    wait(e, ac_x, DC * it + k + 1)
                    e.tensor_tensor(xT[1][:, k, :], ps[:, bank, :], xT[0][:, k, :].bitcast(F32), ALU.subtract).then_inc(dv_x, 1)

                def lo_q(it, c):
                    wait(e, ac_q, DC * it + (c + 1))
                    e.scalar_tensor_tensor(out=qT[1][:, c % DC, :], in0=ps[:, TURNS, :], scalar=bq[:, c % DC:c % DC + 1],
                                           in1=qT[0][:, c % DC, :].bitcast(F32), op0=ALU.add, op1=ALU.subtract).then_inc(dv_q, 1)

                def maxima(it, c, tt):
                    n = (GT * c + tt) % NS
                    wait(e, pe_s, NS * it + (GT * c + tt + 1))
                    b0 = 2 * (n % 2)
                    mark(e.tensor_reduce(mx[:, n, :].rearrange("p (a r) -> p a r", a=2),
                                         ps[:, b0:b0 + 2, 0:2 * SC].rearrange("p a (r s) -> p a r s", r=2), AX.X, ALU.max))
                    settle()
                    e.tensor_scalar(nmx[:, n, :], mx[:, n, :], -SCALE, None, ALU.mult).then_inc(dv_max, 1)

                def recip(it, c, tt):
                    n = (GT * c + tt) % NS
                    wait(e, ac_exp, NS * it + (GT * c + tt + 1))
                    e.reciprocal(rc[:, n, :], sm[:, n, :]).then_inc(dv_rc, 1)

                def lo_p(it, m):
                    k = m % QK
                    wait(e, ac_t, NM * it + m + 1)
                    e.tensor_tensor(pT[1][0:rows_of[k], k, :], ps[0:rows_of[k], 4 + m % 2, :],
                                    pT[0][0:rows_of[k], k, :].bitcast(F32), ALU.subtract).then_inc(dv_t, 1)

                def lo_o(it, c):
                    wait(e, ac_o, DC * it + (c + 1))
                    e.tensor_tensor(oT[1][:, c % DC, :], ps[:, V_BANK, :], oT[0][:, c % DC, :].bitcast(F32), ALU.subtract).then_inc(dv_o, 1)

                def add_x1(it, slot, tt, bank):
                    if tt == 0:
                        wait(e, pl_xb, GT * it + GT, alone=True)
                    wait(e, pe_w, GT * it + (tt + 1))
                    e.tensor_tensor(x_in[:, slot, tt, :], ps[:, bank, :], x_in[:, slot, tt, :], ALU.add).then_inc(dv_x1, 1)

                def moments_y(it, slot, tt):
                    wait(e, dv_x1, GT * it + (tt + 1), alone=True)
                    mark(e.bn_stats(stats_y[:, tt, :], x_in[:, slot, tt, :]))
                    settle()
                    mark(e.bn_aggr(mv_y[:, tt, :], stats_y[:, tt, :]))
                    if tt == GT - 1:
                        settle()
                        e.tensor_scalar(ve_y[:].rearrange("p (t o) -> p t o", o=1), mv_y[:, :, 1:2], EPS, None, ALU.add).then_inc(dv_vy, 1)

                def finish(it, slot, tt):
                    if tt == 0:
                        wait(e, pl_ry, it + 1, alone=True)
                        wait(e, st_y, 32 * it, alone=True)
                    e.tensor_scalar(y[:, tt, :], x_in[:, slot, tt, :], mv_y[:, tt, 0:1], rs_y[:, tt:tt + 1],
                                    ALU.subtract, ALU.mult).then_inc(dv_y, 1)

                def body(g, s):
                    it, old = g.it, not g.first
                    own[0], own[1] = 0, OWN_BEFORE if g.first else OWN * it + (OWN_BEFORE + OWN_FIRST - OWN)
                    for q in range(DC):
                        more = not (g.last and q == DC - 1)
                        for k in range(QK):
                            x1_of = {(0, 2): 0, (0, 3): 1, (1, 0): 2, (1, 1): 3}.get((q, k))
                            if x1_of is not None and old:
                                add_x1(it - 1, g.slot(-1), x1_of, TURNS)
                            if k == 1 and q == 0 and old:
                                lo_o(it, q - 1)
                            if k < GT and more:
                                maxima(it, q + 1, k)
                            if k == 1 and q:
                                lo_o(it, q - 1)
                            if 0 < k < GT and more:
                                recip(it, q + 1, k - 1)
                            lo_p(it, QK * q + k)
                            if k == 3:
                                if more:
                                    recip(it, q + 1, 3)
                                if q < 2 or not g.last:
                                    lo_q(it, q + 2)
                            if (q, k) == (1, 4) and not g.last:
                                lo_x(it + 1, 0, TURNS)
                            elif q == 2 and k < 3 and not g.last:
                                lo_x(it + 1, k + 1, TURNS)
                            if (q, k) in ((0, 4), (1, 2)) and not g.last:
                                normalise(it + 1, g.slot(1), (0, 1) if q == 0 else (2, 3))
                            y_of = {(0, 2): 0, (0, 4): 1, (1, 0): 2, (1, 1): 3}.get((q, k))
                            if y_of is not None and old:
                                moments_y(it - 1, g.slot(-1), y_of)
                            if (q, k) in ((1, 3), (1, 4)) and old:
                                for tt in ((0, 1) if k == 3 else (2, 3)):
                                    finish(it - 1, g.slot(-1), tt)
                            if q == DC - 1 and k in (0, 2) and not g.last:
                                moments(g.slot(2), g.round(2), (0, 1) if k == 0 else (2, 3))
                    assert g.last or own[0] == (OWN_FIRST if g.first else OWN), own[0]

                moments(0, 0, range(GT))
                normalise(0, 0, range(GT))
                for k in range(DC):
                    lo_x(0, k, k)
                moments(1, 0, range(GT))
                wait(e, ld_small, 32)
                lo_q(0, 0)
                maxima(0, 0, 0)
                maxima(0, 0, 1)
                recip(0, 0, 0)
                lo_q(0, 1)
                maxima(0, 0, 2)
                recip(0, 0, 1)
                maxima(0, 0, 3)
                recip(0, 0, 2)
                recip(0, 0, 3)
                assert own[0] == OWN_BEFORE
                run(e, body)
                lo_o(NG, -1)
                slot = (NG - 1) % XSLOTS
                for tt in range(GT):
                    add_x1(NG - 1, slot, tt, tt)
                    moments_y(NG - 1, slot, tt)
                for tt in range(GT):
                    finish(NG - 1, slot, tt)


def attention_sems(sem):
    s = {n: [sem(f"a_{n}{u}") for u in range(4)] for n in ("ld_h", "ld_rot", "ld_y", "st")}
    for n in ("ld_small", "ld_mask", "k_copy", "dv_own", "pe_h", "ac_h", "dv_h", "pe_qkv", "ac_sq", "dv_ssq", "pl_rn", "dv_norm",
              "pl_tab", "pl_m1", "pl_m2", "pl_rot", "ac_v", "dv_v", "pe_r", "ac_r", "dv_r", "pe_s", "dv_s", "ac_exp", "dv_rc", "dv_p",
              "pe_t", "ac_t", "dv_t", "pe_o", "ac_o", "dv_o", "pe_w", "dv_y", "pl_init"):
        s[n] = sem(f"a_{n}")
    return s


def attention_phase(nc, io, ps, ident, s, wait, Split, neg_half, l, dram, zero_row):
    LH = NT * HEADS

    with ExitStack() as st:
        def sb(name, shape, dt=F32):
            return st.enter_context(nc.sbuf_tensor(name, shape, dt))

        wqkv = [sb(f"wqkv_{x}", [P, DC, 3 * D], F32R) for x in "hl"]
        wo = [sb(f"wo_{x}", [P, DC, D], F32R) for x in "hl"]
        hT = [sb(f"hT_{x}", [P, DC, P], F32R) for x in "hl"]
        qT = [sb(f"qT_{x}", [P, 2, DC, P], F32R) for x in "hl"]
        kT = [sb(f"kT_{x}", [P, DC, 6, P], F32R) for x in "hl"]
        v = [sb(f"v_{x}", [P, 4, D], F32R) for x in "hl"]
        pT = [sb(f"pT_{x}", [P, 4, KEYS], F32R) for x in "hl"]
        oT = [sb(f"oT_{x}", [P, DC, P], F32R) for x in "hl"]
        h_in = sb("h_in", [P, 4, D])
        y_in = sb("y_in", [P, 4, D])
        rot = sb("rot", [P, 4, 4, DH])
        qk_scale = sb("qk_scale", [P, 4, DH])
        sq = sb("sq", [P, 2, D])
        ssq = sb("ssq", [P, 2, HEADS])
        rn = sb("rn", [P, 2, HEADS])
        qk = sb("qk", [P, 2, D])
        m1 = sb("m1", [P, 2, D])
        m2 = sb("m2", [P, 2, D])
        mask = sb("mask", [P, KEYS])
        mask01 = sb("mask01", [P, 2, KEYS])
        neg_s = sb("neg_s", [P, 4, KEYS])
        neg_m = sb("neg_m", [P, 4])
        prob = sb("prob", [P, 4, KEYS])
        sm = sb("sm", [P, 4])
        rc = sb("rc", [P, 4])

        def weight(name):
            src = io[name].rearrange("l k n -> (l k) n")
            return [src[bass.ds(l * D + k * P, P), :] for k in range(DC)]

        w = Split("w_attn", st, D,
                  [(a[:, j * D:(j + 1) * D], wqkv[0][:, k, j * D:(j + 1) * D], wqkv[1][:, k, j * D:(j + 1) * D])
                   for j in range(3) for k, a in enumerate(weight("wqkv"))]
                  + [(a, wo[0][:, k, :], wo[1][:, k, :]) for k, a in enumerate(weight("wo"))], l)

        def at(total, i, per, k):
            return l * total + i * per + k if not isinstance(i, int) else l * total + (i * per + k)

        def need(e, name, total, i, per, k, alone=False):
            if isinstance(i, int) and i * per + k <= 0:
                return
            wait(e, s[name], at(total, i, per, k), alone or e is nc.sync)

        def tile_exists(i, j):
            return not isinstance(i, int) or 0 <= 4 * i + j < NT

        def loop(e, body):
            body(0)
            with e.Fori(1, NI - 1) as i:
                body(i)
            body(NI - 1)

        with nc.Block() as block:
            @block.sync
            def _(e):
                def load_h(i, j):
                    if tile_exists(i, j):
                        r = i * 4 * P + j * P
                        r = r if isinstance(r, int) else e.snap(r)
                        need(e, "pe_h", NT, i, 4, j - 3)
                        e.dma_start(h_in[:, j % 4, 0:HALF], dram["src"][bass.ds(r, P), 0:HALF]).then_inc(s["ld_h"][j % 4], 16)
                        e.dma_start(h_in[:, j % 4, HALF:D], dram["src_late"][bass.ds(r, P), :]).then_inc(s["ld_h"][j % 4], 16)

                def load_tables(i, j):
                    if tile_exists(i, j):
                        r = i * 4 * P + j * P
                        r = r if isinstance(r, int) else e.snap(r)
                        need(e, "pl_rot", 2 * NT, i, 8, 2 * (j - 3))
                        e.dma_start(rot[:, j % 4], io["rot"][bass.ds(r, P), :].rearrange("p (a d) -> p a d", a=4)).then_inc(s["ld_rot"][j % 4], 16)

                def load_masks(i):
                    for u in range(2):
                        r = i * 2 * P + u * P
                        r = r if isinstance(r, int) else e.snap(r)
                        need(e, "dv_s", LH, i, 4 * HEADS, -2 * HEADS)
                        e.dma_start(mask01[:, u, 0:2 * P], io["mask01"][bass.ds(r, P), :]).then_inc(s["ld_mask"], 16)

                def store(i, j):
                    if tile_exists(i, j):
                        r = i * 4 * P + j * P
                        r2 = i * 4 * P + (j * P + 1)
                        if not isinstance(i, int):
                            r, r2 = e.snap(r), e.snap(r2)
                        need(e, "dv_y", NT, i, 4, j + 1)
                        e.dma_start(dram["dst"][bass.ds(r, P), :], y_in[:, j % 4, :]).then_inc(s["st"][j % 4], 16)
                        e.dma_start(dram["dst_late"][bass.ds(r2, P), :], y_in[:, j % 4, HALF:D]).then_inc(s["st"][j % 4], 16)

                def body(i):
                    for u in range(4):
                        r = i * 4 * P + u * P
                        r = r if isinstance(r, int) else e.snap(r)
                        if not isinstance(i, int) or i:
                            wait(e, s["st"][u], 32 * (l * NI) + i * 32, alone=True)
                        e.dma_start(y_in[:, u, :], dram["src"][bass.ds(r, P), :]).then_inc(s["ld_y"][u], 16)
                        load_h(i, u + 3)
                        load_tables(i, u + 2)
                        if u >= 2:
                            need(e, "dv_r", 2 * NT, i, 8, 2 * u + 2)
                            need(e, "pe_s", LH, i, 4 * HEADS, HEADS * (u - 1))
                            for part in range(2):
                                e.dma_start(kT[part][:, :, u - 2, :].bitcast(F32), kT[part][:, :, u + 2, :].bitcast(F32)).then_inc(s["k_copy"], 16)
                        if u == 2 and not (isinstance(i, int) and i == NI - 1):
                            load_masks(i + 1)
                        store(i, u - 1)

                load_h(0, 0)
                w.loads(e, 0, w.slots)
                for a, name in enumerate(("q_scale", "k_scale")):
                    src = io[name][bass.ds(l, 1), :]
                    e.dma_start(qk_scale[:, 2 * a, :], src.to_broadcast([P, DH])).then_inc(s["ld_small"], 16)
                    for half in range(2):
                        e.dma_start(qk_scale[:, 2 * a + 1, half * DH // 2:(half + 1) * DH // 2],
                                    src[:, (1 - half) * DH // 2:(2 - half) * DH // 2].to_broadcast([P, DH // 2])).then_inc(s["ld_small"], 16)
                e.dma_start(mask[:], io["mask"]).then_inc(s["ld_small"], 16)
                for u in range(2):
                    e.dma_start(mask01[:, u, 2 * P:KEYS], io["mask"][:, 2 * P:KEYS]).then_inc(s["ld_small"], 16)
                load_tables(0, 0)
                load_h(0, 1)
                w.loads(e, w.slots)
                load_h(0, 2)
                load_tables(0, 1)
                load_masks(0)
                wait(e, s["pl_init"], 4 * l + 4, alone=True)
                loop(e, body)
                store(NI - 1, 3)
                wait(e, s["k_copy"], 64 * (l * NI) + 64 * NI, alone=True)
                for u in range(4):
                    wait(e, s["st"][u], 32 * (l * NI) + 32 * NI)
                e.dma_start(dram["dst_late"][N:N + 1, :], zero_row[:]).then_inc(s["ld_small"], 16)
                wait(e, s["ld_small"], 16 * 10 * l + 16 * 10)

            def token_major_heads(ap):
                return ap.rearrange("p (h d) -> p h d", h=HEADS)

            @block.gpsimd
            def _(e):
                for part in range(2):
                    e.memset(kT[part][:, :, 0:2, :].bitcast(F32), 0.0).then_inc(s["pl_init"], 1)
                    e.memset(v[part][:, 2:4, :].bitcast(F32), 0.0).then_inc(s["pl_init"], 1)
                wait(e, s["ld_small"], 16 * 10 * l + 16 * 9)

                def rotate(i, j):
                    if not tile_exists(i, j):
                        return
                    u = j % 4
                    if isinstance(i, int):
                        base = l * NI + (i + j // 4) + 1
                    else:
                        base = l * NI + i + (j // 4 + 1)
                    wait(e, s["ld_rot"][u], 16 * base)
                    e.tensor_tensor(rot[:, u], rot[:, u], qk_scale[:], ALU.mult).then_inc(s["pl_tab"], 1)
                    need(e, "pl_tab", NT, i, 4, j + 1)
                    hd = DH // 2
                    parts = [[token_major_heads(m[:, a, :]) for m in (qk, m1, m2)] for a in range(2)]
                    tabs = [rot[:, u, a, :].rearrange("p (o d) -> p o d", o=1) for a in range(4)]

                    def root(a):
                        need(e, "dv_ssq", 2 * NT, i, 8, 2 * j + a + 1)
                        e.tensor_tensor(rn[:, a, :], ssq[:, a, :], neg_half[:, 0:HEADS], ALU.pow).then_inc(s["pl_rn"], 1)

                    def times_cos(a):
                        need(e, "dv_norm", 2 * NT, i, 8, 2 * j + a + 1)
                        need(e, "pe_r", 2 * NT, i, 8, 2 * j + a - 1)
                        e.tensor_tensor(parts[a][1], parts[a][0], tabs[2 * a].to_broadcast([P, HEADS, DH]), ALU.mult).then_inc(s["pl_m1"], 1)

                    def plus_sin(a):
                        x, y1, y2 = parts[a]
                        for half in range(2):
                            here, there = (slice(z * hd, z * hd + hd) for z in (half, 1 - half))
                            e.tensor_tensor(y2[:, :, here], x[:, :, there], tabs[2 * a + 1][:, :, here].to_broadcast([P, HEADS, hd]),
                                            ALU.mult).then_inc(s["pl_m2"], 1)
                        need(e, "pl_m1", 2 * NT, i, 8, 2 * j + a + 1)
                        need(e, "pl_m2", 4 * NT, i, 16, 4 * j + 2 * a + 2)
                        e.tensor_tensor(y1, y1, y2, ALU.add).then_inc(s["pl_rot"], 1)

                    root(0)
                    times_cos(0)
                    root(1)
                    plus_sin(0)
                    times_cos(1)
                    plus_sin(1)

                rotate(0, 0)

                def body(i):
                    for u in range(4):
                        rotate(i, u + 1)

                loop(e, body)

            @block.tensor
            def _(e):
                def transpose_h(i, j):
                    if not tile_exists(i, j):
                        return
                    if isinstance(i, int):
                        base = l * NI + (i + j // 4) + 1
                    else:
                        base = l * NI + i + (j // 4 + 1)
                    wait(e, s["ld_h"][j % 4], 32 * base)
                    need(e, "dv_r", 2 * NT, i, 8, 2 * j)
                    for k in range(DC):
                        last = e.transpose(ps[:, 0, k * P:(k + 1) * P], h_in[:, j % 4, k * P:(k + 1) * P], ident[:])
                    last.then_inc(s["pe_h"], 1)

                def project(i, j, a):
                    if not tile_exists(i, j):
                        return
                    if a == 0:
                        need(e, "dv_h", NT, i, 4, j + 1)
                        need(e, "dv_r", 2 * NT, i, 8, 2 * j)
                    elif a == 1:
                        need(e, "dv_r", 2 * NT, i, 8, 2 * j)
                    else:
                        need(e, "dv_norm", 2 * NT, i, 8, 2 * j + 1)
                    for k in range(DC):
                        last = split_matmul(e, ps[:, a % 2, :], [x[:, k, :] for x in hT],
                                            [x[:, k, a * D:(a + 1) * D] for x in wqkv], k == 0, k == DC - 1)
                    last.then_inc(s["pe_qkv"], 1)

                def transpose_qk(i, j):
                    if not tile_exists(i, j):
                        return
                    for a in range(2):
                        need(e, "pl_rot", 2 * NT, i, 8, 2 * j + a + 1)
                        if a == 0:
                            need(e, "dv_norm", 2 * NT, i, 8, 2 * j + 2)
                            need(e, "dv_y", NT, i, 4, j - 1)
                        else:
                            need(e, "dv_v", NT, i, 4, j + 1)
                        for c in range(DC):
                            last = e.transpose(ps[:, 1 - a, c * P:(c + 1) * P], m1[:, a, c * P:(c + 1) * P], ident[:])
                        last.then_inc(s["pe_r"], 1)

                def scores(i, u, h):
                    if not tile_exists(i, u):
                        return
                    n = HEADS * u + h
                    if h == 0:
                        need(e, "dv_r", 2 * NT, i, 8, 2 * u + 2)
                        if u % 4 == 0 and not (isinstance(i, int) and 4 * i + u == 0):
                            if isinstance(i, int):
                                wait(e, s["k_copy"], 64 * (l * NI) + 64 * (i + u // 4))
                            else:
                                wait(e, s["k_copy"], 64 * (l * NI) + i * 64 + 64 * (u // 4))
                    need(e, "dv_s", LH, i, 4 * HEADS, n - 1)
                    r = slice(DH * (h % 2), DH * (h % 2) + DH)
                    uu = u % 4
                    split_matmul(e, ps[:, 2 + h % 2, 0:KEYS], [x[r, uu % 2, h // 2, :] for x in qT],
                                 [x[r, h // 2, uu:uu + 3, :].rearrange("p a k -> p (a k)") for x in kT],
                                 True, True).then_inc(s["pe_s"], 1)

                def transpose_p(i, u, h):
                    n = HEADS * u + h
                    need(e, "dv_p", LH, i, 4 * HEADS, n + 1)
                    need(e, "dv_t", LH, i, 4 * HEADS, n - 1)
                    for k in range(3):
                        last = e.transpose(ps[:, 4 + h % 2, k * P:(k + 1) * P], prob[:, n % 4, k * P:(k + 1) * P], ident[:])
                    last.then_inc(s["pe_t"], 1)

                def values(i, u, h):
                    n = HEADS * u + h
                    need(e, "dv_t", LH, i, 4 * HEADS, n + 1)
                    if h == 0:
                        need(e, "dv_v", NT, i, 4, u + 1)
                    if h % 4 == 0:
                        need(e, "dv_o", 2 * NT, i, 8, 2 * u + h // 4 - 1)
                    for k in range(3):
                        slot = (u + 2 + k) % 4
                        last = split_matmul(e, ps[0:DH, 6 + h // 4, (h % 4) * P:(h % 4 + 1) * P],
                                            [x[:, slot, h * DH:(h + 1) * DH] for x in v],
                                            [x[:, n % 4, k * P:(k + 1) * P] for x in pT], k == 0, k == 2)
                    last.then_inc(s["pe_o"], 1)

                def output(i, u):
                    if u < 0 and isinstance(i, int) and i == 0:
                        return
                    if u == 0 and isinstance(i, int) and i == 0:
                        w.done(e)
                    need(e, "dv_o", 2 * NT, i, 8, 2 * u + 2)
                    if tile_exists(i, u + 2):
                        need(e, "dv_norm", 2 * NT, i, 8, 2 * u + 6)
                    else:
                        need(e, "dv_y", NT, i, 4, u)
                    for c in range(DC):
                        last = split_matmul(e, ps[:, 1, :], [x[:, c, :] for x in oT], [x[:, c, :] for x in wo], c == 0, c == DC - 1)
                    last.then_inc(s["pe_w"], 1)

                transpose_h(0, 0)
                for a in range(3):
                    w.done(e, DC * (a + 1))
                    project(0, 0, a)
                transpose_qk(0, 0)
                transpose_h(0, 1)
                project(0, 1, 0)
                wait(e, s["pl_init"], 4 * l + 4)
                scores(0, 0, 0)
                scores(0, 0, 1)

                def body(i):
                    for u in range(4):
                        for h in range(HEADS):
                            if h < 6:
                                scores(i, u, h + 2)
                            else:
                                scores(i, u + 1, h - 6)
                            transpose_p(i, u, h)
                            if h == 4:
                                transpose_qk(i, u + 1)
                            if h:
                                values(i, u, h - 1)
                            elif not (isinstance(i, int) and i == 0 and u == 0):
                                values(i, u - 1, HEADS - 1)
                            if h < 2:
                                project(i, u + 1, h + 1)
                            elif h == 2:
                                output(i, u - 1)
                            elif h == 5:
                                transpose_h(i, u + 2)
                            elif h == 7:
                                project(i, u + 2, 0)

                loop(e, body)
                values(NI - 1, 3, HEADS - 1)
                output(NI - 1, 3)

            @block.scalar
            def _(e):

                def hi_h(i, j):
                    if tile_exists(i, j):
                        need(e, "pe_h", NT, i, 4, j + 1)
                        e.activation(hT[0][:].rearrange("p c t -> p (c t)"), ps[:, 0, :], ACT.Copy).then_inc(s["ac_h"], 1)

                def squares(i, j, a):
                    if tile_exists(i, j):
                        need(e, "pe_qkv", 3 * NT, i, 12, 3 * j + a + 1)
                        e.activation(sq[:, a, :], ps[:, a, :], ACT.Square).then_inc(s["ac_sq"], 1)

                def hi_v(i, j):
                    if tile_exists(i, j):
                        need(e, "pe_qkv", 3 * NT, i, 12, 3 * j + 3)
                        need(e, "pe_o", LH, i, 4 * HEADS, HEADS * (j - 1))
                        e.activation(v[0][:, j % 4, :], ps[:, 0, :], ACT.Copy).then_inc(s["ac_v"], 1)

                def hi_qk(i, j):
                    if tile_exists(i, j):
                        for a in range(2):
                            need(e, "pe_r", 2 * NT, i, 8, 2 * j + a + 1)
                            if a == 0:
                                dst = qT[0][:, j % 2]
                            else:
                                dst = kT[0][:, :, 2 + j % 4, :]
                                if j % 4 >= 2:
                                    wait_copy(e, i, j)
                            e.activation(dst, ps[:, 1 - a, :].rearrange("p (c t) -> p c t", c=DC), ACT.Copy).then_inc(s["ac_r"], 1)

                def wait_copy(e, i, j):
                    if isinstance(i, int):
                        if i + j // 4 > 0:
                            wait(e, s["k_copy"], 64 * (l * NI) + 64 * (i + j // 4))
                    else:
                        wait(e, s["k_copy"], 64 * (l * NI) + i * 64 + 64 * (j // 4))

                def exponent(i, u, h):
                    if tile_exists(i, u):
                        n = HEADS * u + h
                        need(e, "dv_s", LH, i, 4 * HEADS, n + 1)
                        need(e, "pe_t", LH, i, 4 * HEADS, n - 3)
                        need(e, "dv_p", LH, i, 4 * HEADS, n - 3)
                        m = n % 4
                        e.activation(prob[:, m, :], neg_s[:, m, :], ACT.Exp, bias=neg_m[:, n % 4:n % 4 + 1], scale=-1.0,
                                     accum_out=sm[:, n % 4:n % 4 + 1]).then_inc(s["ac_exp"], 1)

                def hi_p(i, u, h):
                    n = HEADS * u + h
                    need(e, "pe_t", LH, i, 4 * HEADS, n + 1)
                    need(e, "pe_o", LH, i, 4 * HEADS, n - 3)
                    e.activation(pT[0][:, n % 4, :], ps[:, 4 + h % 2, 0:KEYS], ACT.Copy).then_inc(s["ac_t"], 1)

                def hi_o(i, u, half):
                    need(e, "pe_o", LH, i, 4 * HEADS, HEADS * u + 4 * half + 4)
                    if half == 0:
                        need(e, "pe_w", NT, i, 4, u)
                    for odd in range(2):
                        src = ps[0:DH, 6 + half, :].rearrange("p (c o t) -> p c o t", c=2, o=2)[:, :, odd, :]
                        e.activation(oT[0][DH * odd:DH * odd + DH, 2 * half:2 * half + 2, :], src, ACT.Copy).then_inc(s["ac_o"], 1)

                hi_h(0, 0)
                w.his(e, 0, 2 * DC)
                squares(0, 0, 0)
                w.his(e, 2 * DC, 3 * DC)
                squares(0, 0, 1)
                w.his(e, 3 * DC)
                wait(e, s["pl_init"], 4 * l + 4)
                hi_v(0, 0)
                hi_qk(0, 0)
                hi_h(0, 1)
                exponent(0, 0, 0)
                exponent(0, 0, 1)

                def body(i):
                    for u in range(4):
                        for h in range(HEADS):
                            if h == 0:
                                squares(i, u + 1, 0)
                            elif h == 1:
                                squares(i, u + 1, 1)
                            elif h == 2:
                                hi_v(i, u + 1)
                            elif h == 5:
                                hi_qk(i, u + 1)
                            elif h == 6:
                                hi_h(i, u + 2)
                            hi_p(i, u, h)
                            if h < 6:
                                exponent(i, u, h + 2)
                            else:
                                exponent(i, u + 1, h - 6)
                            if h == 1 and not (isinstance(i, int) and i == 0 and u == 0):
                                hi_o(i, u - 1, 1)
                            elif h == 6:
                                hi_o(i, u, 0)

                loop(e, body)
                hi_o(NI - 1, 3, 1)

            @block.vector
            def _(e):

                def lo(out, bank, hi, done):
                    return e.tensor_tensor(out, bank, hi.bitcast(F32), ALU.subtract).then_inc(s[done], 1)

                def lo_h(i, j):
                    if tile_exists(i, j):
                        need(e, "ac_h", NT, i, 4, j + 1)
                        lo(hT[1][:].rearrange("p c t -> p (c t)"), ps[:, 0, :], hT[0][:].rearrange("p c t -> p (c t)"), "dv_h")

                def norms(i, j, a):
                    if tile_exists(i, j):
                        need(e, "ac_sq", 2 * NT, i, 8, 2 * j + a + 1)
                        e.tensor_reduce(ssq[:, a, :], token_major_heads(sq[:, a, :]), AX.X, ALU.add).then_inc(s["dv_own"], 1)
                        need(e, "dv_own", 2 * NT, i, 8, 2 * j + a + 1)
                        e.tensor_scalar(ssq[:, a, :], ssq[:, a, :], 1e-24, None, ALU.max).then_inc(s["dv_ssq"], 1)

                def normalise(i, j, a):
                    if tile_exists(i, j):
                        need(e, "pl_rn", 2 * NT, i, 8, 2 * j + a + 1)
                        need(e, "pl_rot", 2 * NT, i, 8, 2 * j + a - 1)
                        e.tensor_tensor(token_major_heads(qk[:, a, :]), token_major_heads(ps[:, a, :]),
                                        rn[:, a, :].rearrange("p (h o) -> p h o", o=1).to_broadcast([P, HEADS, DH]),
                                        ALU.mult).then_inc(s["dv_norm"], 1)

                def lo_v(i, j):
                    if tile_exists(i, j):
                        need(e, "ac_v", NT, i, 4, j + 1)
                        lo(v[1][:, j % 4, :], ps[:, 0, :], v[0][:, j % 4, :], "dv_v")

                def lo_qk(i, j):
                    if tile_exists(i, j):
                        for a in range(2):
                            need(e, "ac_r", 2 * NT, i, 8, 2 * j + a + 1)
                            hi, out = ((qT[x][:, j % 2] if a == 0 else kT[x][:, :, 2 + j % 4, :]) for x in range(2))
                            lo(out, ps[:, 1 - a, :].rearrange("p (c t) -> p c t", c=DC), hi, "dv_r")

                def masked(i, u, h):
                    if tile_exists(i, u):
                        n = HEADS * u + h
                        if h == 0 and u % 4 == 0:
                            if isinstance(i, int):
                                wait(e, s["ld_mask"], 32 * (l * NI) + 32 * (i + u // 4 + 1), alone=True)
                            else:
                                wait(e, s["ld_mask"], 32 * (l * NI) + i * 32 + 32 * (u // 4 + 1), alone=True)
                        need(e, "pe_s", LH, i, 4 * HEADS, n + 1, alone=True)
                        need(e, "ac_exp", LH, i, 4 * HEADS, n - 3, alone=True)
                        mk = mask01[:, u % 4, :] if u % 4 < 2 else mask[:]
                        e.tensor_tensor_reduce(out=neg_s[:, n % 4, :], in0=ps[:, 2 + h % 2, 0:KEYS], in1=mk, scale=-1.0,
                                               scalar=3.0e38, op0=ALU.add, op1=ALU.min, accum_out=neg_m[:, n % 4:n % 4 + 1]
                                               ).then_inc(s["dv_s"], 1)

                def divide(i, u, h):
                    if tile_exists(i, u):
                        n = HEADS * u + h
                        need(e, "ac_exp", LH, i, 4 * HEADS, n + 1)
                        e.reciprocal(rc[:, n % 4:n % 4 + 1], sm[:, n % 4:n % 4 + 1]).then_inc(s["dv_rc"], 1)
                        need(e, "dv_rc", LH, i, 4 * HEADS, n + 1)
                        e.tensor_scalar(prob[:, n % 4, :], prob[:, n % 4, :], rc[:, n % 4:n % 4 + 1], None, ALU.mult).then_inc(s["dv_p"], 1)

                def lo_p(i, u, h):
                    n = HEADS * u + h
                    need(e, "ac_t", LH, i, 4 * HEADS, n + 1)
                    lo(pT[1][:, n % 4, :], ps[:, 4 + h % 2, 0:KEYS], pT[0][:, n % 4, :], "dv_t")

                def lo_o(i, u, half):
                    need(e, "ac_o", 4 * NT, i, 16, 4 * u + 2 * half + 2)
                    for odd in range(2):
                        src = ps[0:DH, 6 + half, :].rearrange("p (c o t) -> p c o t", c=2, o=2)[:, :, odd, :]
                        r = slice(DH * odd, DH * odd + DH)
                        ins = e.tensor_tensor(oT[1][r, 2 * half:2 * half + 2, :], src,
                                              oT[0][r, 2 * half:2 * half + 2, :].bitcast(F32), ALU.subtract)
                    ins.then_inc(s["dv_o"], 1)

                def residual(i, u):
                    if isinstance(i, int):
                        if 4 * i + u < 0:
                            return
                        base = l * NI + (i + (u // 4)) + 1
                    else:
                        base = l * NI + i + (u // 4 + 1)
                    need(e, "pe_w", NT, i, 4, u + 1)
                    wait(e, s["ld_y"][u % 4], 16 * base)
                    e.tensor_tensor(y_in[:, u % 4, :], ps[:, 1, :], y_in[:, u % 4, :], ALU.add).then_inc(s["dv_y"], 1)

                lo_h(0, 0)
                w.los(e, 0, 2 * DC)
                norms(0, 0, 0)
                w.los(e, 2 * DC, 3 * DC)
                normalise(0, 0, 0)
                norms(0, 0, 1)
                w.los(e, 3 * DC)
                normalise(0, 0, 1)
                wait(e, s["ld_small"], 16 * 10 * l + 16 * 9)
                wait(e, s["pl_init"], 4 * l + 4)
                lo_v(0, 0)
                lo_qk(0, 0)
                lo_h(0, 1)
                masked(0, 0, 0)
                masked(0, 0, 1)
                divide(0, 0, 0)

                def body(i):
                    for u in range(4):
                        for h in range(HEADS):
                            if h == 0:
                                norms(i, u + 1, 0)
                            elif h == 1:
                                normalise(i, u + 1, 0)
                                norms(i, u + 1, 1)
                            elif h == 2:
                                normalise(i, u + 1, 1)
                            elif h == 3:
                                residual(i, u - 1)
                            elif h == 5:
                                lo_qk(i, u + 1)
                            if h < 6:
                                masked(i, u, h + 2)
                            else:
                                masked(i, u + 1, h - 6)
                            if h < 7:
                                divide(i, u, h + 1)
                            else:
                                divide(i, u + 1, 0)
                            lo_p(i, u, h)
                            if h == 1 and not (isinstance(i, int) and i == 0 and u == 0):
                                lo_o(i, u - 1, 1)
                            elif h == 2:
                                lo_v(i, u + 1)
                            elif h == 6:
                                lo_h(i, u + 2)
                            elif h == 7:
                                lo_o(i, u, 0)

                loop(e, body)
                lo_o(NI - 1, 3, 1)
                residual(NI - 1, 3)


def ffn_sems(sem):
    return {n: sem(f"f_{n}") for n in (
        "ld_small", "ld_in", "ld_res", "st", "dv_own", "dv_ve", "pl_rs", "dv_z", "pe_x", "ac_x", "dv_xh", "dv_x",
        "pe_a", "pe_g", "ac_g", "dv_u", "ac_u", "dv_ul", "pe_y", "pl_res", "dv_y", "pl_o")}


def ffn_phase(nc, io, ps, ident, s, wait, Split, neg_half, l, dram, zero_row):
    rows_of = [P] * (MC - 1) + [TAIL]
    cols = [[(x * HID + m * P, x * HID + m * P + rows_of[m]) for x in range(2)] for m in range(MC)]
    OWN = 1 + GT

    with ExitStack() as st:
        def sb(name, shape, dt=F32):
            return st.enter_context(nc.sbuf_tensor(name, shape, dt))

        w1 = [sb(f"w1_{x}", [P, DC, 2 * HID], F32R) for x in "hl"]
        w2 = [sb(f"w2_{x}", [P, MC, D], F32R) for x in "hl"]
        xT = [sb(f"fxT_{x}", [P, DC, G], F32R) for x in "hl"]
        u = [sb(f"u_{x}", [P, 2, G], F32R) for x in "hl"]
        x_full = sb("x_full", [P, 2, G])
        gate = sb("gate", [P, G])
        u_full = sb("u_full", [P, 2, G])
        h_in = sb("f_in", [P, GT, D])
        res = sb("f_res", [P, GT, D])
        x1 = sb("f_x1", [P, GT, D])
        lg, lb = sb("lg", [P, DC]), sb("lb", [P, DC])
        b1 = sb("b1_cols", [P, MC, 2])
        b2 = sb("b2_rows", [P, D])
        stats, mv = sb("f_stats", [P, GT, 6]), sb("f_mv", [P, GT, 2])
        ve, rs = sb("f_ve", [P, GT]), sb("f_rs", [P, GT])

        src1 = io["w1"].rearrange("l k n -> (l k) n")
        src2 = io["w2"].rearrange("l k n -> (l k) n")
        pieces = []
        for c0 in range(0, HID, 2 * P):
            m, n = c0 // P, min(2 * P, HID - c0)
            for x in range(2):
                c = slice(x * HID + c0, x * HID + c0 + n)
                pieces.append((src1[bass.ds(l * D, D), c].rearrange("(k p) c -> p k c", p=P), w1[0][:, :, c], w1[1][:, :, c]))
            if n == 2 * P:
                pieces.append((src2[bass.ds(l * HID + c0, n), :].rearrange("(m p) d -> p m d", p=P),
                               w2[0][:, m:m + 2, :], w2[1][:, m:m + 2, :]))
            else:
                pieces.append((src2[bass.ds(l * HID + c0, n), :], w2[0][0:n, m, :], w2[1][0:n, m, :]))
        PAIR = 3
        w = Split("w_ffn", st, DC * 2 * P, pieces, l)

        def is_first(g):
            return isinstance(g, int) and g == 0

        def is_last(g):
            return isinstance(g, int) and g == NG - 1

        def need(e, name, per, g, k, alone=False):
            if isinstance(g, int) and g * per + k <= 0:
                return
            value = l * (NG * per) + g * per + k if not isinstance(g, int) else l * (NG * per) + (g * per + k)
            wait(e, s[name], value, alone)

        def loop(e, body):
            body(0)
            with e.Fori(1, NG - 1) as g:
                body(g)
            body(NG - 1)

        SMALL = 6

        with nc.Block() as block:
            @block.sync
            def _(e):
                def rows(ap, g, late=0):
                    r = g * G + late
                    r = r if isinstance(r, int) else e.snap(r)
                    return ap[bass.ds(r, G), :].rearrange("(t p) d -> p t d", p=P)

                def load_in(g, behind):
                    a, b = rows(dram["src"], g)[:, :, 0:HALF], rows(dram["src_late"], g)
                    need(e, "pe_x", DC, behind, DC) if behind is not None else None
                    e.dma_start(h_in[:, :, 0:HALF], a).then_inc(s["ld_in"], 16)
                    e.dma_start(h_in[:, :, HALF:D], b).then_inc(s["ld_in"], 16)

                def body(g):
                    a, b = rows(dram["src"], g), rows(dram["x1"], g)
                    if not is_first(g):
                        wait(e, s["st"], l * (48 * NG) + g * 48)
                    e.dma_start(res[:], a).then_inc(s["ld_res"], 16)
                    e.dma_start(x1[:], b).then_inc(s["ld_res"], 16)
                    if not is_last(g):
                        load_in(g + 1, g)
                    if is_first(g):
                        w.loads(e, 4 * PAIR)
                    d = [rows(dram["dst"], g), rows(dram["dst_late"], g, 1), rows(io["out"], g)]
                    need(e, "dv_y", GT, g, GT)
                    e.dma_start(d[0], res[:]).then_inc(s["st"], 16)
                    e.dma_start(d[1], res[:, :, HALF:D]).then_inc(s["st"], 16)
                    need(e, "pl_o", GT, g, GT)
                    e.dma_start(d[2], x1[:]).then_inc(s["st"], 16)

                load_in(0, None)
                for name, t in (("ln_g", lg), ("ln_b", lb)):
                    e.dma_start(t[:], io[name][bass.ds(l * P, P), :]).then_inc(s["ld_small"], 16)
                e.dma_start(b1[:, 0:MC - 1, :], io["b1_main"][bass.ds(l * P, P), :].rearrange("p (m x) -> p m x", x=2)).then_inc(s["ld_small"], 16)
                e.dma_start(b1[0:TAIL, MC - 1, :], io["b1_tail"][bass.ds(l * TAIL, TAIL), :]).then_inc(s["ld_small"], 16)
                e.dma_start(b2[:], io["b2"][bass.ds(l, 1), :].to_broadcast([P, D])).then_inc(s["ld_small"], 16)
                w.loads(e, 0, 4 * PAIR)
                loop(e, body)
                wait(e, s["st"], l * (48 * NG) + 48 * NG)
                e.dma_start(dram["dst_late"][N:N + 1, :], zero_row[:]).then_inc(s["ld_small"], 16)
                wait(e, s["ld_small"], 16 * SMALL * l + 16 * SMALL)

            @block.gpsimd
            def _(e):
                def root(g):
                    need(e, "dv_ve", 1, g, 1)
                    e.tensor_tensor(rs[:], ve[:], neg_half[:, 0:GT], ALU.pow).then_inc(s["pl_rs"], 1)

                def body(g):
                    wait(e, s["ld_res"], l * (32 * NG) + g * 32 + 32)
                    for tt in range(GT):
                        e.tensor_tensor(res[:, tt, :], res[:, tt, :], b2[:], ALU.add).then_inc(s["pl_res"], 1)
                    if not is_last(g):
                        root(g + 1)
                    for tt in range(GT):
                        need(e, "dv_y", GT, g, tt + 1)
                        e.tensor_tensor(x1[:, tt, :], x1[:, tt, :], res[:, tt, :], ALU.add).then_inc(s["pl_o"], 1)

                wait(e, s["ld_small"], 16 * SMALL * l + 16 * (SMALL - 1))
                root(0)
                loop(e, body)

            @block.tensor
            def _(e):
                def transpose_x(g, k, behind):
                    need(e, "dv_z", GT, g, GT)
                    if k >= 2:
                        need(e, "ac_x", DC, g, k - 1)
                    elif behind is not None:
                        need(e, "dv_u", MC, behind, MC - 1)
                    for tt in range(GT):
                        last = e.transpose(ps[:, 2 + k % 2, tt * P:(tt + 1) * P], h_in[:, tt, k * P:(k + 1) * P], ident[:])
                    last.then_inc(s["pe_x"], 1)

                def hidden(g, m):
                    if m == 0:
                        need(e, "dv_x", DC, g, DC)
                    if is_first(g) and m % 2 == 0:
                        w.done(e, PAIR * (m // 2) + 2)
                    need(e, "dv_u", MC, g, m - 1 if m >= 2 else 0)
                    for x in range(2):
                        c = slice(*cols[m][x])
                        for k in range(DC):
                            last = split_matmul(e, ps[0:rows_of[m], 2 * (m % 2) + x, :], [y[:, k, c] for y in w1],
                                                [y[:, k, :] for y in xT], k == 0, k == DC - 1)
                        last.then_inc(s["pe_g" if x else "pe_a"], 1)

                def output(g, m):
                    if is_first(g) and m % 2 == 0:
                        w.done(e, PAIR * (m // 2 + 1))
                    need(e, "dv_ul", MC, g, m + 1)
                    if m == 0:
                        need(e, "dv_y", GT, g, 0)
                    for tt in range(GT):
                        r = slice(0, rows_of[m])
                        last = split_matmul(e, ps[:, 4 + tt, :], [y[r, m % 2, tt * P:(tt + 1) * P] for y in u],
                                            [y[r, m, :] for y in w2], m == 0, m == MC - 1)
                        if m == MC - 1 or tt == GT - 1:
                            last.then_inc(s["pe_y"], 1)

                def body(g):
                    for m in range(MC):
                        hidden(g, m)
                        if m == MC - 1 and not is_last(g):
                            transpose_x(g + 1, 0, g)
                            transpose_x(g + 1, 1, g)
                        if m:
                            output(g, m - 1)
                    if not is_last(g):
                        transpose_x(g + 1, 2, g)
                        transpose_x(g + 1, 3, g)
                    output(g, MC - 1)

                for k in range(DC):
                    transpose_x(0, k, None)
                loop(e, body)

            @block.scalar
            def _(e):
                wait(e, s["ld_small"], 16 * SMALL * l + 16 * (SMALL - 1))

                def affine(g, k):
                    need(e, "pe_x", DC, g, k + 1)
                    need(e, "dv_x", DC, g, k - 1)
                    e.activation(x_full[:, k % 2, :], ps[:, 2 + k % 2, :], ACT.Identity, bias=lb[:, k:k + 1], scale=lg[:, k:k + 1]).then_inc(s["ac_x"], 1)

                def body(g):
                    for m in range(MC):
                        r = slice(0, rows_of[m])
                        need(e, "pe_g", MC, g, m + 1)
                        need(e, "dv_u", MC, g, m)
                        e.activation(gate[r, :], ps[r, 2 * (m % 2) + 1, :], ACT.Gelu, bias=b1[r, m, 1:2]).then_inc(s["ac_g"], 1)
                        if m == MC - 1 and not is_last(g):
                            affine(g + 1, 0)
                        need(e, "dv_u", MC, g, m + 1)
                        need(e, "pe_y", MC - 1 + GT, g, m - 1 if m >= 2 else 0)
                        e.activation(u[0][r, m % 2, :], u_full[r, m % 2, :], ACT.Copy).then_inc(s["ac_u"], 1)
                        if is_first(g) and m % 2 == 0 and m < MC - 1:
                            w.his(e, PAIR * (m // 2 + 1), PAIR * (m // 2 + 2))
                    if not is_last(g):
                        for k in range(1, DC):
                            affine(g + 1, k)

                w.his(e, 0, 2)
                for k in range(DC):
                    affine(0, k)
                w.his(e, 2, PAIR)
                loop(e, body)

            @block.vector
            def _(e):
                wait(e, s["ld_small"], 16 * SMALL * l + 16 * (SMALL - 1))

                def normalise(g, meanwhile=None):
                    wait(e, s["ld_in"], l * (32 * NG) + g * 32 + 32)
                    for tt in range(GT):
                        ins = e.bn_stats(stats[:, tt, :], h_in[:, tt, :])
                    ins.then_inc(s["dv_own"], 1)
                    need(e, "dv_own", OWN, g, 1, alone=True)
                    for tt in range(GT):
                        e.bn_aggr(mv[:, tt, :], stats[:, tt, :]).then_inc(s["dv_own"], 1)
                    need(e, "dv_own", OWN, g, OWN, alone=True)
                    e.tensor_scalar(ve[:].rearrange("p (t o) -> p t o", o=1), mv[:, :, 1:2], EPS, None, ALU.add).then_inc(s["dv_ve"], 1)
                    if meanwhile:
                        meanwhile()
                    need(e, "pl_rs", 1, g, 1)
                    for tt in range(GT):
                        e.tensor_scalar(h_in[:, tt, :], h_in[:, tt, :], mv[:, tt, 0:1], rs[:, tt:tt + 1],
                                        ALU.subtract, ALU.mult).then_inc(s["dv_z"], 1)

                def split_x(g, k):
                    need(e, "ac_x", DC, g, k + 1)
                    e.tensor_copy(xT[0][:, k, :], x_full[:, k % 2, :]).then_inc(s["dv_xh"], 1)
                    need(e, "dv_xh", DC, g, k + 1)
                    e.tensor_tensor(xT[1][:, k, :], x_full[:, k % 2, :], xT[0][:, k, :].bitcast(F32), ALU.subtract).then_inc(s["dv_x"], 1)

                def body(g):
                    for m in range(MC):
                        r = slice(0, rows_of[m])
                        need(e, "pe_a", MC, g, m + 1)
                        need(e, "ac_g", MC, g, m + 1)
                        need(e, "dv_ul", MC, g, max(m - 1, 0))
                        e.scalar_tensor_tensor(out=u_full[r, m % 2, :], in0=ps[r, 2 * (m % 2), :], scalar=b1[r, m, 0:1],
                                               in1=gate[r, :], op0=ALU.add, op1=ALU.mult).then_inc(s["dv_u"], 1)
                        if m == MC - 1 and not is_last(g):
                            split_x(g + 1, 0)
                        need(e, "ac_u", MC, g, m + 1)
                        e.tensor_tensor(u[1][r, m % 2, :], u_full[r, m % 2, :], u[0][r, m % 2, :].bitcast(F32), ALU.subtract).then_inc(s["dv_ul"], 1)
                        if is_first(g) and m % 2 == 0 and m < MC - 1:
                            w.los(e, PAIR * (m // 2 + 1), PAIR * (m // 2 + 2))
                        if m == 5 and not is_last(g):
                            normalise(g + 1)
                    if not is_last(g):
                        for k in range(1, DC):
                            split_x(g + 1, k)
                    need(e, "pl_res", GT, g, GT)
                    for tt in range(GT):
                        need(e, "pe_y", MC - 1 + GT, g, MC + tt)
                        e.tensor_tensor(res[:, tt, :], ps[:, 4 + tt, :], res[:, tt, :], ALU.add).then_inc(s["dv_y"], 1)

                normalise(0, lambda: w.los(e, 0, 1))
                w.los(e, 1, 2)
                for k in range(DC):
                    split_x(0, k)
                w.los(e, 2, PAIR)
                loop(e, body)


def rotary_tables():
    half_idx = np.arange(0, DH, 2, dtype=np.float32)
    inv_freq = (np.float32(1.0) / np.float32(10000.0) ** (half_idx / np.float32(DH))).astype(np.float32)
    t = np.arange(N, dtype=np.float32)
    freqs = t[:, None] * inv_freq[None, :]
    freqs = np.concatenate([freqs, freqs], -1)
    base = (half_idx + np.float32(0.4 * DH)) / np.float32(1.4 * DH)
    power = (t - np.float32(N // 2)) / np.float32(WIN // 2)
    scale = base[None, :] ** power[:, None]
    scale = np.concatenate([scale, scale], -1)
    cos, sin = np.cos(freqs), np.sin(freqs)
    sin[:, :DH // 2] = -sin[:, :DH // 2]
    tab = np.concatenate([cos * scale * 8, sin * scale * 8, cos / scale, sin / scale], -1).astype(np.float32)
    return np.concatenate([tab] * B, 0)


def window_masks():
    q, k = np.arange(P)[:, None], np.arange(KEYS)[None, :] - 2 * P
    mask = np.where((k <= q) & (q <= k + WIN), np.float32(0), np.float32(MASKED)).astype(np.float32)
    first = np.repeat(mask[None, None, :, 0:2 * P], NI, 0).repeat(2, 1)
    for i in range(0, NI, NI // B):
        first[i, 0] = MASKED
        first[i, 1, :, 0:P] = MASKED
    return mask, np.ascontiguousarray(first.reshape(NI * 2 * P, 2 * P))


def kernel(**inputs):
    import concourse.bacc as bacc
    from concourse.bass_utils import run_bass_kernel_spmd

    a = {k: np.asarray(v) for k, v in inputs.items()}
    x_, f_ = "L0_xattn_", "L0_ffn_"
    mask, mask01 = window_masks()
    b1 = a[f_ + "b1"].reshape(DEPTH, 2, HID)
    main = (MC - 1) * P
    arrays = {
        "x": a["x"].reshape(T, D), "ctx": a["ctx_1024"].reshape(B * SC, D),
        "WqT": a[x_ + "Wq"].T, "WkT": a[x_ + "Wk"].T, "WvT": a[x_ + "Wv"].T, "WoT": a[x_ + "Wo"].T,
        "bq": a[x_ + "bq"].reshape(DC, P).T, "bk": a[x_ + "bk"].reshape(DC, P).T,
        "bv": a[x_ + "bv"].reshape(1, D), "bo": a[x_ + "bo"].reshape(1, D),
        "wqkv": a[f_ + "wqkv"], "q_scale": a[f_ + "q_scale"], "k_scale": a[f_ + "k_scale"], "wo": a[f_ + "wo"],
        "ln_g": a[f_ + "ln_g"].reshape(DEPTH, DC, P).transpose(0, 2, 1).reshape(DEPTH * P, DC),
        "ln_b": a[f_ + "ln_b"].reshape(DEPTH, DC, P).transpose(0, 2, 1).reshape(DEPTH * P, DC),
        "w1": a[f_ + "w1"], "w2": a[f_ + "w2"],
        "b1_main": b1[:, :, :main].reshape(DEPTH, 2, MC - 1, P).transpose(0, 3, 2, 1).reshape(DEPTH * P, 2 * (MC - 1)),
        "b1_tail": b1[:, :, main:].transpose(0, 2, 1).reshape(DEPTH * TAIL, 2),
        "b2": a[f_ + "b2"], "rot": rotary_tables(), "mask": mask, "mask01": mask01,
    }
    arrays = {k: np.ascontiguousarray(v) for k, v in arrays.items()}
    nc = bacc.Bacc("TRN2", target_bir_lowering=False, num_devices=1)
    io = {k: nc.dram_tensor(f"in_{k}", v.shape, mybir.dt.from_np(v.dtype), kind="ExternalInput").ap()
          for k, v in arrays.items()}
    io["out"] = nc.dram_tensor("out_rows", (T, D), F32, kind="ExternalOutput").ap()
    build(nc, io)
    r = run_bass_kernel_spmd(nc, [{f"in_{k}": v for k, v in arrays.items()}], core_ids=[0])
    return r.results[0]["out_rows"].reshape(B, N, D)
```
